# Optimizing a Trainium2 kernel written in Bass

```python
import numpy as np
import jax
import jax.numpy as jnp

def _softmax(x, axis=-1):
    return jax.nn.softmax(x, axis=axis)
def _gelu(x):
    return jax.nn.gelu(x, approximate=True)
def _silu(x):
    return jax.nn.silu(x)
def _sigmoid(x):
    return jax.nn.sigmoid(x)
def _layernorm(x, axis=-1, eps=1e-5):
    m = jnp.mean(x, axis=axis, keepdims=True)
    v = jnp.var(x, axis=axis, keepdims=True)
    return (x - m) / jnp.sqrt(v + eps)
def _scatter_add(tgt, idx, src, axis=0):
    return tgt.at[idx].add(src)
def _segment_sum(src, seg, n):
    return jax.ops.segment_sum(src, seg, n)

kernel_name = 'mk_vit_tower_cls_d1_tok_img256_3d28b0'

def setup_inputs(seed: int = 0):
    np.random.seed(seed)
    _w = jnp.asarray
    def _rec_inputs():
        import jax
        import jax.numpy as jnp
        _rk = jax.random.key(seed)
        x = (-0.000125008 + 0.999885 * jax.random.normal(jax.random.fold_in(_rk, 1), (2, 64, 64, 256), jnp.float32))
        cls_tok = 0.02 * jax.random.normal(jax.random.fold_in(_rk, 5), (1, 1, 256), jnp.float32)
        return x, cls_tok
    x, cls_tok = _rec_inputs()
    def _L0_tok_setup():
        import jax, jax.numpy as jnp
        import numpy as np
        DIM = 256
        NH = 8
        WH, WW = (8, 8)

        def _rope_axis(x, axis):
            half = x.shape[-1]
            inv_freq = 1.0 / 10000.0 ** (jnp.arange(0, half, 2, dtype=jnp.float32) / half)
            pos = jnp.arange(x.shape[axis], dtype=jnp.float32)
            ang = pos[:, None] * inv_freq
            cos, sin = (jnp.cos(ang), jnp.sin(ang))
            shape = [1, 1, 1, ang.shape[-1]]
            shape[axis] = ang.shape[0]
            cos = cos.reshape(shape).astype(x.dtype)
            sin = sin.reshape(shape).astype(x.dtype)
            x1, x2 = (x[..., 0::2], x[..., 1::2])
            r1 = x1 * cos - x2 * sin
            r2 = x1 * sin + x2 * cos
            return jnp.stack([r1, r2], axis=-1).reshape(x.shape)

        def _rope2(x):
            half = x.shape[-1] // 2
            return jnp.concatenate([_rope_axis(x[..., :half], 1), _rope_axis(x[..., half:], 2)], axis=-1)
        key = jax.random.key(seed)
        ks = jax.random.split(key, 5)
        B, H, W, C = (32, 64, 64, DIM)
        s = 1.0 / np.sqrt(C)
        return {'x': jax.random.normal(ks[0], (B, H, W, C), dtype=jnp.float32), 'qkv_w': jax.random.uniform(ks[1], (3 * C, C), jnp.float32, -s, s), 'qkv_b': jax.random.uniform(ks[2], (3 * C,), jnp.float32, -s, s), 'proj_w': jax.random.uniform(ks[3], (C, C), jnp.float32, -s, s), 'proj_b': jax.random.uniform(ks[4], (C,), jnp.float32, -s, s)}
    _L0_tok_all = _L0_tok_setup()
    _L0_tok_in = {k: v for k, v in _L0_tok_all.items() if k in ('qkv_w', 'qkv_b', 'proj_w', 'proj_b', )}
    del _L0_tok_all

    def _L0_attn_setup():
        import jax, jax.numpy as jnp
        import numpy as np
        import math
        B, L, D = (2, 2048, 256)
        N_SETS, PLANES_PER_SET = (4, 4)
        TOTAL_PLANES = N_SETS * PLANES_PER_SET
        POS_PLANES = 16
        LTM_PLANES = POS_PLANES
        PI = math.pi
        LN_EPS = 1e-05

        def _mlp2(x, w1, b1, w2, b2):
            h = jax.nn.gelu(x @ w1 + b1, approximate=False)
            return h @ w2 + b2
        key = jax.random.key(seed)
        ks = iter(jax.random.split(key, 40))

        def W(shape):
            return jax.random.normal(next(ks), shape, jnp.float32) / np.float32(np.sqrt(shape[0]))
        z = lambda *s: jnp.zeros(s, jnp.float32)
        return dict(x=jax.random.normal(next(ks), (B, L, D), jnp.float32), ke_w1=W((D, D)), ke_b1=z(D), ke_w2=W((D, TOTAL_PLANES)), ke_b2=z(TOTAL_PLANES), qe_w1=W((D, D)), qe_b1=z(D), qe_w2=W((D, TOTAL_PLANES)), qe_b2=z(TOTAL_PLANES), v_w=W((D, D)), v_b=z(D), out_ln_g=jnp.ones(D, jnp.float32), out_ln_b=z(D), out_w=W((D, D)), out_b=z(D), set_weights=jnp.ones(N_SETS, jnp.float32), pos_weight=jnp.ones((), jnp.float32), gate_w1=W((D, D // 2)), gate_b1=z(D // 2), gate_w2=W((D // 2, 1)), gate_b2=z(1), lke_w1=W((D, D)), lke_b1=z(D), lke_w2=W((D, LTM_PLANES)), lke_b2=z(LTM_PLANES), surprise_scale=jnp.asarray(5.0, jnp.float32), surprise_bias=jnp.asarray(0.0, jnp.float32), resonance_scale=jnp.asarray(5.0, jnp.float32), resonance_threshold=jnp.asarray(0.3, jnp.float32), ltm_weight=jnp.asarray(0.5, jnp.float32), pos_freqs=jnp.exp(jnp.arange(POS_PLANES, dtype=jnp.float32) * (-math.log(10000.0) / POS_PLANES)), ltm_binding_mem=((jax.random.normal(next(ks), (LTM_PLANES, D)) + 1j * jax.random.normal(next(ks), (LTM_PLANES, D))) * 0.5).astype(jnp.complex64), ltm_count=jnp.asarray(100.0, jnp.float32))
    _L0_attn_all = _L0_attn_setup()
    _L0_attn_in = {k: v for k, v in _L0_attn_all.items() if k in ('ke_w1', 'ke_b1', 'ke_w2', 'ke_b2', 'qe_w1', 'qe_b1', 'qe_w2', 'qe_b2', 'v_w', 'v_b', 'out_ln_g', 'out_ln_b', 'out_w', 'out_b', 'set_weights', 'pos_weight', 'gate_w1', 'gate_b1', 'gate_w2', 'gate_b2', 'lke_w1', 'lke_b1', 'lke_w2', 'lke_b2', 'surprise_scale', 'surprise_bias', 'resonance_scale', 'resonance_threshold', 'ltm_weight', 'pos_freqs', 'ltm_binding_mem', 'ltm_count', )}
    del _L0_attn_all

    def _L0_ffn_setup():
        import jax, jax.numpy as jnp
        import numpy as np
        B, S, D = (8, 4096, 256)
        H = 4 * D
        CAPACITY = 0.5
        key = jax.random.key(seed)
        ks = jax.random.split(key, 6)
        x = jax.random.normal(ks[0], (B, S, D), dtype=jnp.float32)
        attention_mask = jnp.zeros((B, 1, 1, S), dtype=jnp.float32)
        wr = jax.random.normal(ks[1], (D, 1), dtype=jnp.float32) * 0.02
        br = jnp.zeros((1,), dtype=jnp.float32)
        w1 = jax.random.normal(ks[2], (D, H), dtype=jnp.float32) * 0.02
        b1 = jnp.zeros((H,), dtype=jnp.float32)
        w2 = jax.random.normal(ks[3], (H, D), dtype=jnp.float32) * 0.02
        b2 = jnp.zeros((D,), dtype=jnp.float32)
        return {'x': x, 'attention_mask': attention_mask, 'wr': wr, 'br': br, 'w1': w1, 'b1': b1, 'w2': w2, 'b2': b2}
    _L0_ffn_all = _L0_ffn_setup()
    _L0_ffn_in = {k: v for k, v in _L0_ffn_all.items() if k in ('attention_mask', 'wr', 'br', 'w1', 'b1', 'w2', 'b2', )}
    del _L0_ffn_all

    return {
        "x": x,
        "cls_tok": cls_tok,
        "L0_tok_qkv_w": _L0_tok_in["qkv_w"],
        "L0_tok_qkv_b": _L0_tok_in["qkv_b"],
        "L0_tok_proj_w": _L0_tok_in["proj_w"],
        "L0_tok_proj_b": _L0_tok_in["proj_b"],
        "L0_attn_ke_w1": _L0_attn_in["ke_w1"],
        "L0_attn_ke_b1": _L0_attn_in["ke_b1"],
        "L0_attn_ke_w2": _L0_attn_in["ke_w2"],
        "L0_attn_ke_b2": _L0_attn_in["ke_b2"],
        "L0_attn_qe_w1": _L0_attn_in["qe_w1"],
        "L0_attn_qe_b1": _L0_attn_in["qe_b1"],
        "L0_attn_qe_w2": _L0_attn_in["qe_w2"],
        "L0_attn_qe_b2": _L0_attn_in["qe_b2"],
        "L0_attn_v_w": _L0_attn_in["v_w"],
        "L0_attn_v_b": _L0_attn_in["v_b"],
        "L0_attn_out_ln_g": _L0_attn_in["out_ln_g"],
        "L0_attn_out_ln_b": _L0_attn_in["out_ln_b"],
        "L0_attn_out_w": _L0_attn_in["out_w"],
        "L0_attn_out_b": _L0_attn_in["out_b"],
        "L0_attn_set_weights": _L0_attn_in["set_weights"],
        "L0_attn_pos_weight": _L0_attn_in["pos_weight"],
        "L0_attn_gate_w1": _L0_attn_in["gate_w1"],
        "L0_attn_gate_b1": _L0_attn_in["gate_b1"],
        "L0_attn_gate_w2": _L0_attn_in["gate_w2"],
        "L0_attn_gate_b2": _L0_attn_in["gate_b2"],
        "L0_attn_lke_w1": _L0_attn_in["lke_w1"],
        "L0_attn_lke_b1": _L0_attn_in["lke_b1"],
        "L0_attn_lke_w2": _L0_attn_in["lke_w2"],
        "L0_attn_lke_b2": _L0_attn_in["lke_b2"],
        "L0_attn_surprise_scale": _L0_attn_in["surprise_scale"],
        "L0_attn_surprise_bias": _L0_attn_in["surprise_bias"],
        "L0_attn_resonance_scale": _L0_attn_in["resonance_scale"],
        "L0_attn_resonance_threshold": _L0_attn_in["resonance_threshold"],
        "L0_attn_ltm_weight": _L0_attn_in["ltm_weight"],
        "L0_attn_pos_freqs": _L0_attn_in["pos_freqs"],
        "L0_attn_ltm_binding_mem": _L0_attn_in["ltm_binding_mem"],
        "L0_attn_ltm_count": _L0_attn_in["ltm_count"],
        "L0_ffn_attention_mask": _L0_ffn_in["attention_mask"],
        "L0_ffn_wr": _L0_ffn_in["wr"],
        "L0_ffn_br": _L0_ffn_in["br"],
        "L0_ffn_w1": _L0_ffn_in["w1"],
        "L0_ffn_b1": _L0_ffn_in["b1"],
        "L0_ffn_w2": _L0_ffn_in["w2"],
        "L0_ffn_b2": _L0_ffn_in["b2"],
    }

def reference(x, cls_tok, L0_tok_qkv_w, L0_tok_qkv_b, L0_tok_proj_w, L0_tok_proj_b, L0_attn_ke_w1, L0_attn_ke_b1, L0_attn_ke_w2, L0_attn_ke_b2, L0_attn_qe_w1, L0_attn_qe_b1, L0_attn_qe_w2, L0_attn_qe_b2, L0_attn_v_w, L0_attn_v_b, L0_attn_out_ln_g, L0_attn_out_ln_b, L0_attn_out_w, L0_attn_out_b, L0_attn_set_weights, L0_attn_pos_weight, L0_attn_gate_w1, L0_attn_gate_b1, L0_attn_gate_w2, L0_attn_gate_b2, L0_attn_lke_w1, L0_attn_lke_b1, L0_attn_lke_w2, L0_attn_lke_b2, L0_attn_surprise_scale, L0_attn_surprise_bias, L0_attn_resonance_scale, L0_attn_resonance_threshold, L0_attn_ltm_weight, L0_attn_pos_freqs, L0_attn_ltm_binding_mem, L0_attn_ltm_count, L0_ffn_attention_mask, L0_ffn_wr, L0_ffn_br, L0_ffn_w1, L0_ffn_b1, L0_ffn_w2, L0_ffn_b2):
    import jax
    import jax.numpy as jnp
    def _L0_tok_ref(x, qkv_w, qkv_b, proj_w, proj_b):
        import jax, jax.numpy as jnp
        import numpy as np
        DIM = 256
        NH = 8
        WH, WW = (8, 8)

        def _rope_axis(x, axis):
            half = x.shape[-1]
            inv_freq = 1.0 / 10000.0 ** (jnp.arange(0, half, 2, dtype=jnp.float32) / half)
            pos = jnp.arange(x.shape[axis], dtype=jnp.float32)
            ang = pos[:, None] * inv_freq
            cos, sin = (jnp.cos(ang), jnp.sin(ang))
            shape = [1, 1, 1, ang.shape[-1]]
            shape[axis] = ang.shape[0]
            cos = cos.reshape(shape).astype(x.dtype)
            sin = sin.reshape(shape).astype(x.dtype)
            x1, x2 = (x[..., 0::2], x[..., 1::2])
            r1 = x1 * cos - x2 * sin
            r2 = x1 * sin + x2 * cos
            return jnp.stack([r1, r2], axis=-1).reshape(x.shape)

        def _rope2(x):
            half = x.shape[-1] // 2
            return jnp.concatenate([_rope_axis(x[..., :half], 1), _rope_axis(x[..., half:], 2)], axis=-1)
        B, H, W, C = x.shape
        hd = C // NH
        N = WH * WW
        xw = x.reshape(B, H // WH, WH, W // WW, WW, C).transpose(0, 1, 3, 2, 4, 5).reshape(-1, N, C)
        qkv = xw @ qkv_w.T + qkv_b
        qkv = qkv.reshape(-1, N, 3, NH, hd).transpose(2, 0, 3, 1, 4)
        q, k, v = (qkv[0], qkv[1], qkv[2])
        q = _rope2(q.reshape(-1, WH, WW, hd)).reshape(-1, NH, N, hd)
        k = _rope2(k.reshape(-1, WH, WW, hd)).reshape(-1, NH, N, hd)
        scale = hd ** (-0.5)
        attn = jax.nn.softmax(q * scale @ jnp.swapaxes(k, -2, -1), axis=-1)
        out = (attn @ v).transpose(0, 2, 1, 3).reshape(-1, N, C)
        out = out.reshape(B, H // WH, W // WW, WH, WW, C).transpose(0, 1, 3, 2, 4, 5).reshape(B, H * W, C)
        return out @ proj_w.T + proj_b

    def _L0_attn_ref(x, ke_w1, ke_b1, ke_w2, ke_b2, qe_w1, qe_b1, qe_w2, qe_b2, v_w, v_b, out_ln_g, out_ln_b, out_w, out_b, set_weights, pos_weight, gate_w1, gate_b1, gate_w2, gate_b2, lke_w1, lke_b1, lke_w2, lke_b2, surprise_scale, surprise_bias, resonance_scale, resonance_threshold, ltm_weight, pos_freqs, ltm_binding_mem, ltm_count):
        import jax, jax.numpy as jnp
        import numpy as np
        import math
        B, L, D = (2, 2048, 256)
        N_SETS, PLANES_PER_SET = (4, 4)
        TOTAL_PLANES = N_SETS * PLANES_PER_SET
        POS_PLANES = 16
        LTM_PLANES = POS_PLANES
        PI = math.pi
        LN_EPS = 1e-05

        def _mlp2(x, w1, b1, w2, b2):
            h = jax.nn.gelu(x @ w1 + b1, approximate=False)
            return h @ w2 + b2
        B_, L_, D_ = x.shape
        key_phasor = jnp.exp(1j * (jnp.tanh(_mlp2(x, ke_w1, ke_b1, ke_w2, ke_b2)) * PI))
        query_phasor = jnp.exp(1j * (jnp.tanh(_mlp2(x, qe_w1, qe_b1, qe_w2, qe_b2)) * PI))
        kp = key_phasor.reshape(B_, L_, N_SETS, PLANES_PER_SET)
        qp = query_phasor.reshape(B_, L_, N_SETS, PLANES_PER_SET)
        weights = jax.nn.softmax(set_weights)
        V_real = x @ v_w + v_b
        joint_key = jnp.prod(kp, axis=2)
        joint_query = jnp.prod(qp, axis=2)
        km = jnp.cumsum(joint_key, axis=1)
        key_memory = jnp.concatenate([jnp.zeros_like(km[:, :1]), km[:, :-1]], axis=1)
        resonance_mag = jnp.abs(key_memory * jnp.conj(joint_query)).mean(-1, keepdims=True)
        positions = jnp.maximum(jnp.arange(L_, dtype=x.dtype), 1.0)
        norm_res = resonance_mag / jnp.sqrt(positions)[None, :, None]
        scale = jnp.clip(resonance_scale, 1.0, 20.0)
        thr = jnp.clip(resonance_threshold, 0.1, 0.9)
        surprise = 0.5 * (1.0 - jnp.tanh(scale * (norm_res - thr)))
        write_gate = jax.nn.sigmoid(surprise_scale * (surprise - 0.5) + surprise_bias)
        Vg = (V_real * write_gate).astype(jnp.complex64)
        bound = joint_key[..., None] * Vg[:, :, None, :]
        mem = jnp.cumsum(bound, axis=1)
        cross = jnp.real((mem * jnp.conj(joint_query)[..., None]).sum(2))
        bound_all = key_phasor[..., None] * Vg[:, :, None, :]
        mem_all = jnp.cumsum(bound_all, axis=1)
        ret_all = mem_all * jnp.conj(query_phasor)[..., None]
        per_bank = jnp.real(ret_all.reshape(B_, L_, N_SETS, PLANES_PER_SET, D_).sum(3))
        total = (per_bank * weights[None, None, :, None]).sum(2)
        total = (total + cross) / (N_SETS + 1)
        pos_phase = jnp.arange(L_, dtype=x.dtype)[:, None] * pos_freqs * (2.0 * PI)
        pos_phasor = jnp.exp(1j * pos_phase)
        Vc = V_real.astype(jnp.complex64)
        bound_pos = pos_phasor[None, :, :, None] * Vc[:, :, None, :]
        mem_pos = jnp.cumsum(bound_pos, axis=1)
        ret_pos = jnp.real((mem_pos * jnp.conj(pos_phasor)[None, :, :, None]).sum(2))
        gate = jax.nn.sigmoid(_mlp2(x, gate_w1, gate_b1, gate_w2, gate_b2))
        total = gate * total + (1.0 - gate) * (jax.nn.sigmoid(pos_weight) * ret_pos)
        ltm_phasor = jnp.exp(1j * (jnp.tanh(_mlp2(x, lke_w1, lke_b1, lke_w2, lke_b2)) * PI))
        persistent = jnp.real((ltm_binding_mem[None, None] * jnp.conj(ltm_phasor)[..., None]).sum(2))
        pnorm = jnp.sqrt(jnp.maximum(ltm_count, 1.0) * LTM_PLANES)
        total = total + jax.nn.sigmoid(ltm_weight) * (persistent / pnorm)
        mu = total.mean(-1, keepdims=True)
        var = ((total - mu) ** 2).mean(-1, keepdims=True)
        h = (total - mu) / jnp.sqrt(var + LN_EPS) * out_ln_g + out_ln_b
        return h @ out_w + out_b

    def _L0_ffn_ref(x, attention_mask, wr, br, w1, b1, w2, b2):
        import jax, jax.numpy as jnp
        import numpy as np
        B, S, D = (8, 4096, 256)
        H = 4 * D
        CAPACITY = 0.5
        b, s, d = x.shape
        weights = (jnp.einsum('bsd,do->bso', x, wr) + br)[..., 0]
        k = max(1, int(CAPACITY * s))
        kk = k - 1 if k > 1 else 1
        _, idx = jax.lax.top_k(weights, k)
        sel_idx = idx[:, :kk]
        sel = jnp.take_along_axis(x, sel_idx[:, :, None], axis=1)
        h = jax.nn.gelu(jnp.einsum('bkd,dh->bkh', sel, w1) + b1)
        y = jnp.einsum('bkh,hd->bkd', h, w2) + b2
        w_sel = jnp.take_along_axis(weights, sel_idx, axis=1)
        y = y * w_sel[..., None]
        batch_idx = jnp.arange(b)[:, None]
        processed = jnp.zeros_like(x).at[batch_idx, sel_idx].set(y)
        return processed + x

    h = _L0_tok_ref(x, L0_tok_qkv_w, L0_tok_qkv_b, L0_tok_proj_w, L0_tok_proj_b)
    h = jnp.concatenate([jnp.broadcast_to(cls_tok, (h.shape[0], 1, h.shape[2])), h], axis=1)
    h = h + _L0_attn_ref(_layernorm(h, axis=-1), L0_attn_ke_w1, L0_attn_ke_b1, L0_attn_ke_w2, L0_attn_ke_b2, L0_attn_qe_w1, L0_attn_qe_b1, L0_attn_qe_w2, L0_attn_qe_b2, L0_attn_v_w, L0_attn_v_b, L0_attn_out_ln_g, L0_attn_out_ln_b, L0_attn_out_w, L0_attn_out_b, L0_attn_set_weights, L0_attn_pos_weight, L0_attn_gate_w1, L0_attn_gate_b1, L0_attn_gate_w2, L0_attn_gate_b2, L0_attn_lke_w1, L0_attn_lke_b1, L0_attn_lke_w2, L0_attn_lke_b2, L0_attn_surprise_scale, L0_attn_surprise_bias, L0_attn_resonance_scale, L0_attn_resonance_threshold, L0_attn_ltm_weight, L0_attn_pos_freqs, L0_attn_ltm_binding_mem, L0_attn_ltm_count)
    h = h + _L0_ffn_ref(_layernorm(h, axis=-1), L0_ffn_attention_mask, L0_ffn_wr, L0_ffn_br, L0_ffn_w1, L0_ffn_b1, L0_ffn_w2, L0_ffn_b2)
    return h


_drawn_inputs = setup_inputs


def setup_inputs(seed=0):
    import zlib

    import numpy as np

    out = dict(_drawn_inputs(seed))
    spreads = {'L0_attn_ke_b1': (0.0, 0.8),
     'L0_attn_ke_b2': (0.0, 0.8),
     'L0_attn_qe_b1': (0.0, 0.8),
     'L0_attn_qe_b2': (0.0, 0.8),
     'L0_attn_v_b': (0.0, 0.1),
     'L0_attn_out_ln_g': (1.0, 0.2),
     'L0_attn_out_ln_b': (0.0, 0.1),
     'L0_attn_out_b': (0.0, 0.1),
     'L0_attn_set_weights': (1.0, 0.6),
     'L0_attn_gate_b1': (0.0, 0.8),
     'L0_attn_lke_b1': (0.0, 0.8),
     'L0_attn_lke_b2': (0.0, 0.8),
     'L0_ffn_b1': (0.0, 0.8),
     'L0_ffn_b2': (0.0, 0.8)}
    factors = {'cls_tok': 2.789,
     'L0_attn_ke_w1': 4.084,
     'L0_attn_ke_w2': 4.169,
     'L0_attn_qe_w1': 3.831,
     'L0_attn_qe_w2': 4.129,
     'L0_attn_gate_w1': 7.905,
     'L0_attn_gate_w2': 6.194,
     'L0_attn_lke_w1': 8.0,
     'L0_attn_lke_w2': 8.0,
     'L0_attn_pos_freqs': 8.0,
     'L0_ffn_wr': 6.296,
     'L0_ffn_w1': 8.0,
     'L0_ffn_w2': 8.0}
    for name, (base, spread) in spreads.items():
        noise = np.random.default_rng([zlib.crc32(name.encode()), seed]).standard_normal(out[name].shape)
        drawn = base * np.exp(spread * noise) if base else spread * noise
        out[name] = jnp.asarray(drawn.astype(out[name].dtype))
    for name, factor in factors.items():
        out[name] = (out[name] * factor).astype(out[name].dtype)
    return out
```

```python
from contextlib import ExitStack

import numpy as np

import concourse.bass as bass
from concourse import mybir

ALU = mybir.AluOpType
ACT = mybir.ActivationFunctionType
AX_X = mybir.AxisListType.X
F32 = mybir.dt.float32
F32R = mybir.dt.float32r
BF16 = mybir.dt.bfloat16
I32 = mybir.dt.int32

P = 128
B, IMG, DIM = 2, 64, 256
KC = DIM // P
WIN, HEADS = 8, 8
HD = DIM // HEADS
WTOK = WIN * WIN
NPAIR = B * IMG * IMG // P
UNIT = 4
NUNIT = NPAIR // UNIT
UTOK = UNIT * P
TPB = IMG * IMG // P
CLS = NPAIR
NT = NPAIR + 1
EPS = 1e-5
SCALE = HD ** -0.5

C_ID, C_TRI, C_STRICT, C_ONES = 0, P, 2 * P, 3 * P
C_COS = 4 * P
C_SIN = C_COS + HD
C_HEAD = C_SIN + HD
C_POS = C_HEAD + 4
C_SEG = C_POS + TPB
NCONST = C_SEG + 8 * TPB


def after(eng, sem, value):
    if not isinstance(value, int) or value > 0:
        eng.wait_ge(sem, value)


HI, LO = 0, 1


def high(ap):
    return ap.bitcast(F32)


def parts(f):
    return f(HI), f(LO)


def product(nc, out, lhs, rhs, start, stop):
    nc.tensor.matmul(out, lhs[HI], rhs[HI], start=start, stop=False)
    nc.tensor.matmul(out, lhs[HI], rhs[LO], start=False, stop=False)
    return nc.tensor.matmul(out, lhs[LO], rhs[HI], start=False, stop=stop)


def tokenizer(nc, g, x_t, qkv_w_t, proj_w_t):
    with ExitStack() as ctx:
        sb = lambda name, shape, dt=F32: ctx.enter_context(nc.sbuf_tensor(name, shape, dt))
        sem = lambda name: ctx.enter_context(nc.semaphore(name))
        wqkv = sb("wqkv", [P, KC, 3 * DIM])
        wqkv_hl = sb("wqkv_hl", [P, 2, KC, 3 * DIM], F32R)
        wproj = sb("wproj", [P, KC, DIM])
        xt = sb("xt", [P, UNIT, KC, P])
        xt_hl = sb("xt_hl", [P, 2, 2, KC, P], F32R)
        rope_c = sb("rope_c", [P, 2 * DIM])
        rope_s = sb("rope_s", [P, 2 * DIM])
        qk_rot = sb("qk_rot", [P, 2 * DIM])
        q_t = sb("q_t", [P, KC, P])
        k_blk = sb("k_blk", [P, KC, 2, 4, WTOK])
        v_half = sb("v_half", [P, UNIT, 2, P])
        probs = sb("probs", [P, HEADS, WTOK])
        smax = sb("smax", [P, HEADS])
        ssum = sb("ssum", [P, HEADS])
        sinv = sb("sinv", [P, HEADS])
        p_t = sb("p_t", [P, 4, 2, WTOK])
        o_t = sb("o_t", [P, KC, UTOK])

        w_loaded, w_high, w_split, x_high, x_split = sem("w_loaded"), sem("w_high"), sem("w_split"), sem("x_high"), sem("x_split")
        x_loaded = [sem(f"x_loaded{j}") for j in range(UNIT)]
        qk_ready, v_ready, tq_ready, sc_ready = sem("qk_ready"), sem("v_ready"), sem("tq_ready"), sem("sc_ready")
        pt_ready, av_ready, proj_ready = sem("pt_ready"), sem("av_ready"), sem("proj_ready")
        rope_done, rope_added, v_copied, qt_copied = sem("rope_done"), sem("rope_added"), sem("v_copied"), sem("qt_copied")
        kblk_done, max_done, sub_done, exp_done, sum_done = sem("kblk_done"), sem("max_done"), sem("sub_done"), sem("exp_done"), sem("sum_done")
        inv_done = sem("inv_done")
        p_ready, pt_copied, out0_copied, out1_copied = sem("p_ready"), sem("pt_copied"), sem("out0_copied"), sem("out1_copied")
        h_copied = sem("h_copied")

        ps_qk, ps_v, ps_tq, ps_sc, ps_pt, ps_av0, ps_av1, ps_proj = g["bank"]
        const, h, raw = g["const"], g["h"], g["raw"]
        ident = const[:, C_ID:C_ID + P]
        cos = const[:, C_COS:C_COS + HD]
        sin = const[:, C_SIN:C_SIN + HD]
        ones3, bias3 = g["ones3"], g["bias3"]
        LAST = NPAIR

        def live(s, lag):
            return not isinstance(s, int) or 0 <= s - lag < LAST

        def steps(eng, step):
            for s in range(UNIT):
                step(s, s, 0)
            with eng.Fori(1, NUNIT) as u:
                for j in range(UNIT):
                    step(u * UNIT + j, j, u)
            for s in range(LAST, LAST + 4):
                step(s, s % UNIT, NUNIT)

        def split_steps(eng, step):
            for s in range(UNIT):
                step(s, s, 0)
            with eng.Fori(1, NUNIT - 1) as u:
                for j in range(UNIT):
                    step(u * UNIT + j, j, u)
            for s in range(LAST - UNIT, LAST + 4):
                step(s, s % UNIT, s // UNIT)

        def next_x(s, j, u, split):
            if not isinstance(s, int) or s + 1 < LAST:
                split(s + 1, (j + 1) % UNIT, u + (j + 1) // UNIT)

        def o_rows(q, c, pair):
            return o_t[q * HD:(q + 1) * HD, c, :].rearrange("p (r w n) -> p w r n", r=WIN, w=WIN)[:, 2 * pair:2 * pair + 2]

        def o_head(ps, q):
            return ps[q * HD:(q + 1) * HD, :].rearrange("p (w h r n) -> p w h r n", w=2, h=4, r=WIN)[:, :, q]

        def unit_done(s, j):
            return j == 2 and (not isinstance(s, int) or s >= UNIT)

        with nc.Block() as block:
            @block.sync
            def _(sp):
                sp.dma_start(wqkv[:, :, :], qkv_w_t.rearrange("(k p) n -> p k n", p=P)).then_inc(w_loaded, 16)
                sp.dma_start(wproj[:, :, :], proj_w_t.rearrange("(k p) n -> p k n", p=P)).then_inc(w_loaded, 16)

                for j in range(UNIT):
                    sp.dma_start(xt[:, j, :, :], x_t[:, 0:1, j * P:(j + 1) * P]
                                 .rearrange("(k p) a n -> p k (a n)", p=P)).then_inc(x_loaded[j], 16)
                with sp.Fori(1, NUNIT) as u:
                    for j in range(UNIT):
                        sp.wait_ge(x_split, u * UNIT + j - 3)
                        sp.dma_start(xt[:, j, :, :], x_t[:, bass.ds(u, 1), j * P:(j + 1) * P]
                                     .rearrange("(k p) a n -> p k (a n)", p=P)).then_inc(x_loaded[j], 16)

            @block.tensor
            def _(pe):
                pe.wait_ge(w_loaded, 32)
                pe.wait_ge(w_split, 1)

                def project(u, half):
                    if half:
                        pe.wait_ge(h_copied, (u - 1) * 2 + half)
                    for i in range(2):
                        po, tile = ps_proj[:, i * DIM:(i + 1) * DIM], 2 * half + i
                        for k in range(KC):
                            nc.tensor.matmul(po, o_t[:, k, tile * P:(tile + 1) * P], wproj[:, k, :], start=(k == 0), stop=False)
                        t = nc.tensor.matmul(po, ones3[:, :], bias3[:, 3 * DIM:4 * DIM], start=False, stop=True)
                    t.then_inc(proj_ready, 1)

                def step(s, j, u):
                    if live(s, 1):
                        pe.wait_ge(rope_added, s)
                        after(pe, kblk_done, s - 1)
                        for c in range(4):
                            t = nc.tensor.transpose(ps_tq[:, c * P:(c + 1) * P], qk_rot[:, c * P:(c + 1) * P], ident)
                        t.then_inc(tq_ready, 1)
                    if live(s, 0):
                        pe.wait_ge(x_split, s + 1)
                        after(pe, rope_done, s)
                        for k in range(KC):
                            product(nc, ps_qk[:, :], parts(lambda c: xt_hl[:, j % 2, c, k, :]),
                                    parts(lambda c: wqkv_hl[:, c, k, 0:2 * DIM]), k == 0, False)
                        nc.tensor.matmul(ps_qk[:, :], ones3[:, :], bias3[:, 0:2 * DIM], start=False, stop=True).then_inc(qk_ready, 1)
                        after(pe, v_copied, s)
                        for k in range(KC):
                            product(nc, ps_v[:, 0:DIM], parts(lambda c: xt_hl[:, j % 2, c, k, :]),
                                    parts(lambda c: wqkv_hl[:, c, k, 2 * DIM:3 * DIM]), k == 0, False)
                        nc.tensor.matmul(ps_v[:, 0:DIM], ones3[:, :], bias3[:, 2 * DIM:3 * DIM], start=False, stop=True).then_inc(v_ready, 1)
                    if unit_done(s, j):
                        pe.wait_ge(out0_copied, (u - 1) * UNIT + UNIT)
                        pe.wait_ge(out1_copied, (u - 1) * UNIT + UNIT)
                        project(u, 0)
                    if live(s, 2):
                        pe.wait_ge(p_ready, s - 1)
                        after(pe, pt_copied, s - 2)
                        for c in range(4):
                            t = nc.tensor.transpose(ps_pt[:, c * P:(c + 1) * P], probs[:, 2 * c:2 * c + 2, :], ident)
                        t.then_inc(pt_ready, 1)
                    if live(s, 1):
                        pe.wait_ge(qt_copied, s)
                        pe.wait_ge(kblk_done, s)
                        after(pe, sub_done, s - 1)
                        for w in range(2):
                            for c in range(KC):
                                t = nc.tensor.matmul(ps_sc[w * WTOK:(w + 1) * WTOK, :].rearrange("p (t c n) -> p t c n", t=4, c=KC)[:, :, c, :],
                                                     q_t[:, c, w * WTOK:(w + 1) * WTOK],
                                                     k_blk[:, c, w, :, :], start=True, stop=True)
                        t.then_inc(sc_ready, 1)
                    if unit_done(s, j):
                        project(u, 1)
                    if live(s, 2):
                        pe.wait_ge(pt_copied, s - 1)
                        pe.wait_ge(v_copied, s - 1)
                        after(pe, out0_copied, s - 2)
                        after(pe, out1_copied, s - 2)
                        for c, dst in enumerate((ps_av0, ps_av1)):
                            for w in range(2):
                                t = nc.tensor.matmul(dst[:, w * 256:(w + 1) * 256],
                                                     v_half[c * WTOK:(c + 1) * WTOK, (j - 2) % UNIT, w, :],
                                                     p_t[c * WTOK:(c + 1) * WTOK, :, w, :], start=True, stop=True)
                        t.then_inc(av_ready, 1)
                steps(pe, step)

            @block.vector
            def _(dve):
                dve.wait_ge(w_high, 1)
                nc.vector.tensor_tensor(wqkv_hl[:, LO], wqkv[:, :, :], high(wqkv_hl[:, HI]), ALU.subtract).then_inc(w_split, 1)

                def step(s, j, u):
                    if live(s, 1):
                        dve.wait_ge(tq_ready, s)
                        dve.wait_ge(qt_copied, s)
                        after(dve, sc_ready, s - 1)
                        for c in range(KC):
                            kt = ps_tq[:, (2 + c) * P:(3 + c) * P].rearrange("p (w n) -> p w n", w=2)
                            mask = const[:, C_HEAD:C_HEAD + 4]
                            t = nc.vector.tensor_tensor(k_blk[:, c, :, :, :], kt.unsqueeze(2).to_broadcast([P, 2, 4, WTOK]),
                                                        mask.unsqueeze(1).unsqueeze(3).to_broadcast([P, 2, 4, WTOK]), ALU.mult)
                        t.then_inc(kblk_done, 1)
                    if live(s, 0):
                        dve.wait_ge(qk_ready, s + 1)
                        after(dve, rope_added, s)
                        z = ps_qk[:, :].rearrange("p (a n) -> p a n", n=HD)
                        nc.vector.tensor_tensor(rope_c[:, :].rearrange("p (a n) -> p a n", n=HD), z,
                                                cos.unsqueeze(1).to_broadcast([P, 2 * HEADS, HD]), ALU.mult)
                        rs = rope_s[:, :].rearrange("p (a n) -> p a n", n=HD)
                        for e in range(2):
                            t = nc.vector.tensor_tensor(rs[:, :, e::2], z[:, :, 1 - e::2],
                                                        sin[:, e::2].unsqueeze(1).to_broadcast([P, 2 * HEADS, HD // 2]), ALU.mult)
                        t.then_inc(rope_done, 1)
                    if live(s, 1):
                        dve.wait_ge(sc_ready, s)
                        sc = ps_sc[:, :].rearrange("p (h n) -> p h n", h=HEADS)
                        nc.vector.tensor_reduce(smax[:, :], sc, AX_X, ALU.max).then_inc(max_done, 1)
                        dve.wait_ge(max_done, s)
                        after(dve, pt_ready, s - 1)
                        nc.vector.tensor_tensor(probs[:, :, :], sc, smax[:, :].unsqueeze(2).to_broadcast([P, HEADS, WTOK]),
                                                ALU.subtract).then_inc(sub_done, 1)
                    if live(s, 2):
                        dve.wait_ge(av_ready, s - 1)
                        for q in range(4):
                            t = nc.vector.tensor_copy(
                                o_rows(q, 0, (j - 2) % UNIT),
                                o_head(ps_av0, q))
                        t.then_inc(out0_copied, 1)
                    if live(s, 1):
                        dve.wait_ge(exp_done, s)
                        nc.vector.tensor_reduce(ssum[:, :], probs[:, :, :], AX_X, ALU.add).then_inc(sum_done, 1)
                        dve.wait_ge(sum_done, s)
                        after(dve, p_ready, s - 1)
                        nc.vector.reciprocal(sinv[:, :], ssum[:, :]).then_inc(inv_done, 1)
                    if j == 3 and (not isinstance(s, int) or s >= UNIT):
                        dve.wait_ge(h_copied, u * 2)
                        for i in range(UNIT):
                            nc.vector.bn_stats(raw[:, bass.ds(((u - 1) * UNIT + i) * 6, 6)],
                                               h[:, bass.ds(((u - 1) * UNIT + i) * DIM, DIM)])
                steps(dve, step)
                nc.vector.bn_stats(raw[:, CLS * 6:NT * 6], h[:, CLS * DIM:NT * DIM])

            @block.gpsimd
            def _(pool):
                def low_x(s, j, u):
                    pool.wait_ge(x_high, s + 1)
                    nc.gpsimd.tensor_tensor(xt_hl[:, j % 2, LO], xt[:, j], high(xt_hl[:, j % 2, HI]), ALU.subtract).then_inc(x_split, 1)

                def step(s, j, u):
                    next_x(s, j, u, low_x)
                    if live(s, 0):
                        pool.wait_ge(rope_done, s + 1)
                        after(pool, tq_ready, s)
                        nc.gpsimd.tensor_tensor(qk_rot[:, :], rope_c[:, :], rope_s[:, :], ALU.add).then_inc(rope_added, 1)
                    if live(s, 1):
                        pool.wait_ge(inv_done, s)
                        nc.gpsimd.tensor_tensor(probs[:, :, :], probs[:, :, :], sinv[:, :].unsqueeze(2).to_broadcast([P, HEADS, WTOK]),
                                                ALU.mult).then_inc(p_ready, 1)
                low_x(0, 0, 0)
                split_steps(pool, step)
            @block.scalar
            def _(act):
                act.wait_ge(w_loaded, 32)
                nc.scalar.activation(wqkv_hl[:, HI], wqkv[:, :, :], ACT.Copy).then_inc(w_high, 1)

                def move_h(u, half):
                    act.wait_ge(proj_ready, (u - 1) * 2 + half + 1)
                    nc.scalar.activation(h[:, bass.ds(((u - 1) * 2 + half) * 2 * DIM, 2 * DIM)], ps_proj[:, :], ACT.Copy).then_inc(h_copied, 1)

                def high_x(s, j, u):
                    act.wait_ge(x_loaded[j], u * 16 + 16)
                    after(act, v_ready, s - 1)
                    nc.scalar.activation(xt_hl[:, j % 2, HI], xt[:, j], ACT.Copy).then_inc(x_high, 1)

                def step(s, j, u):
                    next_x(s, j, u, high_x)
                    if live(s, 1):
                        act.wait_ge(tq_ready, s)
                        after(act, sc_ready, s - 1)
                        nc.scalar.activation(q_t[:, :, :], ps_tq[:, 0:2 * P].rearrange("p (k n) -> p k n", k=KC), ACT.Copy).then_inc(qt_copied, 1)
                    if live(s, 0):
                        act.wait_ge(v_ready, s + 1)
                        after(act, av_ready, s - 3)
                        for c in range(KC):
                            for w in range(2):
                                t = nc.scalar.activation(v_half[c * WTOK:(c + 1) * WTOK, j, w, :],
                                                         ps_v[w * WTOK:(w + 1) * WTOK, c * P:(c + 1) * P], ACT.Copy)
                        t.then_inc(v_copied, 1)
                    if unit_done(s, j):
                        move_h(u, 0)
                    if live(s, 2):
                        act.wait_ge(pt_ready, s - 1)
                        after(act, av_ready, s - 2)
                        nc.scalar.activation(p_t[:, :, :, :], ps_pt[:, :].rearrange("p (c w n) -> p c w n", c=4, w=2), ACT.Copy).then_inc(pt_copied, 1)
                    if live(s, 1):
                        act.wait_ge(sub_done, s)
                        nc.scalar.activation(probs[:, :, :], probs[:, :, :], ACT.Exp, scale=SCALE).then_inc(exp_done, 1)
                    if unit_done(s, j):
                        move_h(u, 1)
                    if live(s, 2):
                        act.wait_ge(av_ready, s - 1)
                        for q in range(4):
                            t = nc.scalar.activation(
                                o_rows(q, 1, (j - 2) % UNIT),
                                o_head(ps_av1, q), ACT.Copy)
                        t.then_inc(out1_copied, 1)
                high_x(0, 0, 0)
                split_steps(act, step)


NHID = 7
PLANES, SETS = 16, 4
JOINT = PLANES // SETS
NPH = 2 * (JOINT + PLANES) + PLANES
COL_K, COL_Q, COL_L, COL_G = 0, JOINT + PLANES, 2 * (JOINT + PLANES), NPH
NCOL = NPH + 1
KF = 2 * (JOINT + PLANES)
PF = 2 * PLANES
LT = P - PF
MAGIC = 1.5 * 2.0 ** 23
PI = float(np.float32(np.pi))


def normaliser(nc, g, block_name):
    with ExitStack() as ctx:
        sb = lambda name, shape, dt=F32: ctx.enter_context(nc.sbuf_tensor(name + block_name, shape, dt))
        sem = lambda name: ctx.enter_context(nc.semaphore(name + block_name))
        raw, mean, rstd = g["raw"], g["mean"], g["rstd"]
        view = raw[:, :].rearrange("p (t f) -> p t f", f=6)
        dif, var = sb("dif", [P, NT]), sb("var", [P, NT])
        step_done, var_ready, std_ready = sem("ln_step_done"), sem("var_ready"), sem("std_ready")
        with nc.Block() as block:
            @block.vector
            def _(dve):
                nc.vector.tensor_tensor(mean[:, :], view[:, :, 1], view[:, :, 4], ALU.add)
                nc.vector.tensor_tensor(dif[:, :], view[:, :, 1], view[:, :, 4], ALU.subtract)
                nc.vector.tensor_tensor(var[:, :], view[:, :, 2], view[:, :, 5], ALU.add).then_inc(step_done, 1)
                dve.wait_ge(step_done, 1)
                nc.vector.tensor_scalar(mean[:, :], mean[:, :], 0.5, None, ALU.mult)
                nc.vector.tensor_tensor(dif[:, :], dif[:, :], dif[:, :], ALU.mult)
                nc.vector.tensor_scalar(var[:, :], var[:, :], 1.0 / DIM, EPS, ALU.mult, ALU.add).then_inc(step_done, 1)
                dve.wait_ge(step_done, 2)
                nc.vector.scalar_tensor_tensor(out=var[:, :], in0=dif[:, :], scalar=0.25, in1=var[:, :],
                                               op0=ALU.mult, op1=ALU.add).then_inc(var_ready, 1)
                dve.wait_ge(std_ready, 1)
                nc.vector.reciprocal(rstd[:, :], var[:, :])

            @block.scalar
            def _(act):
                act.wait_ge(var_ready, 1)
                nc.scalar.activation(var[:, :], var[:, :], ACT.Sqrt).then_inc(std_ready, 1)


def encoders(nc, g, a):
    with ExitStack() as ctx:
        sb = lambda name, shape, dt=F32: ctx.enter_context(nc.sbuf_tensor(name, shape, dt))
        sem = lambda name: ctx.enter_context(nc.semaphore(name))
        w1 = sb("enc_w1", [P, KC, NHID * P])
        w2 = sb("enc_w2", [P, NHID, NCOL])
        wv = sb("enc_wv", [P, KC, DIM])
        b1 = sb("enc_b1", [P, NHID])
        b2 = sb("enc_b2", [NCOL, 2])
        xn = sb("xn", [P, UNIT, DIM])
        xn_t = sb("xn_t", [P, KC, UTOK])
        hid = sb("hid", [P, NHID, UTOK])
        ph_t = sb("ph_t", [P, UTOK])
        w_loaded, b2_ready = sem("enc_w_loaded"), sem("b2_ready")
        xn_ready, xt_ready, xt0_copied, xt1_copied = sem("xn_ready"), sem("xt_ready"), sem("xt0_copied"), sem("xt1_copied")
        hid_ready, gelu_done, v_ready, v_copied = sem("hid_ready"), sem("gelu_done"), sem("ev_ready"), sem("ev_copied")
        l2_ready, tanh_done, pht_ready, ph_copied = sem("l2_ready"), sem("tanh_done"), sem("pht_ready"), sem("ph_copied")
        ps_t0, ps_t1, ps_v, ps_l2, ps_ph = g["bank"][0:5]
        ring = g["bank"][5:8]
        h, V, th, mean, rstd, ident = g["h"], g["V"], g["th"], g["mean"], g["rstd"], g["const"][:, C_ID:C_ID + P]
        ones3, bias3 = g["ones3"], g["bias3"]

        def tiles(u):
            return 1 if isinstance(u, int) and u == NUNIT else UNIT

        with nc.Block() as block:
            @block.sync
            def _(sp):
                for dst, src in ((w1[:, :, :], a["enc_w1"].rearrange("(k p) n -> p k n", p=P)),
                                 (wv[:, :, :], a["enc_wv"].rearrange("(k p) n -> p k n", p=P)),
                                 (w2[:, :, :], a["enc_w2"].rearrange("(c p) n -> p c n", p=P)),
                                 (b1[:, :], a["enc_b1"]), (b2[:, :], a["enc_b2"])):
                    sp.dma_start(dst, src).then_inc(w_loaded, 16)

            @block.vector
            def _(dve):
                nc.vector.memset(ph_t[:, :], 0.0).then_inc(b2_ready, 1)
                dve.wait_ge(w_loaded, 5 * 16)
                nc.vector.tensor_scalar(b2[:, 0:1], b2[:, 0:1], b2[:, 1:2], None, ALU.mult).then_inc(b2_ready, 1)

                def normalise(u):
                    after(dve, xt_ready, u)
                    for i in range(tiles(u)):
                        t = u * UNIT + i
                        n = nc.vector.tensor_scalar(xn[:, i, :], h[:, bass.ds(t * DIM, DIM)], mean[:, bass.ds(t, 1)],
                                                    rstd[:, bass.ds(t, 1)], ALU.subtract, ALU.mult)
                    n.then_inc(xn_ready, 1)

                def copy_xt(u):
                    dve.wait_ge(xt_ready, u + 1)
                    after(dve, v_ready, 2 * u)
                    n = tiles(u) * P
                    nc.vector.tensor_copy(xn_t[:, 1, 0:n], ps_t1[:, 0:n]).then_inc(xt1_copied, 1)

                def unit(u):
                    last = isinstance(u, int) and u > NUNIT
                    if isinstance(u, int) and u == 0:
                        normalise(u)
                        copy_xt(u)
                    if not last and not (isinstance(u, int) and u == NUNIT):
                        normalise(u + 1)
                    if not (isinstance(u, int) and u == 0):
                        dve.wait_ge(pht_ready, u)
                        m = tiles(u - 1)
                        nc.vector.tensor_copy(th[:, bass.ds((u - 1) * UNIT * NCOL, m * NCOL)].rearrange("p (i n) -> p i n", n=NCOL),
                                              ps_ph[:, 0:m * P].rearrange("p (i n) -> p i n", n=P)[:, :, 0:NCOL]).then_inc(ph_copied, 1)
                    if not last:
                        for half in range(2 if tiles(u) > 1 else 1):
                            dve.wait_ge(v_ready, 2 * u + half + 1)
                            n = 2 * DIM if tiles(u) > 1 else DIM
                            nc.vector.tensor_copy(V[:, bass.ds((u * UNIT + 2 * half) * DIM, n)], ps_v[:, 0:n]).then_inc(v_copied, 1)
                    if not last and not (isinstance(u, int) and u == NUNIT):
                        copy_xt(u + 1)
                unit(0)
                with dve.Fori(1, NUNIT - 1) as u:
                    unit(u)
                unit(NUNIT - 1)
                unit(NUNIT)
                unit(NUNIT + 1)

            @block.scalar
            def _(act):
                def copy_xt(u):
                    act.wait_ge(xt_ready, u + 1)
                    after(act, v_ready, 2 * u)
                    n = tiles(u) * P
                    nc.scalar.activation(xn_t[:, 0, 0:n], ps_t0[:, 0:n], ACT.Copy).then_inc(xt0_copied, 1)

                def unit(u):
                    n = tiles(u) * P
                    for c in range(NHID):
                        act.wait_ge(hid_ready, u * NHID + c + 1)
                        if c == 0:
                            after(act, l2_ready, u)
                        nc.scalar.activation(hid[:, c, 0:n], ring[c % 3][:, 0:n], ACT.Gelu, bias=b1[:, c:c + 1]).then_inc(gelu_done, 1)
                    if not (isinstance(u, int) and u == NUNIT):
                        copy_xt(u + 1)
                    act.wait_ge(l2_ready, u + 1)
                    after(act, pht_ready, u)
                    nc.scalar.activation(ph_t[0:NCOL, 0:n], ps_l2[0:NCOL, 0:n], ACT.Tanh, bias=b2[:, 0:1], scale=b2[:, 1:2]).then_inc(tanh_done, 1)
                act.wait_ge(w_loaded, 5 * 16)
                act.wait_ge(b2_ready, 2)
                copy_xt(0)
                unit(0)
                with act.Fori(1, NUNIT - 1) as u:
                    unit(u)
                unit(NUNIT - 1)
                unit(NUNIT)

            @block.tensor
            def _(pe):
                pe.wait_ge(w_loaded, 5 * 16)

                def turn(u):
                    pe.wait_ge(xn_ready, u + 1)
                    after(pe, xt0_copied, u)
                    after(pe, xt1_copied, u)
                    for k, dst in enumerate((ps_t0, ps_t1)):
                        for i in range(tiles(u)):
                            t = nc.tensor.transpose(dst[:, i * P:(i + 1) * P], xn[:, i, k * P:(k + 1) * P], ident)
                    t.then_inc(xt_ready, 1)

                def turn_phases(u):
                    pe.wait_ge(tanh_done, u + 1)
                    if isinstance(u, int):
                        after(pe, ph_copied, u)
                    for i in range(tiles(u)):
                        t = nc.tensor.transpose(ps_ph[:, i * P:(i + 1) * P], ph_t[:, i * P:(i + 1) * P], ident)
                    t.then_inc(pht_ready, 1)

                def unit(u):
                    n = tiles(u) * P
                    pe.wait_ge(xt0_copied, u + 1)
                    pe.wait_ge(xt1_copied, u + 1)
                    for c in range(NHID):
                        if c == 0 or c > 2:
                            after(pe, gelu_done, u * NHID + (c - 2 if c else 0))
                        for k in range(KC):
                            t = nc.tensor.matmul(ring[c % 3][:, 0:n], w1[:, k, c * P:(c + 1) * P], xn_t[:, k, 0:n], start=(k == 0), stop=(k == KC - 1))
                        t.then_inc(hid_ready, 1)
                    if not (isinstance(u, int) and u == NUNIT):
                        turn(u + 1)
                    if not (isinstance(u, int) and u == 0):
                        turn_phases(u - 1)
                    for half in range(2 if tiles(u) > 1 else 1):
                        after(pe, v_copied, 2 * u + half)
                        for i in range(2 if tiles(u) > 1 else 1):
                            i0 = (2 * half + i) * P
                            for k in range(KC):
                                nc.tensor.matmul(ps_v[:, i * DIM:(i + 1) * DIM], xn_t[:, k, i0:i0 + P], wv[:, k, :], start=(k == 0), stop=False)
                            t = nc.tensor.matmul(ps_v[:, i * DIM:(i + 1) * DIM], ones3[:, :], bias3[:, 4 * DIM:5 * DIM], start=False, stop=True)
                        t.then_inc(v_ready, 1)
                    after(pe, tanh_done, u)
                    for c in range(NHID):
                        pe.wait_ge(gelu_done, u * NHID + c + 1)
                        t = nc.tensor.matmul(ps_l2[0:NCOL, 0:n], w2[:, c, :], hid[:, c, 0:n], start=(c == 0), stop=(c == NHID - 1))
                    t.then_inc(l2_ready, 1)
                turn(0)
                unit(0)
                with pe.Fori(1, NUNIT - 1) as u:
                    unit(u)
                unit(NUNIT - 1)
                unit(NUNIT)
                turn_phases(NUNIT)


PI_IN = 3.1415925
TWO_PI = float(np.float32(2 * np.pi))
TP1 = 6.28125
TP2 = 253 / 2.0 ** 17
TP3 = float(np.float32(2 * np.pi - TP1 - TP2))
(S_SETW, S_POSW, S_SSCALE, S_SBIAS, S_RSCALE, S_RTHR, S_LTMW, S_COUNT, S_FREQ, NSCAL) = (0, 4, 5, 6, 7, 8, 9, 10, 11, 27)
NBIAS = 7 * DIM


def prologue(nc, g, a):
    with ExitStack() as ctx:
        sb = lambda name, shape, dt=F32: ctx.enter_context(nc.sbuf_tensor(name, shape, dt))
        sem = lambda name: ctx.enter_context(nc.semaphore(name))
        row = sb("bias_row", [1, NBIAS])
        parts = sb("bias_parts", [1, 3, NBIAS], BF16)
        t = sb("pro_t", [P, 16])
        ph, turns = sb("pos_phase", [P, TPB * PLANES]), sb("pos_turns", [P, TPB * PLANES])
        posn = sb("pos_n", [P, TPB])
        zero = sb("pro_zero", [P, 1])
        lnb, lng = sb("lnb", [P, KC]), sb("lng", [P, KC])
        ltm = sb("ltm_rows", [P, DIM])
        loaded, bias_sent, step_done, act_done = sem("pro_loaded"), sem("bias_sent"), sem("pro_step_done"), sem("pro_act_done")
        shift_ready, wout_loaded, ltm_loaded = sem("shift_ready"), sem("wout_loaded"), sem("ltm_loaded")
        const, scal, sc, wout, st, post, rpos = g["const"], g["scal"], g["sc"], g["wout"], g["st"], g["post"], g["rpos"]
        bias_ready, arguments_ready = sem("bias_ready"), sem("arguments_ready")
        ps = g["bank"][0]
        with nc.Block() as block:
            @block.sync
            def _(sp):
                sp.dma_start(const[:, :], a["const"]).then_inc(loaded, 16)
                sp.dma_start(row[:, :], a["bias"]).then_inc(loaded, 16)
                sp.dma_start(scal[:, :], a["scal"].to_broadcast([P, NSCAL])).then_inc(loaded, 16)
                sp.dma_start(g["h"][:, CLS * DIM:NT * DIM], a["cls"].to_broadcast([P, DIM])).then_inc(loaded, 16)
                sp.dma_start(wout[:, :, :], a["out_w"].rearrange("(k p) n -> p k n", p=P)).then_inc(wout_loaded, 16)
                sp.dma_start(lng[:, :], a["ln_g"]).then_inc(wout_loaded, 16)
                sp.dma_start(lnb[:, :], a["ln_b"]).then_inc(wout_loaded, 16)
                sp.dma_start(ltm[LT:P, :], a["ltm"]).then_inc(ltm_loaded, 16)
                sp.wait_ge(bias_ready, 1)
                sp.dma_start(g["bias3"][:, :], parts[:, :, :]).then_inc(bias_sent, 16)
                sp.wait_ge(bias_sent, 16)

            @block.tensor
            def _(pe):
                pe.wait_ge(wout_loaded, 48)
                pe.wait_ge(loaded, 64)
                for k in range(KC):
                    m = nc.tensor.matmul(ps[0:1, 0:DIM], lnb[:, k:k + 1], wout[:, k, :], start=(k == 0), stop=(k == KC - 1))
                m.then_inc(shift_ready, 1)

            @block.vector
            def _(dve):
                count = [0]

                def done(ins):
                    count[0] += 1
                    ins.then_inc(step_done, 1)
                    dve.wait_ge(step_done, count[0])

                V = nc.vector
                V.memset(g["ones3"][:, :], 1.0)
                V.memset(g["half_pi"][:, :], float(np.float32(np.pi / 2)))
                V.memset(g["eps"][:, :], EPS)
                V.memset(g["kq"][:, :, :, :], 0.0)
                V.memset(st[:, :, :], 0.0)
                dve.wait_ge(loaded, 64)
                dve.wait_ge(shift_ready, 1)
                done(V.tensor_tensor(row[:, 5 * DIM:6 * DIM], row[:, 5 * DIM:6 * DIM], ps[0:1, 0:DIM], ALU.add))
                for k in range(KC):
                    V.tensor_scalar(wout[:, k, :], wout[:, k, :], lng[:, k:k + 1], None, ALU.mult)
                for i in range(3):
                    done(V.tensor_copy(parts[:, i, :], row[:, :]))
                    if i < 2:
                        done(V.tensor_tensor(row[:, :], row[:, :], parts[:, i, :], ALU.subtract))
                V.memset(zero[:, :], 0.0).then_inc(bias_ready, 1)
                p3 = ph[:, :].rearrange("p (t f) -> p t f", f=PLANES)
                done(V.tensor_tensor(p3, const[:, C_POS:C_POS + TPB].unsqueeze(2).to_broadcast([P, TPB, PLANES]),
                                     scal[:, S_FREQ:S_FREQ + PLANES].unsqueeze(1).to_broadcast([P, TPB, PLANES]), ALU.mult))
                done(V.tensor_scalar(ph[:, :], ph[:, :], TWO_PI, None, ALU.mult))
                done(V.tensor_scalar(turns[:, :], ph[:, :], float(np.float32(1 / (2 * np.pi))), MAGIC, ALU.mult, ALU.add))
                done(V.tensor_scalar(turns[:, :], turns[:, :], MAGIC, None, ALU.subtract))
                for part in (TP1, TP2, TP3):
                    done(V.scalar_tensor_tensor(out=ph[:, :], in0=turns[:, :], scalar=-part, in1=ph[:, :], op0=ALU.mult, op1=ALU.add))
                done(V.tensor_scalar(ph[:, :], ph[:, :], PI_IN, -PI_IN, ALU.min, ALU.max))
                done(V.scalar_tensor_tensor(out=turns[:, :], in0=ph[:, :], scalar=-1.0, in1=ph[:, :], op0=ALU.mult, op1=ALU.max))
                done(V.tensor_reduce(t[:, 0:1], scal[:, S_SETW:S_SETW + SETS], AX_X, ALU.max))
                done(V.tensor_scalar(sc["setw"], scal[:, S_SETW:S_SETW + SETS], t[:, 0:1], None, ALU.subtract))
                V.tensor_scalar(sc["posw"], scal[:, S_POSW:S_POSW + 1], 0.5, None, ALU.mult)
                V.tensor_scalar(sc["rscale"], scal[:, S_RSCALE:S_RSCALE + 1], 1.0, 20.0, ALU.max, ALU.min)
                V.tensor_scalar(sc["rthr"], scal[:, S_RTHR:S_RTHR + 1], 0.1, 0.9, ALU.max, ALU.min)
                V.tensor_scalar(sc["count"], scal[:, S_COUNT:S_COUNT + 1], 1.0, float(PLANES), ALU.max, ALU.mult)
                V.tensor_scalar(posn[:, :], const[:, C_POS:C_POS + TPB], 1.0, None, ALU.max)
                done(V.tensor_scalar(sc["ltmw"], scal[:, S_LTMW:S_LTMW + 1], 0.5, None, ALU.mult))
                done(V.tensor_tensor(sc["nthr"], sc["rscale"], sc["rthr"], ALU.mult))
                V.tensor_scalar(sc["nthr"], sc["nthr"], -1.0, None, ALU.mult).then_inc(arguments_ready, 1)
                dve.wait_ge(act_done, 7)
                done(V.reciprocal(t[:, 1:2], t[:, 1:2]))
                V.tensor_scalar(sc["setw"], sc["setw"], t[:, 1:2], None, ALU.mult)
                V.tensor_scalar(sc["posw"], sc["posw"], 0.5, 0.5, ALU.mult, ALU.add)
                V.tensor_scalar(sc["ltmw"], sc["ltmw"], 0.5, 0.5, ALU.mult, ALU.add)
                V.reciprocal(rpos[:, :], posn[:, :])
                done(V.reciprocal(sc["count"], sc["count"]))
                done(V.tensor_tensor(t[:, 2:3], sc["ltmw"], sc["count"], ALU.mult))
                dve.wait_ge(ltm_loaded, 16)
                for i in range(2):
                    V.tensor_scalar(st[LT:P, i, :], ltm[LT:P, :], t[LT:P, 2:3], None, ALU.mult)
                V.memset(sc["wtab"], 1.0).then_inc(step_done, 1)
                count[0] += 1
                dve.wait_ge(step_done, count[0])
                V.tensor_copy(sc["wtab"][:, JOINT:].rearrange("p (s j) -> p s j", s=SETS),
                              sc["setw"].unsqueeze(2).to_broadcast([P, SETS, JOINT]))
                V.memset(post[:, TPB, 0, :], 1.0)
                V.memset(post[:, TPB, 1, :], 0.0)
            @block.scalar
            def _(act):
                act.wait_ge(arguments_ready, 1)
                p3 = ph[:, :].rearrange("p (t f) -> p t f", f=PLANES)
                n3 = turns[:, :].rearrange("p (t f) -> p t f", f=PLANES)
                nc.scalar.activation(sc["setw"], sc["setw"], ACT.Exp, accum_out=t[:, 1:2]).then_inc(act_done, 1)
                nc.scalar.activation(sc["posw"], sc["posw"], ACT.Tanh).then_inc(act_done, 1)
                nc.scalar.activation(sc["ltmw"], sc["ltmw"], ACT.Tanh).then_inc(act_done, 1)
                nc.scalar.activation(post[:, 0:TPB, 1, :], p3, ACT.Sin).then_inc(act_done, 1)
                nc.scalar.activation(post[:, 0:TPB, 0, :], n3, ACT.Sin, bias=g["half_pi"][:, :], scale=-1.0).then_inc(act_done, 1)
                nc.scalar.activation(posn[:, :], posn[:, :], ACT.Sqrt).then_inc(act_done, 1)
                nc.scalar.activation(sc["count"], sc["count"], ACT.Sqrt).then_inc(act_done, 1)


def phasors(nc, g):
    with ExitStack() as ctx:
        sb = lambda name, shape, dt=F32: ctx.enter_context(nc.sbuf_tensor(name, shape, dt))
        sem = lambda name: ctx.enter_context(nc.semaphore(name))
        th, trig, wg, gg, sc, const, rpos = g["th"], g["trig"], g["wg"], g["gg"], g["sc"], g["const"], g["rpos"]
        t3 = th[:, :].rearrange("p (t n) -> p t n", n=NCOL)
        NJ = B * 2 * JOINT * TPB
        turn = sb("turn", [P, NT, 2, JOINT])
        part = [sb(f"part{i}", [P, NT, 2, JOINT]) for i in range(2)]
        tot, km = sb("tot", [P, NJ]), sb("km", [P, NJ])
        pr = [x[:, :, :, :].rearrange("p t q j -> p (t q j)")[:, i * NJ // 2:(i + 1) * NJ // 2]
              .rearrange("p (b f t) -> p b f t", b=B, f=JOINT) for x in (turn, part[1]) for i in range(2)]
        mag = sb("mag", [P, NT])
        joint_ready, sin_done, abs_done, trig_ready = sem("joint_ready"), sem("sin_done"), sem("abs_done"), sem("trig_ready")
        step_done, sums_ready, square_ready, root_ready = sem("ph_step_done"), sem("sums_ready"), sem("square_ready"), sem("root_ready")
        arg_ready, surprise_ready, arg2_ready, gate_ready = sem("arg_ready"), sem("surprise_ready"), sem("arg2_ready"), sem("gate_ready")
        ps_pre, ps_tot = g["bank"][0:2]
        with nc.Block() as block:
            @block.vector
            def _(dve):
                count = [0]
                V = nc.vector

                def done(ins):
                    count[0] += 1
                    ins.then_inc(step_done, 1)
                    dve.wait_ge(step_done, count[0])

                def sets(c, s):
                    return t3[:, :, c + JOINT + s * JOINT:c + JOINT + (s + 1) * JOINT]
                for q, c in enumerate((COL_K, COL_Q)):
                    V.tensor_tensor(part[0][:, :, q, :], sets(c, 0), sets(c, 1), ALU.add)
                    V.tensor_tensor(part[1][:, :, q, :], sets(c, 2), sets(c, 3), ALU.add)
                done(V.memset(mag[:, CLS:NT], 0.0))
                done(V.tensor_tensor(part[0][:, :, :, :], part[0][:, :, :, :], part[1][:, :, :, :], ALU.add))
                done(V.tensor_scalar(turn[:, :, :, :], part[0][:, :, :, :], 0.5, MAGIC, ALU.mult, ALU.add))
                done(V.tensor_scalar(turn[:, :, :, :], turn[:, :, :, :], MAGIC, None, ALU.subtract))
                for q, c in enumerate((COL_K, COL_Q)):
                    n = V.scalar_tensor_tensor(out=t3[:, :, c:c + JOINT], in0=turn[:, :, q, :], scalar=-2.0,
                                               in1=part[0][:, :, q, :], op0=ALU.mult, op1=ALU.add)
                n.then_inc(joint_ready, 1)
                V.tensor_scalar(gg[:, 0, :], t3[:, :, COL_G], 0.1, 0.1, ALU.mult, ALU.add)
                done(V.tensor_scalar(gg[:, 1, :], t3[:, :, COL_G], -0.5, 0.5, ALU.mult, ALU.add))
                V.tensor_scalar(gg[:, 1, :], gg[:, 1, :], sc["posw"], None, ALU.mult)
                dve.wait_ge(sin_done, 1)
                dve.wait_ge(joint_ready, 1)
                V.scalar_tensor_tensor(out=t3[:, :, 0:NPH], in0=t3[:, :, 0:NPH], scalar=-1.0, in1=t3[:, :, 0:NPH],
                                       op0=ALU.mult, op1=ALU.max).then_inc(abs_done, 1)
                dve.wait_ge(sums_ready, 1)
                half = 2 * JOINT * TPB
                for b in range(B):
                    n = V.tensor_tensor_scan(tot[:, b * half:(b + 1) * half], const[:, C_SEG:C_SEG + half],
                                             ps_tot[:, b * half:(b + 1) * half], 0.0, ALU.mult, ALU.add)
                done(n)
                done(V.tensor_tensor(tot[:, :], tot[:, :], ps_tot[:, :], ALU.subtract))
                done(V.tensor_tensor(km[:, :], tot[:, :], ps_pre[:, :], ALU.add))
                k5 = km[:, :].rearrange("p (b c f t) -> p b c f t", b=B, c=2, f=JOINT)
                for b in range(B):
                    n = V.tensor_tensor(k5[:, b].rearrange("p c f t -> p (c f) t"), k5[:, b].rearrange("p c f t -> p (c f) t"),
                                        g["jcls"][:, :].unsqueeze(2).to_broadcast([P, 2 * JOINT, TPB]), ALU.add)
                done(n)
                jq = [trig[:, 0:NPAIR, c, COL_Q:COL_Q + JOINT].rearrange("p (b t) f -> p b f t", b=B) for c in range(2)]
                V.tensor_tensor(pr[0][:, :, :, :], k5[:, :, 0], jq[0], ALU.mult)
                V.tensor_tensor(pr[1][:, :, :, :], k5[:, :, 1], jq[1], ALU.mult)
                V.tensor_tensor(pr[2][:, :, :, :], k5[:, :, 1], jq[0], ALU.mult)
                done(V.tensor_tensor(pr[3][:, :, :, :], k5[:, :, 0], jq[1], ALU.mult))
                V.tensor_tensor(pr[0][:, :, :, :], pr[0][:, :, :, :], pr[1][:, :, :, :], ALU.add)
                done(V.tensor_tensor(pr[2][:, :, :, :], pr[2][:, :, :, :], pr[3][:, :, :, :], ALU.subtract))
                V.tensor_tensor(pr[0][:, :, :, :], pr[0][:, :, :, :], pr[0][:, :, :, :], ALU.mult)
                done(V.tensor_tensor(pr[2][:, :, :, :], pr[2][:, :, :, :], pr[2][:, :, :, :], ALU.mult))
                V.tensor_tensor(pr[0][:, :, :, :], pr[0][:, :, :, :], pr[2][:, :, :, :], ALU.add).then_inc(square_ready, 1)
                dve.wait_ge(root_ready, 1)
                done(V.tensor_reduce(mag[:, 0:NPAIR].rearrange("p (b t) -> p b t", b=B),
                                     pr[1][:, :, :, :].rearrange("p b f t -> p b t f"), AX_X, ALU.add))
                m3 = mag[:, 0:NPAIR].rearrange("p (b t) -> p b t", b=B)
                done(V.scalar_tensor_tensor(out=m3, in0=m3, scalar=1.0 / JOINT, in1=rpos[:, :].unsqueeze(1).to_broadcast([P, B, TPB]),
                                            op0=ALU.mult, op1=ALU.mult))
                V.tensor_scalar(mag[:, :], mag[:, :], sc["rscale"], sc["nthr"], ALU.mult, ALU.add).then_inc(arg_ready, 1)
                dve.wait_ge(surprise_ready, 1)
                done(V.tensor_scalar(mag[:, :], mag[:, :], -0.5, g["scal"][:, S_SSCALE:S_SSCALE + 1], ALU.mult, ALU.mult))
                V.tensor_scalar(mag[:, :], mag[:, :], g["scal"][:, S_SBIAS:S_SBIAS + 1], 0.5, ALU.add, ALU.mult).then_inc(arg2_ready, 1)
                dve.wait_ge(gate_ready, 1)
                V.tensor_scalar(wg[:, :], mag[:, :], 0.5, 0.5, ALU.mult, ALU.add)

            @block.scalar
            def _(act):
                act.wait_ge(joint_ready, 1)
                nc.scalar.activation(trig[:, :, 1, :], t3[:, :, 0:NPH], ACT.Sin, scale=PI_IN).then_inc(sin_done, 1)
                act.wait_ge(abs_done, 1)
                nc.scalar.activation(trig[:, :, 0, :], t3[:, :, 0:NPH], ACT.Sin, bias=g["half_pi"][:, :], scale=-PI).then_inc(trig_ready, 1)
                act.wait_ge(trig_ready, 1)
                nc.scalar.activation(g["jcls"][:, :].rearrange("p (c f) -> p c f", c=2), trig[:, CLS, :, 0:JOINT], ACT.Copy).then_inc(trig_ready, 1)
                act.wait_ge(square_ready, 1)
                nc.scalar.activation(pr[1][:, :, :, :], pr[0][:, :, :, :], ACT.Sqrt).then_inc(root_ready, 1)
                act.wait_ge(arg_ready, 1)
                nc.scalar.activation(mag[:, :], mag[:, :], ACT.Tanh).then_inc(surprise_ready, 1)
                act.wait_ge(arg2_ready, 1)
                nc.scalar.activation(mag[:, :], mag[:, :], ACT.Tanh).then_inc(gate_ready, 1)

            @block.tensor
            def _(pe):
                pe.wait_ge(trig_ready, 2)
                for b in range(B):
                    for c in range(2):
                        keys = trig[:, b * TPB:(b + 1) * TPB, c, COL_K:COL_K + JOINT].rearrange("p t f -> p f t")
                        at = (b * 2 + c) * JOINT * TPB
                        for dst, col in ((ps_pre, C_STRICT), (ps_tot, C_ONES)):
                            n = nc.tensor.matmul(dst[:, at:at + JOINT * TPB], const[:, col:col + P], keys, start=True, stop=True)
                n.then_inc(sums_ready, 1)


def retrieval(nc, g):
    with ExitStack() as ctx:
        sb = lambda name, shape, dt=F32: ctx.enter_context(nc.sbuf_tensor(name, shape, dt))
        sem = lambda name: ctx.enter_context(nc.semaphore(name))
        kq, st, post, trig, V, h, raw = g["kq"], g["st"], g["post"], g["trig"], g["V"], g["h"], g["raw"]
        wg, gg, sc, const, wout, ones3, bias3 = g["wg"], g["gg"], g["sc"], g["const"], g["wout"], g["ones3"], g["bias3"]
        ident = const[:, C_ID:C_ID + P]
        kq_t = sb("kq_t", [P, 2, 2, P])
        kcls, vcls = sb("kcls", [1, P]), sb("vcls", [1, DIM])
        masked = sb("masked", [P, 2, P])
        ln_raw, ln_agg, ln_std, ln_rstd = sb("ln_raw", [P, 2, 6]), sb("ln_agg", [P, 2, 2]), sb("ln_std", [P, 2]), sb("ln_rstd", [P, 2])
        y, y_t = sb("y", [P, 2, DIM]), sb("y_t", [P, 2, KC, P])
        kq_ready, kqt_ready, kqt_copied, query_scaled = sem("kq_ready"), sem("kqt_ready"), sem("kqt_copied"), sem("query_scaled")
        s_ready, masked_ready, o_ready, state_ready, state_copied = sem("s_ready"), sem("masked_ready"), sem("o_ready"), sem("state_ready"), sem("state_copied")
        raw_done, agg_done, std_done, rstd_done, y_ready = sem("raw_done"), sem("agg_done"), sem("std_done"), sem("rstd_done"), sem("y_ready")
        yt_ready, yt_copied, w_ready, h_done, cls_kept = sem("yt_ready"), sem("yt_copied"), sem("w_ready"), sem("h_done"), sem("cls_kept")
        ps_kq, ps_s, ps_o0, ps_o1, ps_state, ps_yt, ps_w = g["bank"][0:7]
        ps_o = (ps_o0, ps_o1)
        LAGS = 4
        STATES = TPB + 1

        def order(eng, step):
            for s in range(1 + LAGS):
                step(0, CLS, s, 1, None, s % 4)
            with eng.Fori(0, B) as b:
                for s in range(LAGS):
                    step(1 + b * TPB, b * TPB, s, TPB, b, s % 4)
                with eng.Fori(LAGS // 4, TPB // 4) as r:
                    for i in range(4):
                        step(1 + b * TPB, b * TPB, r * 4 + i, TPB, b, i)
                for s in range(TPB, TPB + LAGS):
                    step(1 + b * TPB, b * TPB, s, TPB, b, s % 4)

        def live(s, lag, n):
            return not isinstance(s, int) or 0 <= s - lag < n

        def two_before(no, t):
            return no if isinstance(t, int) and t == 0 else no - 1

        with nc.Block() as block:
            @block.gpsimd
            def _(pool):
                def wide(column):
                    return column.unsqueeze(2).to_broadcast([P, 2, KF // 2])

                def step(n0, t0, s, n, b, q):
                    if live(s, 0, n):
                        no, t = n0 + s, t0 + s
                        tile = trig[:, bass.ds(t, 1), :, :].rearrange("p a c f -> p (a c) f")
                        pos = post[:, bass.ds(TPB if b is None else s, 1), :, :].rearrange("p a c f -> p (a c f)")
                        if isinstance(s, int) and s == 0:
                            after(pool, o_ready, no)
                            if b is not None:
                                pool.wait_ge(cls_kept, 2)
                        elif not (isinstance(s, int) and s < 3):
                            pool.wait_ge(o_ready, no - 2)
                        fk = kq[:, q, 0, 0:KF].rearrange("p (c f) -> p c f", c=2)
                        fq = kq[:, q, 1, 0:KF].rearrange("p (c f) -> p c f", c=2)
                        nc.gpsimd.tensor_tensor(fq, tile[:, :, COL_Q:COL_Q + KF // 2], wide(gg[:, 0, bass.ds(t, 1)]), ALU.mult).then_inc(query_scaled, 1)
                        nc.gpsimd.tensor_tensor(fk, tile[:, :, COL_K:COL_K + KF // 2], wide(wg[:, bass.ds(t, 1)]), ALU.mult)
                        nc.gpsimd.tensor_copy(kq[:, q, 0, KF:KF + PF], pos)
                        nc.gpsimd.tensor_tensor(kq[:, q, 1, KF:KF + PF], pos, gg[:, 1, bass.ds(t, 1)].to_broadcast([P, PF]), ALU.mult)
                        nc.gpsimd.tensor_copy(kq[:, q, 1, LT:P].rearrange("p (c f) -> p c f", c=2), tile[:, :, COL_L:COL_L + PLANES])
                        pool.wait_ge(query_scaled, no + 1)
                        nc.gpsimd.tensor_tensor(fq, fq, sc["wtab"].unsqueeze(1).to_broadcast([P, 2, KF // 2]), ALU.mult).then_inc(kq_ready, 1)
                order(pool, step)

            @block.tensor
            def _(pe):
                def step(n0, t0, s, n, b, q):
                    m = q % 2
                    if live(s, 0, n):
                        no = n0 + s
                        pe.wait_ge(kq_ready, no + 1)
                        after(pe, kqt_copied, no)
                        nc.tensor.transpose(ps_kq[:, 0:P], kq[:, q, 0, :], ident)
                        nc.tensor.transpose(ps_kq[:, P:2 * P], kq[:, q, 1, :], ident).then_inc(kqt_ready, 1)
                    if b is not None and isinstance(s, int) and s == 2:
                        pe.wait_ge(cls_kept, 2)
                        pe.wait_ge(yt_copied, n0)
                        nc.tensor.matmul(ps_state[0:LT, 0:DIM], kcls[0:1, 0:LT], vcls[:, :], start=True, stop=False,
                                         skip_group_check=True).then_inc(state_ready, 1)
                    if live(s, 2, n):
                        no, t = n0 + s - 2, s - 2
                        v = V[:, bass.ds((t0 + t) * DIM, DIM)]
                        pe.wait_ge(masked_ready, no + 1)
                        after(pe, y_ready, two_before(no, t))
                        nc.tensor.matmul(ps_o[m][:, 0:DIM], masked[:, m, :], v, start=True, stop=False)
                        if b is not None:
                            pe.wait_ge(state_copied, b * STATES + t + 1)
                        nc.tensor.matmul(ps_o[m][:, 0:DIM], kq_t[:, m, 1, :], st[:, m if b is not None else 1, :],
                                         start=False, stop=True).then_inc(o_ready, 1)
                        if b is not None:
                            nc.tensor.matmul(ps_state[0:LT, 0:DIM], kq[:, (q - 2) % 4, 0, 0:LT], v, start=False, stop=False,
                                             skip_group_check=True).then_inc(state_ready, 1)
                    if live(s, 1, n):
                        no = n0 + s - 1
                        pe.wait_ge(kqt_copied, no + 1)
                        after(pe, masked_ready, no)
                        nc.tensor.matmul(ps_s[:, 0:P], kq_t[:, 1 - m, 0, :], kq_t[:, 1 - m, 1, :], start=True, stop=True).then_inc(s_ready, 1)
                    if live(s, 3, n):
                        no = n0 + s - 3
                        pe.wait_ge(y_ready, no + 1)
                        after(pe, yt_copied, no)
                        for k in range(KC):
                            x = nc.tensor.transpose(ps_yt[:, k * P:(k + 1) * P], y[:, 1 - m, k * P:(k + 1) * P], ident)
                        x.then_inc(yt_ready, 1)
                    if live(s, 4, n):
                        no = n0 + s - 4
                        pe.wait_ge(yt_copied, no + 1)
                        after(pe, h_done, no)
                        for k in range(KC):
                            nc.tensor.matmul(ps_w[:, 0:DIM], y_t[:, m, k, :], wout[:, k, :], start=(k == 0), stop=False)
                        nc.tensor.matmul(ps_w[:, 0:DIM], ones3[:, :], bias3[:, 5 * DIM:6 * DIM], start=False, stop=True).then_inc(w_ready, 1)
                order(pe, step)

            @block.scalar
            def _(act):
                def step(n0, t0, s, n, b, q):
                    m = q % 2
                    if b is not None and isinstance(s, int) and s == 2:
                        act.wait_ge(state_ready, b * STATES + 1)
                        nc.scalar.activation(st[0:LT, 0, :], ps_state[0:LT, 0:DIM], ACT.Copy).then_inc(state_copied, 1)
                    if live(s, 0, n):
                        no = n0 + s
                        act.wait_ge(kqt_ready, no + 1)
                        after(act, o_ready, two_before(no, s))
                        nc.scalar.activation(kq_t[:, m, :, :], ps_kq[:, 0:2 * P].rearrange("p (c n) -> p c n", c=2), ACT.Copy).then_inc(kqt_copied, 1)
                    if live(s, 2, n):
                        no, t = n0 + s - 2, s - 2
                        if b is not None:
                            act.wait_ge(state_ready, b * STATES + t + 2)
                            nc.scalar.activation(st[0:LT, 1 - m, :], ps_state[0:LT, 0:DIM], ACT.Copy).then_inc(state_copied, 1)
                        act.wait_ge(agg_done, no + 1)
                        after(act, rstd_done, two_before(no, t))
                        nc.scalar.activation(ln_std[:, m:m + 1], ln_agg[:, m, 1:2], ACT.Sqrt, bias=g["eps"][:, :]).then_inc(std_done, 1)
                    if live(s, 3, n):
                        no, t = n0 + s - 3, s - 3
                        act.wait_ge(yt_ready, no + 1)
                        after(act, w_ready, two_before(no, t))
                        nc.scalar.activation(y_t[:, 1 - m, :, :], ps_yt[:, 0:DIM].rearrange("p (k n) -> p k n", k=KC), ACT.Copy).then_inc(yt_copied, 1)
                order(act, step)

            @block.vector
            def _(dve):
                def step(n0, t0, s, n, b, q):
                    m = q % 2
                    if b is None and s == 0:
                        dve.wait_ge(kq_ready, 1)
                        nc.vector.tensor_copy(kcls[:, :], kq[0:1, 0, 0, :]).then_inc(cls_kept, 1)
                        nc.vector.tensor_copy(vcls[:, :], V[0:1, CLS * DIM:NT * DIM]).then_inc(cls_kept, 1)
                    if live(s, 2, n):
                        no, t = n0 + s - 2, s - 2
                        dve.wait_ge(o_ready, no + 1)
                        nc.vector.bn_stats(ln_raw[:, m, :], ps_o[m][:, 0:DIM]).then_inc(raw_done, 1)
                        after(dve, y_ready, two_before(no, t))
                        dve.wait_ge(raw_done, no + 1)
                    if live(s, 1, n):
                        no, t = n0 + s - 1, s - 1
                        dve.wait_ge(s_ready, no + 1)
                        after(dve, o_ready, two_before(no, t))
                        mask = ident if b is None else const[:, C_TRI:C_TRI + P]
                        nc.vector.tensor_tensor(masked[:, 1 - m, :], ps_s[:, 0:P], mask, ALU.mult).then_inc(masked_ready, 1)
                    if live(s, 3, n):
                        no = n0 + s - 3
                        dve.wait_ge(std_done, no + 1)
                        nc.vector.reciprocal(ln_rstd[:, 1 - m:2 - m], ln_std[:, 1 - m:2 - m]).then_inc(rstd_done, 1)
                        dve.wait_ge(rstd_done, no + 1)
                        after(dve, yt_ready, two_before(no, s - 3))
                        nc.vector.tensor_scalar(y[:, 1 - m, :], ps_o[1 - m][:, 0:DIM], ln_agg[:, 1 - m, 0:1], ln_rstd[:, 1 - m:2 - m],
                                                ALU.subtract, ALU.mult).then_inc(y_ready, 1)
                    if live(s, 2, n):
                        nc.vector.bn_aggr(ln_agg[:, m, :], ln_raw[:, m, :]).then_inc(agg_done, 1)
                    if live(s, 4, n):
                        no, t = n0 + s - 4, t0 + s - 4
                        dve.wait_ge(w_ready, no + 1)
                        tile = h[:, bass.ds(t * DIM, DIM)]
                        nc.vector.tensor_tensor(tile, ps_w[:, 0:DIM], tile, ALU.add).then_inc(h_done, 1)
                        dve.wait_ge(h_done, no + 1)
                        nc.vector.bn_stats(raw[:, bass.ds(t * 6, 6)], tile)
                order(dve, step)


ROUTED = (IMG * IMG + 1) // 2 - 1
FH = 4 * DIM
FC = FH // P
DIGIT, ROUNDS = 4, 8
NCAND = 2 ** DIGIT - 1
COLS = TPB + 1


def router(nc, g, a):
    with ExitStack() as ctx:
        sb = lambda name, shape, dt=F32: ctx.enter_context(nc.sbuf_tensor(name, shape, dt))
        sem = lambda name: ctx.enter_context(nc.semaphore(name))
        h, mean, rstd, sw, const = g["h"], g["mean"], g["rstd"], g["sw"], g["const"]
        wr, prod, xn = sb("wr", [P, DIM + 1]), sb("w_prod", [P, DIM]), sb("w_xn", [P, 2, DIM])
        tok_w = sb("tok_w", [P, NT])
        w = sb("w_cols", [P, B, COLS])
        ge = sb("ge", [P, B, NCAND, COLS])
        cnt = sb("cnt", [P, B, NCAND])
        key, cand, sign, cut = (sb(n, [P, B, NCAND], I32) for n in ("key", "cand", "sign", "cut"))
        over = sb("over", [P, B, NCAND])
        dig_f, dig_i = sb("dig_f", [P, B]), sb("dig_i", [P, B], I32)
        prefix = sb("prefix", [P, B], I32)
        gt, eq, rank = sb("gt", [P, B, COLS]), sb("eq", [P, B, COLS]), sb("rank", [P, B, COLS])
        ngt = sb("ngt", [P, B])
        xn_ready, step_done, sums_wanted, sums_ready = sem("r_xn_ready"), sem("r_step_done"), sem("sums_wanted"), sem("r_sums_ready")
        w_done, wr_loaded = sem("w_done"), sem("wr_loaded")
        wslot, digits = sb("wslot", [P, 2]), sb("digits", [P, ROUNDS, NCAND], I32)
        ps, ps_rank, ps_cols = g["bank"][0:3]
        ones, tri = const[:, C_ONES:C_ONES + P], const[:, C_TRI:C_TRI + P]
        with nc.Block() as block:
            @block.sync
            def _(sp):
                sp.dma_start(wr[:, :], a["ffn_wr"].to_broadcast([P, DIM + 1])).then_inc(wr_loaded, 16)
                sp.dma_start(digits[:, :, :], a["digits"].to_broadcast([P, ROUNDS * NCAND])
                             .rearrange("p (r n) -> p r n", r=ROUNDS)).then_inc(wr_loaded, 16)
                sp.dma_start(g["ffn_w1"][:, :, :], a["ffn_w1"].rearrange("(k p) n -> p k n", p=P)).then_inc(wr_loaded, 16)
                sp.dma_start(g["ffn_w2"][:, :, :], a["ffn_w2"].rearrange("(k p) n -> p k n", p=P)).then_inc(wr_loaded, 16)
                sp.dma_start(g["ffn_b1"][:, :], a["ffn_b1"]).then_inc(wr_loaded, 16)
                sp.wait_ge(wr_loaded, 80)

            @block.vector
            def _(dve):
                dve.wait_ge(wr_loaded, 80)
                V = nc.vector
                count = [0]

                def done(ins):
                    count[0] += 1
                    ins.then_inc(step_done, 1)
                    dve.wait_ge(step_done, count[0])

                def weigh(t, i, no):
                    tile = h[:, bass.ds(t * DIM, DIM)]
                    V.tensor_scalar(xn[:, i, :], tile, mean[:, bass.ds(t, 1)], rstd[:, bass.ds(t, 1)], ALU.subtract, ALU.mult).then_inc(xn_ready, 1)
                    dve.wait_ge(xn_ready, no + 1)
                    V.tensor_tensor_reduce(prod[:, :], xn[:, i, :], wr[:, 0:DIM], 1.0, 0.0, ALU.mult, ALU.add, wslot[:, i:i + 1]).then_inc(w_done, 1)
                    dve.wait_ge(w_done, no + 1)
                    V.tensor_copy(tok_w[:, bass.ds(t, 1)], wslot[:, i:i + 1])
                with dve.Fori(0, NPAIR // 2) as r:
                    for i in range(2):
                        weigh(r * 2 + i, i, r * 2 + i)
                weigh(CLS, 0, CLS)
                V.memset(w[:, :, :], -3.4e38)
                done(V.memset(prefix[:, :], 0))
                done(V.tensor_scalar(tok_w[:, :], tok_w[:, :], wr[:, DIM:DIM + 1], None, ALU.add))
                V.tensor_copy(w[:, :, 1:COLS], tok_w[:, 0:NPAIR].rearrange("p (b t) -> p b t", b=B))
                done(V.tensor_copy(w[0:1, :, 0:1], tok_w[0:1, CLS:NT].unsqueeze(1).to_broadcast([1, B, 1])))
                four = [P, B, NCAND, COLS]
                for r in range(ROUNDS):
                    shift = DIGIT * (ROUNDS - 1 - r)
                    done(V.tensor_tensor(cand[:, :, :], prefix[:, :].unsqueeze(2).to_broadcast([P, B, NCAND]),
                                         digits[:, r, :].unsqueeze(1).to_broadcast([P, B, NCAND]), ALU.bitwise_or))
                    done(V.tensor_scalar(sign[:, :, :], cand[:, :, :], 31, 0x7FFFFFFF, ALU.arith_shift_right, ALU.bitwise_and))
                    done(V.tensor_tensor(cut[:, :, :], cand[:, :, :], sign[:, :, :], ALU.bitwise_xor))
                    done(V.tensor_scalar(cut[:, :, :], cut[:, :, :], -1, None, ALU.bitwise_xor))
                    for b in range(B):
                        n = V.tensor_tensor(ge[:, b], w[:, b, :].unsqueeze(1).to_broadcast([P, NCAND, COLS]),
                                            cut[:, b, :].bitcast(F32).unsqueeze(2).to_broadcast([P, NCAND, COLS]), ALU.is_ge)
                    done(n)
                    V.tensor_reduce(cnt[:, :, :], ge[:, :, :, :], AX_X, ALU.add).then_inc(sums_wanted, 1)
                    dve.wait_ge(sums_ready, r + 1)
                    done(V.tensor_scalar(over[:, :, :], ps[:, 0:B * NCAND].rearrange("p (b n) -> p b n", b=B), float(ROUTED), None, ALU.is_ge))
                    done(V.tensor_reduce(dig_f[:, :], over[:, :, :], AX_X, ALU.add))
                    done(V.tensor_copy(dig_i[:, :], dig_f[:, :]))
                    if shift:
                        done(V.tensor_scalar(dig_i[:, :], dig_i[:, :], shift, None, ALU.logical_shift_left))
                    done(V.tensor_tensor(prefix[:, :], prefix[:, :], dig_i[:, :], ALU.bitwise_or))
                done(V.tensor_scalar(dig_i[:, :], prefix[:, :], 31, 0x7FFFFFFF, ALU.arith_shift_right, ALU.bitwise_and))
                done(V.tensor_tensor(prefix[:, :], prefix[:, :], dig_i[:, :], ALU.bitwise_xor))
                done(V.tensor_scalar(prefix[:, :], prefix[:, :], -1, None, ALU.bitwise_xor))
                thr = prefix[:, :].bitcast(F32).unsqueeze(2).to_broadcast([P, B, COLS])
                V.tensor_tensor(gt[:, :, :], w[:, :, :], thr, ALU.is_gt)
                done(V.tensor_tensor(eq[:, :, :], w[:, :, :], thr, ALU.is_equal))
                V.tensor_reduce(ngt[:, :], gt[:, :, :], AX_X, ALU.add).then_inc(sums_wanted, 1)
                dve.wait_ge(sums_ready, ROUNDS + 1)
                done(V.tensor_scalar(ngt[:, :], ps[:, 0:B], -1.0, float(ROUTED), ALU.mult, ALU.add))
                for b in range(B):
                    n = V.tensor_tensor_scan(rank[:, b, :], ones[:, 0:COLS], ps_cols[:, b * COLS:(b + 1) * COLS], 0.0, ALU.mult, ALU.add)
                done(n)
                flat = rank[:, :, :].rearrange("p b t -> p (b t)")
                done(V.tensor_tensor(flat, flat, ps_cols[:, 0:B * COLS], ALU.subtract))
                done(V.tensor_tensor(flat, flat, ps_rank[:, 0:B * COLS], ALU.add))
                for b in range(B):
                    n = V.tensor_scalar(rank[:, b, :], rank[:, b, :], ngt[:, b:b + 1], None, ALU.is_le)
                done(n)
                done(V.tensor_tensor(eq[:, :, :], eq[:, :, :], rank[:, :, :], ALU.mult))
                done(V.tensor_tensor(gt[:, :, :], gt[:, :, :], eq[:, :, :], ALU.add))
                V.tensor_tensor(sw[:, 0:NPAIR].rearrange("p (b t) -> p b t", b=B), gt[:, :, 1:COLS], w[:, :, 1:COLS], ALU.mult)
                V.tensor_tensor(sw[:, NPAIR:NPAIR + B], gt[:, :, 0], w[:, :, 0], ALU.mult)

            @block.tensor
            def _(pe):
                for r in range(ROUNDS):
                    pe.wait_ge(sums_wanted, r + 1)
                    nc.tensor.matmul(ps[:, 0:B * NCAND], ones, cnt[:, :, :].rearrange("p b n -> p (b n)"), start=True, stop=True).then_inc(sums_ready, 1)
                pe.wait_ge(sums_wanted, ROUNDS + 1)
                eqs = eq[:, :, :].rearrange("p b t -> p (b t)")
                nc.tensor.matmul(ps_rank[:, 0:B * COLS], tri, eqs, start=True, stop=True)
                nc.tensor.matmul(ps_cols[:, 0:B * COLS], ones, eqs, start=True, stop=True)
                nc.tensor.matmul(ps[:, 0:B], ones, ngt[:, :], start=True, stop=True).then_inc(sums_ready, 1)


def feed_forward(nc, g, a, out):
    with ExitStack() as ctx:
        sb = lambda name, shape, dt=F32: ctx.enter_context(nc.sbuf_tensor(name, shape, dt))
        sem = lambda name: ctx.enter_context(nc.semaphore(name))
        w1, w2, b1 = g["ffn_w1"], g["ffn_w2"], g["ffn_b1"]
        xn = sb("f_xn", [P, UNIT, DIM])
        xn_t = sb("f_xn_t", [P, KC, UTOK])
        hid = sb("f_hid", [P, FC, UTOK])
        res = sb("f_res", [P, 2, UNIT, DIM])
        xn_ready, base_done, xt_ready, xt0_copied, xt1_copied = sem("f_xn_ready"), sem("f_base_done"), sem("f_xt_ready"), sem("f_xt0"), sem("f_xt1")
        hid_ready, gelu_done, y_ready, res_ready = sem("f_hid_ready"), sem("f_gelu_done"), sem("f_y_ready"), sem("f_res_ready")
        stored = [sem("stored0"), sem("stored1")]
        ps_t0, ps_t1 = g["bank"][0:2]
        ring, ps_y = g["bank"][2:5], g["bank"][5:8]
        h, mean, rstd, sw, ident = g["h"], g["mean"], g["rstd"], g["sw"], g["const"][:, C_ID:C_ID + P]
        ones3, bias3 = g["ones3"], g["bias3"]
        HC = UNIT // 2
        is_cls = lambda u: isinstance(u, int) and u == NUNIT
        tiles = lambda u: 1 if is_cls(u) else UNIT
        first = lambda u: isinstance(u, int) and u == 0

        def order(eng, unit):
            unit(0, 0)
            unit(1, 1)
            with eng.Fori(1, NUNIT // 2 - 1) as r:
                unit(r * 2, 0)
                unit(r * 2 + 1, 1)
            unit(NUNIT - 2, 0)
            unit(NUNIT - 1, 1)
            unit(NUNIT, 0)

        with nc.Block() as block:
            @block.sync
            def _(sp):
                rows = out.rearrange("b t d -> (b t) d")
                seq = IMG * IMG + 1
                for b in range(B):
                    with sp.Fori(0, NUNIT // B // 2) as r:
                        for i in range(2):
                            sp.wait_ge(res_ready, (b * (NUNIT // B) + r * 2 + i + 1) * HC)
                            sp.dma_start(rows[bass.ds(b * seq + 1 + (r * 2 + i) * UTOK, UTOK), :].rearrange("(i p) d -> p i d", p=P),
                                         res[:, i, :, :]).then_inc(stored[i], 16)
                for b in range(B):
                    sp.wait_ge(res_ready, NUNIT * HC + b + 1)
                    sp.dma_start(rows[b * seq:b * seq + 1, :], res[0:1, 0, b, :]).then_inc(stored[0], 16)
                sp.wait_ge(stored[0], 16 * (NUNIT // 2 + B))
                sp.wait_ge(stored[1], 16 * (NUNIT // 2))

            @block.vector
            def _(dve):
                def normalise(u):
                    after(dve, xt_ready, u)
                    after(dve, base_done, u)
                    for i in range(tiles(u)):
                        t = u * UNIT + i
                        n = nc.vector.tensor_scalar(xn[:, i, :], h[:, bass.ds(t * DIM, DIM)], mean[:, bass.ds(t, 1)],
                                                    rstd[:, bass.ds(t, 1)], ALU.subtract, ALU.mult)
                    n.then_inc(xn_ready, 1)

                def copy_xt(u):
                    dve.wait_ge(xt_ready, u + 1)
                    after(dve, hid_ready, u * FC)
                    n = tiles(u) * P
                    nc.vector.tensor_copy(xn_t[:, 1, 0:n], ps_t1[:, 0:n]).then_inc(xt1_copied, 1)

                def combine(u, m):
                    for c in range(1 if is_cls(u) else HC):
                        dve.wait_ge(y_ready, u * HC + c + 1)
                        dve.wait_ge(base_done, u + 1)
                        if not (isinstance(u, int) and u < 2):
                            dve.wait_ge(stored[m], 16 * ((u - m) // 2) if isinstance(u, int) else (u - m) * 8)
                        for i in range(2):
                            t = NPAIR + i if is_cls(u) else u * UNIT + 2 * c + i
                            src = 0 if is_cls(u) else i
                            base = h[:, CLS * DIM:NT * DIM] if is_cls(u) else h[:, bass.ds(t * DIM, DIM)]
                            k = nc.vector.scalar_tensor_tensor(out=res[:, m, 2 * c + i, :], in0=ps_y[c][:, src * DIM:(src + 1) * DIM],
                                                               scalar=sw[:, bass.ds(t, 1)], in1=base, op0=ALU.mult, op1=ALU.add)
                            if is_cls(u):
                                k.then_inc(res_ready, 1)
                        if not is_cls(u):
                            k.then_inc(res_ready, 1)

                def unit(u, m):
                    if first(u):
                        normalise(u)
                        copy_xt(u)
                    if not is_cls(u):
                        normalise(u + 1)
                        copy_xt(u + 1)
                    combine(u, m)
                order(dve, unit)

            @block.gpsimd
            def _(pool):
                def unit(u, m):
                    pool.wait_ge(xn_ready, u + 1)
                    for i in range(tiles(u)):
                        tile = h[:, bass.ds((u * UNIT + i) * DIM, DIM)]
                        n = nc.gpsimd.tensor_tensor(tile, tile, xn[:, i, :], ALU.add)
                    n.then_inc(base_done, 1)
                order(pool, unit)

            @block.scalar
            def _(act):
                def copy_xt(u):
                    act.wait_ge(xt_ready, u + 1)
                    after(act, hid_ready, u * FC)
                    n = tiles(u) * P
                    nc.scalar.activation(xn_t[:, 0, 0:n], ps_t0[:, 0:n], ACT.Copy).then_inc(xt0_copied, 1)

                def unit(u, m):
                    n = tiles(u) * P
                    if first(u):
                        copy_xt(u)
                    for c in range(FC):
                        act.wait_ge(hid_ready, u * FC + c + 1)
                        if c == 0:
                            after(act, y_ready, u * HC)
                        nc.scalar.activation(hid[:, c, 0:n], ring[c % 3][:, 0:n], ACT.Gelu_apprx_tanh, bias=b1[:, c:c + 1]).then_inc(gelu_done, 1)
                    if not is_cls(u):
                        copy_xt(u + 1)
                order(act, unit)

            @block.tensor
            def _(pe):
                def turn(u):
                    pe.wait_ge(xn_ready, u + 1)
                    after(pe, xt0_copied, u)
                    after(pe, xt1_copied, u)
                    for k, dst in enumerate((ps_t0, ps_t1)):
                        for i in range(tiles(u)):
                            t = nc.tensor.transpose(dst[:, i * P:(i + 1) * P], xn[:, i, k * P:(k + 1) * P], ident)
                    t.then_inc(xt_ready, 1)

                def unit(u, m):
                    n = tiles(u) * P
                    if first(u):
                        turn(u)
                    pe.wait_ge(xt0_copied, u + 1)
                    pe.wait_ge(xt1_copied, u + 1)
                    for c in range(FC):
                        if c == 0 or c > 2:
                            after(pe, gelu_done, u * FC + (c - 2 if c else 0))
                        for k in range(KC):
                            t = nc.tensor.matmul(ring[c % 3][:, 0:n], w1[:, k, c * P:(c + 1) * P], xn_t[:, k, 0:n], start=(k == 0), stop=(k == KC - 1))
                        t.then_inc(hid_ready, 1)
                    if not is_cls(u):
                        turn(u + 1)
                    for c in range(1 if is_cls(u) else HC):
                        pe.wait_ge(gelu_done, (u + 1) * FC)
                        after(pe, res_ready, (u - 1) * HC + c + 1)
                        for i in range(1 if is_cls(u) else 2):
                            i0 = (2 * c + i) * P
                            for k in range(FC):
                                nc.tensor.matmul(ps_y[c][:, i * DIM:(i + 1) * DIM], hid[:, k, i0:i0 + P], w2[:, k, :], start=(k == 0), stop=False)
                            t = nc.tensor.matmul(ps_y[c][:, i * DIM:(i + 1) * DIM], ones3[:, :], bias3[:, 6 * DIM:7 * DIM], start=False, stop=True)
                        t.then_inc(y_ready, 1)
                order(pe, unit)


def constants():
    c = np.zeros((P, NCONST), np.float32)
    p = np.arange(P)
    c[:, C_ID:C_ID + P] = np.eye(P)
    c[:, C_TRI:C_TRI + P] = p[:, None] <= p[None, :]
    c[:, C_STRICT:C_STRICT + P] = p[:, None] < p[None, :]
    c[:, C_ONES:C_ONES + P] = 1
    half = HD // 2
    inv_freq = (1.0 / 10000.0 ** (np.arange(0, half, 2, dtype=np.float32) / half)).astype(np.float32)
    row, col = (p % WTOK) // WIN, p % WIN
    ang = np.concatenate([row[:, None] * inv_freq, col[:, None] * inv_freq], 1).astype(np.float32)
    c[:, C_COS:C_COS + HD] = np.repeat(np.cos(ang), 2, axis=1)
    s = np.repeat(np.sin(ang), 2, axis=1)
    s[:, 0::2] *= -1
    c[:, C_SIN:C_SIN + HD] = s
    c[:, C_HEAD:C_HEAD + 4] = p[:, None] // HD == np.arange(4)
    c[:, C_POS:C_POS + TPB] = 1 + p[:, None] + P * np.arange(TPB)
    seg = np.ones((8, TPB))
    seg[:, 0] = 0
    c[:, C_SEG:] = seg.reshape(1, -1)
    return c


def program(nc, a, out):
    with ExitStack() as ctx:
        sb = lambda name, shape, dt=F32: ctx.enter_context(nc.sbuf_tensor(name, shape, dt))
        g = {"bank": [ctx.enter_context(nc.psum_tensor(f"bank{i}", [P, 512], F32)) for i in range(8)]}
        g["const"] = sb("const", [P, NCONST])
        g["h"] = sb("h", [P, NT * DIM])
        g["raw"] = sb("raw", [P, NT * 6])
        g["mean"], g["rstd"] = sb("mean", [P, NT]), sb("rstd", [P, NT])
        g["scal"] = sb("scal", [P, NSCAL])
        scalars = sb("scalars", [P, 10 + KF // 2])
        at = 0
        g["sc"] = {}
        for name, n in (("setw", SETS), ("posw", 1), ("rscale", 1), ("rthr", 1), ("count", 1), ("ltmw", 1), ("nthr", 1), ("wtab", KF // 2)):
            g["sc"][name] = scalars[:, at:at + n]
            at += n
        g["ones3"], g["bias3"] = sb("ones3", [3, P], BF16), sb("bias3", [3, NBIAS], BF16)
        g["half_pi"], g["eps"] = sb("half_pi", [P, 1]), sb("eps", [P, 1])
        g["sw"] = sb("sw", [P, NPAIR + B])
        with ExitStack() as mid:
            sm = lambda name, shape, dt=F32: mid.enter_context(nc.sbuf_tensor(name, shape, dt))
            g["wout"] = sm("wout", [P, KC, DIM])
            g["st"] = sm("st", [P, 2, DIM])
            g["kq"] = sm("kq", [P, 4, 2, P])
            g["post"] = sm("post", [P, TPB + 1, 2, PLANES])
            g["rpos"] = sm("rpos", [P, TPB])
            g["wg"], g["gg"], g["jcls"] = sm("wg", [P, NT]), sm("gg", [P, 2, NT]), sm("jcls", [P, 2 * JOINT])
            prologue(nc, g, a)
            tokenizer(nc, g, a["x_t"], a["qkv_w"], a["proj_w"])
            normaliser(nc, g, "_1")
            with ExitStack() as late:
                g["V"] = late.enter_context(nc.sbuf_tensor("V", [P, NT * DIM], F32))
                g["th"] = late.enter_context(nc.sbuf_tensor("th", [P, NT * NCOL], F32))
                encoders(nc, g, a)
                g["trig"] = late.enter_context(nc.sbuf_tensor("trig", [P, NT, 2, NPH], F32))
                phasors(nc, g)
                retrieval(nc, g)
        normaliser(nc, g, "_2")
        g["ffn_w1"], g["ffn_w2"], g["ffn_b1"] = sb("ffn_w1", [P, KC, FH]), sb("ffn_w2", [P, FC, DIM]), sb("ffn_b1", [P, FC])
        router(nc, g, a)
        feed_forward(nc, g, a, out)


def columns(v):
    return v.reshape(-1, P).T


def kernel(**inputs):
    import concourse.bacc as bacc
    from concourse.bass_utils import run_bass_kernel_spmd

    i = {k.removeprefix("L0_"): np.asarray(v) for k, v in inputs.items()}
    w = WIN
    mem = i["attn_ltm_binding_mem"]
    w2 = np.zeros((NHID * P, NCOL), np.float32)
    b2 = np.zeros((NCOL, 2), np.float32)
    b2[:, 1] = 1.0
    b2[COL_G, 1] = 0.5
    at = 0
    for name, col, n in (("ke", COL_K + JOINT, PLANES), ("qe", COL_Q + JOINT, PLANES), ("lke", COL_L, PLANES), ("gate", COL_G, 1)):
        hidden = i[f"attn_{name}_w2"].shape[0]
        w2[at:at + hidden, col:col + n] = i[f"attn_{name}_w2"]
        b2[col:col + n, 0] = i[f"attn_{name}_b2"]
        at += hidden
    digits = (np.arange(1, NCAND + 1, dtype=np.int64)[None, :] << (DIGIT * (ROUNDS - 1 - np.arange(ROUNDS)))[:, None])
    arrays = {
        "const": constants(),
        "digits": digits.astype(np.uint32).view(np.int32).reshape(1, -1),
        "x_t": i["x"].reshape(B, IMG // w, w, IMG // w, w, DIM).transpose(5, 0, 1, 3, 2, 4).reshape(DIM, NUNIT, UTOK),
        "cls": i["cls_tok"].reshape(1, DIM),
        "qkv_w": i["tok_qkv_w"].T,
        "proj_w": i["tok_proj_w"].T,
        "bias": np.concatenate([i["tok_qkv_b"], i["tok_proj_b"], i["attn_v_b"], i["attn_out_b"], i["ffn_b2"]])[None],
        "scal": np.concatenate([i["attn_set_weights"]] + [i[f"attn_{n}"].reshape(1) for n in (
            "pos_weight", "surprise_scale", "surprise_bias", "resonance_scale", "resonance_threshold", "ltm_weight", "ltm_count")]
            + [i["attn_pos_freqs"]])[None],
        "enc_w1": np.concatenate([i[f"attn_{n}_w1"] for n in ("ke", "qe", "lke", "gate")], axis=1),
        "enc_b1": columns(np.concatenate([i[f"attn_{n}_b1"] for n in ("ke", "qe", "lke", "gate")])),
        "enc_w2": w2,
        "enc_b2": b2,
        "enc_wv": i["attn_v_w"],
        "out_w": i["attn_out_w"],
        "ln_g": columns(i["attn_out_ln_g"]),
        "ln_b": columns(i["attn_out_ln_b"]),
        "ltm": np.concatenate([mem.real, mem.imag], axis=0),
        "ffn_wr": np.concatenate([i["ffn_wr"].reshape(-1), i["ffn_br"]])[None],
        "ffn_w1": i["ffn_w1"],
        "ffn_b1": columns(i["ffn_b1"]),
        "ffn_w2": i["ffn_w2"],
    }
    arrays = {k: np.ascontiguousarray(v) for k, v in arrays.items()}
    nc = bacc.Bacc("TRN2", target_bir_lowering=False, num_devices=1)
    a = {k: nc.dram_tensor(f"in_{k}", v.shape, mybir.dt.from_np(v.dtype), kind="ExternalInput").ap() for k, v in arrays.items()}
    out = nc.dram_tensor("out", [B, IMG * IMG + 1, DIM], F32, kind="ExternalOutput").ap()
    program(nc, a, out)
    r = run_bass_kernel_spmd(nc, [{f"in_{k}": v for k, v in arrays.items()}], core_ids=[0])
    return r.results[0]["out"]
```

```python
from contextlib import ExitStack

import numpy as np

import concourse.bass as bass
from concourse import mybir

ALU = mybir.AluOpType
ACT = mybir.ActivationFunctionType
AX_X = mybir.AxisListType.X
F32 = mybir.dt.float32
F32R = mybir.dt.float32r
BF16 = mybir.dt.bfloat16
I32 = mybir.dt.int32

P = 128
B, IMG, DIM = 2, 64, 256
KC = DIM // P
WIN, HEADS = 8, 8
HD = DIM // HEADS
WTOK = WIN * WIN
NPAIR = B * IMG * IMG // P
UNIT = 4
NUNIT = NPAIR // UNIT
UTOK = UNIT * P
TPB = IMG * IMG // P
CLS = NPAIR
NT = NPAIR + 1
EPS = 1e-5
SCALE = HD ** -0.5

C_ID, C_TRI, C_STRICT, C_ONES = 0, P, 2 * P, 3 * P
C_COS = 4 * P
C_SIN = C_COS + HD
C_HEAD = C_SIN + HD
C_POS = C_HEAD + 4
C_SEG = C_POS + TPB
NCONST = C_SEG + 8 * TPB


def after(eng, sem, value):
    if not isinstance(value, int) or value > 0:
        eng.wait_ge(sem, value)


HI, LO = 0, 1


def high(ap):
    return ap.bitcast(F32)


def parts(f):
    return f(HI), f(LO)


def product(nc, out, lhs, rhs, start, stop):
    nc.tensor.matmul(out, lhs[HI], rhs[HI], start=start, stop=False)
    nc.tensor.matmul(out, lhs[HI], rhs[LO], start=False, stop=False)
    return nc.tensor.matmul(out, lhs[LO], rhs[HI], start=False, stop=stop)


def tokenizer(nc, g, a):
    with ExitStack() as ctx:
        sb = lambda name, shape, dt=F32: ctx.enter_context(nc.sbuf_tensor(name, shape, dt))
        sem = lambda name: ctx.enter_context(nc.semaphore(name))
        spare = g["V"]
        at = [0]

        def early(n, m):
            at[0] += n * m
            return spare[:, at[0] - n * m:at[0]].rearrange("p (k n) -> p k n", n=m)
        wqkv = early(KC, 3 * DIM)
        enc_w = [early(n, m) for n, m in ((KC, NHID * P), (KC, DIM), (NHID, NCOL))]
        wqkv_hl = sb("wqkv_hl", [P, 2, KC, 3 * DIM], F32R)
        wproj = sb("wproj", [P, KC, DIM])
        x_t, enc_hl = a["x_t"], (g["enc_w1"], g["enc_wv"], g["enc_w2"])
        xt = early(UNIT, KC * P).rearrange("p j (k n) -> p j k n", k=KC)
        xt_hl = sb("xt_hl", [P, 2, 2, KC, P], F32R)
        rope_c, rope_s, qk_rot = (early(1, 2 * DIM)[:, 0] for _ in range(3))
        q_t = sb("q_t", [P, KC, P])
        k_blk = early(KC, 8 * WTOK).rearrange("p k (w h n) -> p k w h n", w=2, h=4)
        v_half = early(UNIT, 2 * P).rearrange("p j (w n) -> p j w n", w=2)
        probs = sb("probs", [P, HEADS, WTOK])
        smax = sb("smax", [P, HEADS])
        ssum = sb("ssum", [P, HEADS])
        sinv = sb("sinv", [P, HEADS])
        p_t = sb("p_t", [P, 4, 2, WTOK])
        o_t = early(KC, UTOK)

        enc_loaded, enc_high = sem("enc_loaded"), sem("enc_high")
        w_loaded, w_high, w_split, x_high, x_split = sem("w_loaded"), sem("w_high"), sem("w_split"), sem("x_high"), sem("x_split")
        x_loaded = [sem(f"x_loaded{j}") for j in range(UNIT)]
        qk_ready, v_ready, tq_ready, sc_ready = sem("qk_ready"), sem("v_ready"), sem("tq_ready"), sem("sc_ready")
        pt_ready, av_ready, proj_ready = sem("pt_ready"), sem("av_ready"), sem("proj_ready")
        rope_done, rope_added, v_copied, qt_copied = sem("rope_done"), sem("rope_added"), sem("v_copied"), sem("qt_copied")
        kblk_done, max_done, sub_done, exp_done, sum_done = sem("kblk_done"), sem("max_done"), sem("sub_done"), sem("exp_done"), sem("sum_done")
        inv_done = sem("inv_done")
        p_ready, pt_copied, out0_copied, out1_copied = sem("p_ready"), sem("pt_copied"), sem("out0_copied"), sem("out1_copied")
        h_copied = sem("h_copied")

        ps_qk, ps_v, ps_tq, ps_sc, ps_pt, ps_av0, ps_av1, ps_proj = g["bank"]
        const, h, raw = g["const"], g["h"], g["raw"]
        ident = const[:, C_ID:C_ID + P]
        cos = const[:, C_COS:C_COS + HD]
        sin = const[:, C_SIN:C_SIN + HD]
        ones3, bias3 = g["ones3"], g["bias3"]
        LAST = NPAIR

        def live(s, lag):
            return not isinstance(s, int) or 0 <= s - lag < LAST

        def steps(eng, step):
            for s in range(UNIT):
                step(s, s, 0)
            with eng.Fori(1, NUNIT) as u:
                for j in range(UNIT):
                    step(u * UNIT + j, j, u)
            for s in range(LAST, LAST + 4):
                step(s, s % UNIT, NUNIT)

        def split_steps(eng, step):
            for s in range(UNIT):
                step(s, s, 0)
            with eng.Fori(1, NUNIT - 1) as u:
                for j in range(UNIT):
                    step(u * UNIT + j, j, u)
            for s in range(LAST - UNIT, LAST + 4):
                step(s, s % UNIT, s // UNIT)

        def next_x(s, j, u, split):
            if not isinstance(s, int) or s + 1 < LAST:
                split(s + 1, (j + 1) % UNIT, u + (j + 1) // UNIT)

        def o_rows(q, c, pair):
            return o_t[q * HD:(q + 1) * HD, c, :].rearrange("p (r w n) -> p w r n", r=WIN, w=WIN)[:, 2 * pair:2 * pair + 2]

        def o_head(ps, q):
            return ps[q * HD:(q + 1) * HD, :].rearrange("p (w h r n) -> p w h r n", w=2, h=4, r=WIN)[:, :, q]

        def unit_done(s, j):
            return j == 2 and (not isinstance(s, int) or s >= UNIT)

        with nc.Block() as block:
            @block.sync
            def _(sp):
                sp.dma_start(wqkv[:, :, :], a["qkv_w"].rearrange("(k p) n -> p k n", p=P)).then_inc(w_loaded, 16)
                sp.dma_start(wproj[:, :, :], a["proj_w"].rearrange("(k p) n -> p k n", p=P)).then_inc(w_loaded, 16)

                for j in range(UNIT):
                    sp.dma_start(xt[:, j, :, :], x_t[:, 0:1, j * P:(j + 1) * P]
                                 .rearrange("(k p) a n -> p k (a n)", p=P)).then_inc(x_loaded[j], 16)
                for w, name in zip(enc_w, ("enc_w1", "enc_wv", "enc_w2")):
                    sp.dma_start(w[:, :, :], a[name].rearrange("(k p) n -> p k n", p=P)).then_inc(enc_loaded, 16)
                with sp.Fori(1, NUNIT) as u:
                    for j in range(UNIT):
                        sp.wait_ge(x_split, u * UNIT + j - 3)
                        sp.dma_start(xt[:, j, :, :], x_t[:, bass.ds(u, 1), j * P:(j + 1) * P]
                                     .rearrange("(k p) a n -> p k (a n)", p=P)).then_inc(x_loaded[j], 16)

            @block.tensor
            def _(pe):
                pe.wait_ge(w_loaded, 32)
                pe.wait_ge(w_split, 1)

                def project(u, half):
                    if half:
                        pe.wait_ge(h_copied, (u - 1) * 2 + half)
                    for i in range(2):
                        po, tile = ps_proj[:, i * DIM:(i + 1) * DIM], 2 * half + i
                        for k in range(KC):
                            nc.tensor.matmul(po, o_t[:, k, tile * P:(tile + 1) * P], wproj[:, k, :], start=(k == 0), stop=False)
                        t = nc.tensor.matmul(po, ones3[:, :], bias3[:, 3 * DIM:4 * DIM], start=False, stop=True)
                    t.then_inc(proj_ready, 1)

                def step(s, j, u):
                    if live(s, 1):
                        pe.wait_ge(rope_added, s)
                        after(pe, kblk_done, s - 1)
                        for c in range(4):
                            t = nc.tensor.transpose(ps_tq[:, c * P:(c + 1) * P], qk_rot[:, c * P:(c + 1) * P], ident)
                        t.then_inc(tq_ready, 1)
                    if live(s, 0):
                        pe.wait_ge(x_split, s + 1)
                        after(pe, rope_done, s)
                        for k in range(KC):
                            product(nc, ps_qk[:, :], parts(lambda c: xt_hl[:, j % 2, c, k, :]),
                                    parts(lambda c: wqkv_hl[:, c, k, 0:2 * DIM]), k == 0, False)
                        nc.tensor.matmul(ps_qk[:, :], ones3[:, :], bias3[:, 0:2 * DIM], start=False, stop=True).then_inc(qk_ready, 1)
                        after(pe, v_copied, s)
                        for k in range(KC):
                            product(nc, ps_v[:, 0:DIM], parts(lambda c: xt_hl[:, j % 2, c, k, :]),
                                    parts(lambda c: wqkv_hl[:, c, k, 2 * DIM:3 * DIM]), k == 0, False)
                        nc.tensor.matmul(ps_v[:, 0:DIM], ones3[:, :], bias3[:, 2 * DIM:3 * DIM], start=False, stop=True).then_inc(v_ready, 1)
                    if unit_done(s, j):
                        pe.wait_ge(out0_copied, (u - 1) * UNIT + UNIT)
                        pe.wait_ge(out1_copied, (u - 1) * UNIT + UNIT)
                        project(u, 0)
                    if live(s, 2):
                        pe.wait_ge(p_ready, s - 1)
                        after(pe, pt_copied, s - 2)
                        for c in range(4):
                            t = nc.tensor.transpose(ps_pt[:, c * P:(c + 1) * P], probs[:, 2 * c:2 * c + 2, :], ident)
                        t.then_inc(pt_ready, 1)
                    if live(s, 1):
                        pe.wait_ge(qt_copied, s)
                        pe.wait_ge(kblk_done, s)
                        after(pe, sub_done, s - 1)
                        for w in range(2):
                            for c in range(KC):
                                t = nc.tensor.matmul(ps_sc[w * WTOK:(w + 1) * WTOK, :].rearrange("p (t c n) -> p t c n", t=4, c=KC)[:, :, c, :],
                                                     q_t[:, c, w * WTOK:(w + 1) * WTOK],
                                                     k_blk[:, c, w, :, :], start=True, stop=True)
                        t.then_inc(sc_ready, 1)
                    if unit_done(s, j):
                        project(u, 1)
                    if live(s, 2):
                        pe.wait_ge(pt_copied, s - 1)
                        pe.wait_ge(v_copied, s - 1)
                        after(pe, out0_copied, s - 2)
                        after(pe, out1_copied, s - 2)
                        for c, dst in enumerate((ps_av0, ps_av1)):
                            for w in range(2):
                                t = nc.tensor.matmul(dst[:, w * 256:(w + 1) * 256],
                                                     v_half[c * WTOK:(c + 1) * WTOK, (j - 2) % UNIT, w, :],
                                                     p_t[c * WTOK:(c + 1) * WTOK, :, w, :], start=True, stop=True)
                        t.then_inc(av_ready, 1)
                steps(pe, step)

            @block.vector
            def _(dve):
                dve.wait_ge(w_high, 1)
                nc.vector.tensor_tensor(wqkv_hl[:, LO], wqkv[:, :, :], high(wqkv_hl[:, HI]), ALU.subtract).then_inc(w_split, 1)

                def step(s, j, u):
                    if live(s, 1):
                        dve.wait_ge(tq_ready, s)
                        dve.wait_ge(qt_copied, s)
                        after(dve, sc_ready, s - 1)
                        for c in range(KC):
                            kt = ps_tq[:, (2 + c) * P:(3 + c) * P].rearrange("p (w n) -> p w n", w=2)
                            mask = const[:, C_HEAD:C_HEAD + 4]
                            t = nc.vector.tensor_tensor(k_blk[:, c, :, :, :], kt.unsqueeze(2).to_broadcast([P, 2, 4, WTOK]),
                                                        mask.unsqueeze(1).unsqueeze(3).to_broadcast([P, 2, 4, WTOK]), ALU.mult)
                        t.then_inc(kblk_done, 1)
                    if live(s, 0):
                        dve.wait_ge(qk_ready, s + 1)
                        after(dve, rope_added, s)
                        z = ps_qk[:, :].rearrange("p (a n) -> p a n", n=HD)
                        nc.vector.tensor_tensor(rope_c.rearrange("p (a n) -> p a n", n=HD), z,
                                                cos.unsqueeze(1).to_broadcast([P, 2 * HEADS, HD]), ALU.mult)
                        rs = rope_s.rearrange("p (a n) -> p a n", n=HD)
                        for e in range(2):
                            t = nc.vector.tensor_tensor(rs[:, :, e::2], z[:, :, 1 - e::2],
                                                        sin[:, e::2].unsqueeze(1).to_broadcast([P, 2 * HEADS, HD // 2]), ALU.mult)
                        t.then_inc(rope_done, 1)
                    if live(s, 1):
                        dve.wait_ge(sc_ready, s)
                        sc = ps_sc[:, :].rearrange("p (h n) -> p h n", h=HEADS)
                        nc.vector.tensor_reduce(smax[:, :], sc, AX_X, ALU.max).then_inc(max_done, 1)
                        dve.wait_ge(max_done, s)
                        after(dve, pt_ready, s - 1)
                        nc.vector.tensor_tensor(probs[:, :, :], sc, smax[:, :].unsqueeze(2).to_broadcast([P, HEADS, WTOK]),
                                                ALU.subtract).then_inc(sub_done, 1)
                    if live(s, 2):
                        dve.wait_ge(av_ready, s - 1)
                        for q in range(4):
                            t = nc.vector.tensor_copy(
                                o_rows(q, 0, (j - 2) % UNIT),
                                o_head(ps_av0, q))
                        t.then_inc(out0_copied, 1)
                    if live(s, 1):
                        dve.wait_ge(exp_done, s)
                        nc.vector.tensor_reduce(ssum[:, :], probs[:, :, :], AX_X, ALU.add).then_inc(sum_done, 1)
                        dve.wait_ge(sum_done, s)
                        after(dve, p_ready, s - 1)
                        nc.vector.reciprocal(sinv[:, :], ssum[:, :]).then_inc(inv_done, 1)
                    if j == 3 and (not isinstance(s, int) or s >= UNIT):
                        dve.wait_ge(h_copied, u * 2)
                        for i in range(UNIT):
                            nc.vector.bn_stats(raw[:, bass.ds(((u - 1) * UNIT + i) * 6, 6)],
                                               h[:, bass.ds(((u - 1) * UNIT + i) * DIM, DIM)])
                steps(dve, step)
                nc.vector.bn_stats(raw[:, CLS * 6:NT * 6], h[:, CLS * DIM:NT * DIM])

            @block.gpsimd
            def _(pool):
                def low_x(s, j, u):
                    pool.wait_ge(x_high, s + 1)
                    nc.gpsimd.tensor_tensor(xt_hl[:, j % 2, LO], xt[:, j], high(xt_hl[:, j % 2, HI]), ALU.subtract).then_inc(x_split, 1)

                def step(s, j, u):
                    next_x(s, j, u, low_x)
                    if live(s, 0):
                        pool.wait_ge(rope_done, s + 1)
                        after(pool, tq_ready, s)
                        nc.gpsimd.tensor_tensor(qk_rot, rope_c, rope_s, ALU.add).then_inc(rope_added, 1)
                    if live(s, 1):
                        pool.wait_ge(inv_done, s)
                        nc.gpsimd.tensor_tensor(probs[:, :, :], probs[:, :, :], sinv[:, :].unsqueeze(2).to_broadcast([P, HEADS, WTOK]),
                                                ALU.mult).then_inc(p_ready, 1)
                low_x(0, 0, 0)
                split_steps(pool, step)
                for i in range(len(enc_w)):
                    pool.wait_ge(enc_high, i + 1)
                    nc.gpsimd.tensor_tensor(enc_hl[i][:, LO], enc_w[i][:, :, :], high(enc_hl[i][:, HI]), ALU.subtract)

            @block.scalar
            def _(act):
                act.wait_ge(w_loaded, 32)
                nc.scalar.activation(wqkv_hl[:, HI], wqkv[:, :, :], ACT.Copy).then_inc(w_high, 1)

                def move_h(u, half):
                    act.wait_ge(proj_ready, (u - 1) * 2 + half + 1)
                    nc.scalar.activation(h[:, bass.ds(((u - 1) * 2 + half) * 2 * DIM, 2 * DIM)], ps_proj[:, :], ACT.Copy).then_inc(h_copied, 1)

                def high_x(s, j, u):
                    act.wait_ge(x_loaded[j], u * 16 + 16)
                    after(act, v_ready, s - 1)
                    nc.scalar.activation(xt_hl[:, j % 2, HI], xt[:, j], ACT.Copy).then_inc(x_high, 1)

                def step(s, j, u):
                    next_x(s, j, u, high_x)
                    if live(s, 1):
                        act.wait_ge(tq_ready, s)
                        after(act, sc_ready, s - 1)
                        nc.scalar.activation(q_t[:, :, :], ps_tq[:, 0:2 * P].rearrange("p (k n) -> p k n", k=KC), ACT.Copy).then_inc(qt_copied, 1)
                    if live(s, 0):
                        act.wait_ge(v_ready, s + 1)
                        after(act, av_ready, s - 3)
                        for c in range(KC):
                            for w in range(2):
                                t = nc.scalar.activation(v_half[c * WTOK:(c + 1) * WTOK, j, w, :],
                                                         ps_v[w * WTOK:(w + 1) * WTOK, c * P:(c + 1) * P], ACT.Copy)
                        t.then_inc(v_copied, 1)
                    if unit_done(s, j):
                        move_h(u, 0)
                    if live(s, 2):
                        act.wait_ge(pt_ready, s - 1)
                        after(act, av_ready, s - 2)
                        nc.scalar.activation(p_t[:, :, :, :], ps_pt[:, :].rearrange("p (c w n) -> p c w n", c=4, w=2), ACT.Copy).then_inc(pt_copied, 1)
                    if live(s, 1):
                        act.wait_ge(sub_done, s)
                        nc.scalar.activation(probs[:, :, :], probs[:, :, :], ACT.Exp, scale=SCALE).then_inc(exp_done, 1)
                    if unit_done(s, j):
                        move_h(u, 1)
                    if live(s, 2):
                        act.wait_ge(av_ready, s - 1)
                        for q in range(4):
                            t = nc.scalar.activation(
                                o_rows(q, 1, (j - 2) % UNIT),
                                o_head(ps_av1, q), ACT.Copy)
                        t.then_inc(out1_copied, 1)
                    if isinstance(s, int) and s == UNIT - 1:
                        act.wait_ge(enc_loaded, len(enc_w) * 16)
                        for part, w in zip(enc_hl, enc_w):
                            nc.scalar.activation(part[:, HI], w, ACT.Copy).then_inc(enc_high, 1)
                high_x(0, 0, 0)
                split_steps(act, step)


NHID = 7
PLANES, SETS = 16, 4
JOINT = PLANES // SETS
NPH = 2 * (JOINT + PLANES) + PLANES
COL_K, COL_Q, COL_L, COL_G = 0, JOINT + PLANES, 2 * (JOINT + PLANES), NPH
NCOL = NPH + 1
KF = 2 * (JOINT + PLANES)
PF = 2 * PLANES
LT = P - PF
MAGIC = 1.5 * 2.0 ** 23
PI = float(np.float32(np.pi))


def normaliser(nc, g, block_name):
    with ExitStack() as ctx:
        sb = lambda name, shape, dt=F32: ctx.enter_context(nc.sbuf_tensor(name + block_name, shape, dt))
        sem = lambda name: ctx.enter_context(nc.semaphore(name + block_name))
        raw, mean, rstd = g["raw"], g["mean"], g["rstd"]
        view = raw[:, :].rearrange("p (t f) -> p t f", f=6)
        dif, var = sb("dif", [P, NT]), sb("var", [P, NT])
        step_done, var_ready, std_ready = sem("ln_step_done"), sem("var_ready"), sem("std_ready")
        with nc.Block() as block:
            @block.vector
            def _(dve):
                nc.vector.tensor_tensor(mean[:, :], view[:, :, 1], view[:, :, 4], ALU.add)
                nc.vector.tensor_tensor(dif[:, :], view[:, :, 1], view[:, :, 4], ALU.subtract)
                nc.vector.tensor_tensor(var[:, :], view[:, :, 2], view[:, :, 5], ALU.add).then_inc(step_done, 1)
                dve.wait_ge(step_done, 1)
                nc.vector.tensor_scalar(mean[:, :], mean[:, :], 0.5, None, ALU.mult)
                nc.vector.tensor_tensor(dif[:, :], dif[:, :], dif[:, :], ALU.mult)
                nc.vector.tensor_scalar(var[:, :], var[:, :], 1.0 / DIM, EPS, ALU.mult, ALU.add).then_inc(step_done, 1)
                dve.wait_ge(step_done, 2)
                nc.vector.scalar_tensor_tensor(out=var[:, :], in0=dif[:, :], scalar=0.25, in1=var[:, :],
                                               op0=ALU.mult, op1=ALU.add).then_inc(var_ready, 1)
                dve.wait_ge(std_ready, 1)
                nc.vector.reciprocal(rstd[:, :], var[:, :])

            @block.scalar
            def _(act):
                act.wait_ge(var_ready, 1)
                nc.scalar.activation(var[:, :], var[:, :], ACT.Sqrt).then_inc(std_ready, 1)


def encoders(nc, g, a):
    with ExitStack() as ctx:
        sb = lambda name, shape, dt=F32: ctx.enter_context(nc.sbuf_tensor(name, shape, dt))
        sem = lambda name: ctx.enter_context(nc.semaphore(name))
        EU, RING, BUF = 2, 4, 3
        SPLIT = NHID - 1
        UNITS, ETOK = NPAIR // EU, EU * P
        w1, wv, w2 = g["enc_w1"], g["enc_wv"], g["enc_w2"]
        b1 = sb("enc_b1", [P, NHID])
        b2 = sb("enc_b2", [NCOL, 2])
        xn = sb("xn", [P, EU, DIM])
        xn_t = sb("xn_t", [P, 2, KC, ETOK], F32R)
        hid = sb("hid", [P, BUF, ETOK])
        hid_hl = sb("hid_hl", [P, 2, SPLIT, ETOK], F32R)
        ph_t = sb("ph_t", [P, ETOK])
        b_loaded, b2_ready = sem("enc_b_loaded"), sem("b2_ready")
        xn_ready, xt_ready, xt_high, xt_split = sem("xn_ready"), sem("xt_ready"), sem("xt_high"), sem("xt_split")
        hid_ready, gelu_done, hid_high, hid_split = sem("hid_ready"), sem("gelu_done"), sem("hid_high"), sem("hid_split")
        v_ready, v_copied = sem("ev_ready"), sem("ev_copied")
        l2_begun = sem("l2_begun")
        l2_ready, tanh_done, pht_ready, ph_copied = sem("l2_ready"), sem("tanh_done"), sem("pht_ready"), sem("ph_copied")
        ps_t, ps_v, ps_l2, ps_ph = g["bank"][0:4]
        ring = g["bank"][4:8]
        h, V, th, mean, rstd, ident = g["h"], g["V"], g["th"], g["mean"], g["rstd"], g["const"][:, C_ID:C_ID + P]
        ones3, bias3 = g["ones3"], g["bias3"]
        is_cls = lambda u: isinstance(u, int) and u == UNITS
        first = lambda u: isinstance(u, int) and u == 0
        tiles = lambda u: 1 if is_cls(u) else EU

        def tokens(u, ap):
            return ap[:, :].rearrange("p (k n) -> p k n", k=KC)[:, :, 0:tiles(u) * P]

        def order(eng, unit):
            unit(0)
            with eng.Fori(1, UNITS - 1) as u:
                unit(u)
            unit(UNITS - 1)
            unit(UNITS)

        with nc.Block() as block:
            @block.sync
            def _(sp):
                for dst, src in ((b1[:, :], a["enc_b1"]), (b2[:, :], a["enc_b2"])):
                    sp.dma_start(dst, src).then_inc(b_loaded, 16)

            @block.vector
            def _(dve):
                nc.vector.memset(ph_t[:, :], 0.0).then_inc(b2_ready, 1)

                def normalise(u):
                    after(dve, xt_ready, u)
                    for i in range(tiles(u)):
                        t = u * EU + i
                        n = nc.vector.tensor_scalar(xn[:, i, :], h[:, bass.ds(t * DIM, DIM)], mean[:, bass.ds(t, 1)],
                                                    rstd[:, bass.ds(t, 1)], ALU.subtract, ALU.mult)
                    n.then_inc(xn_ready, 1)

                def low_xt(u):
                    dve.wait_ge(xt_high, u + 1)
                    n = tiles(u) * P
                    nc.vector.tensor_tensor(xn_t[:, LO, :, 0:n], tokens(u, ps_t), high(xn_t[:, HI, :, 0:n]), ALU.subtract).then_inc(xt_split, 1)

                def low_hid(u, chunks):
                    n = tiles(u) * P
                    for c in chunks:
                        dve.wait_ge(hid_high, u * NHID + c + 1)
                        nc.vector.tensor_tensor(hid_hl[:, LO, c % SPLIT, 0:n], hid[:, c % BUF, 0:n], high(hid_hl[:, HI, c % SPLIT, 0:n]),
                                                ALU.subtract).then_inc(hid_split, 1)

                def move_phases(u):
                    dve.wait_ge(pht_ready, u + 1)
                    m = tiles(u)
                    nc.vector.tensor_copy(th[:, bass.ds(u * EU * NCOL, m * NCOL)].rearrange("p (i n) -> p i n", n=NCOL),
                                          ps_ph[:, 0:m * P].rearrange("p (i n) -> p i n", n=P)[:, :, 0:NCOL]).then_inc(ph_copied, 1)

                def unit(u):
                    if first(u):
                        normalise(u)
                        dve.wait_ge(b_loaded, 2 * 16)
                        nc.vector.tensor_scalar(b2[:, 0:1], b2[:, 0:1], b2[:, 1:2], None, ALU.mult).then_inc(b2_ready, 1)
                        low_xt(u)
                    low_hid(u, range(NHID // 2))
                    if not is_cls(u):
                        normalise(u + 1)
                    low_hid(u, range(NHID // 2, NHID))
                    if not is_cls(u):
                        low_xt(u + 1)
                    if not first(u):
                        move_phases(u - 1)
                    dve.wait_ge(v_ready, u + 1)
                    n = tiles(u) * DIM
                    nc.vector.tensor_copy(V[:, bass.ds(u * EU * DIM, n)], ps_v[:, 0:n]).then_inc(v_copied, 1)
                order(dve, unit)
                move_phases(UNITS)

            @block.scalar
            def _(act):
                def high_xt(u):
                    act.wait_ge(xt_ready, u + 1)
                    after(act, v_ready, u)
                    n = tiles(u) * P
                    nc.scalar.activation(xn_t[:, HI, :, 0:n], tokens(u, ps_t), ACT.Copy).then_inc(xt_high, 1)

                def high_hid(u, c):
                    n = tiles(u) * P
                    act.wait_ge(gelu_done, u * NHID + c + 1)
                    if c == SPLIT:
                        act.wait_ge(l2_begun, u + 1)
                    nc.scalar.activation(hid_hl[:, HI, c % SPLIT, 0:n], hid[:, c % BUF, 0:n], ACT.Copy).then_inc(hid_high, 1)

                def tanh(u):
                    n = tiles(u) * P
                    act.wait_ge(l2_ready, u + 1)
                    after(act, pht_ready, u)
                    nc.scalar.activation(ph_t[0:NCOL, 0:n], ps_l2[0:NCOL, 0:n], ACT.Tanh, bias=b2[:, 0:1], scale=b2[:, 1:2]).then_inc(tanh_done, 1)

                def unit(u):
                    n = tiles(u) * P
                    for c in range(NHID):
                        act.wait_ge(hid_ready, u * NHID + c + 1)
                        if c >= BUF:
                            act.wait_ge(hid_split, u * NHID + c + 1 - BUF)
                        elif c == 0:
                            after(act, hid_split, u * NHID)
                        nc.scalar.activation(hid[:, c % BUF, 0:n], ring[c % RING][:, 0:n], ACT.Gelu, bias=b1[:, c:c + 1]).then_inc(gelu_done, 1)
                        if c == 0 and not first(u):
                            tanh(u - 1)
                        if c:
                            high_hid(u, c - 1)
                    high_hid(u, NHID - 1)
                    if not is_cls(u):
                        high_xt(u + 1)
                act.wait_ge(b_loaded, 2 * 16)
                act.wait_ge(b2_ready, 2)
                high_xt(0)
                order(act, unit)
                tanh(UNITS)

            @block.tensor
            def _(pe):
                def turn(u):
                    pe.wait_ge(xn_ready, u + 1)
                    after(pe, xt_split, u)
                    for k in range(KC):
                        for i in range(tiles(u)):
                            t = nc.tensor.transpose(ps_t[:, (k * EU + i) * P:(k * EU + i + 1) * P], xn[:, i, k * P:(k + 1) * P], ident)
                    t.then_inc(xt_ready, 1)

                def turn_phases(u):
                    pe.wait_ge(tanh_done, u + 1)
                    after(pe, ph_copied, u)
                    for i in range(tiles(u)):
                        t = nc.tensor.transpose(ps_ph[:, i * P:(i + 1) * P], ph_t[:, i * P:(i + 1) * P], ident)
                    t.then_inc(pht_ready, 1)

                def unit(u):
                    n = tiles(u) * P
                    pe.wait_ge(xt_split, u + 1)

                    def second(c):
                        pe.wait_ge(hid_split, u * NHID + c + 1)
                        return product(nc, ps_l2[0:NCOL, 0:n], parts(lambda e: w2[:, e, c, :]), parts(lambda e: hid_hl[:, e, c % SPLIT, 0:n]),
                                       c == 0, c == NHID - 1)
                    for c in range(NHID):
                        if c == SPLIT:
                            after(pe, tanh_done, u)
                            second(0).then_inc(l2_begun, 1)
                        if c >= RING:
                            pe.wait_ge(gelu_done, u * NHID + c + 1 - RING)
                        for k in range(KC):
                            t = product(nc, ring[c % RING][:, 0:n], parts(lambda e: w1[:, e, k, c * P:(c + 1) * P]),
                                        parts(lambda e: xn_t[:, e, k, 0:n]), k == 0, k == KC - 1)
                        t.then_inc(hid_ready, 1)
                    if not is_cls(u):
                        turn(u + 1)
                    if not first(u):
                        turn_phases(u - 1)
                    after(pe, v_copied, u)
                    for i in range(tiles(u)):
                        v = ps_v[:, i * DIM:(i + 1) * DIM]
                        for k in range(KC):
                            product(nc, v, parts(lambda e: xn_t[:, e, k, i * P:(i + 1) * P]), parts(lambda e: wv[:, e, k, :]), k == 0, False)
                        t = nc.tensor.matmul(v, ones3[:, :], bias3[:, 4 * DIM:5 * DIM], start=False, stop=True)
                    t.then_inc(v_ready, 1)
                    for c in range(1, NHID):
                        t = second(c)
                    t.then_inc(l2_ready, 1)
                turn(0)
                order(pe, unit)
                turn_phases(UNITS)


PI_IN = 3.1415925
TWO_PI = float(np.float32(2 * np.pi))
TP1 = 6.28125
TP2 = 253 / 2.0 ** 17
TP3 = float(np.float32(2 * np.pi - TP1 - TP2))
(S_SETW, S_POSW, S_SSCALE, S_SBIAS, S_RSCALE, S_RTHR, S_LTMW, S_COUNT, S_FREQ, NSCAL) = (0, 4, 5, 6, 7, 8, 9, 10, 11, 27)
NBIAS = 7 * DIM


def prologue(nc, g, a):
    with ExitStack() as ctx:
        sb = lambda name, shape, dt=F32: ctx.enter_context(nc.sbuf_tensor(name, shape, dt))
        sem = lambda name: ctx.enter_context(nc.semaphore(name))
        row = sb("bias_row", [1, NBIAS])
        parts = sb("bias_parts", [1, 3, NBIAS], BF16)
        t = sb("pro_t", [P, 16])
        ph, turns = sb("pos_phase", [P, TPB * PLANES]), sb("pos_turns", [P, TPB * PLANES])
        posn = sb("pos_n", [P, TPB])
        zero = sb("pro_zero", [P, 1])
        lnb, lng = sb("lnb", [P, KC]), sb("lng", [P, KC])
        ltm = sb("ltm_rows", [P, DIM])
        loaded, bias_sent, step_done, act_done = sem("pro_loaded"), sem("bias_sent"), sem("pro_step_done"), sem("pro_act_done")
        shift_ready, wout_loaded, ltm_loaded = sem("shift_ready"), sem("wout_loaded"), sem("ltm_loaded")
        const, scal, sc, wout, st, post, rpos = g["const"], g["scal"], g["sc"], g["wout"], g["st"], g["post"], g["rpos"]
        bias_ready, arguments_ready = sem("bias_ready"), sem("arguments_ready")
        ps = g["bank"][0]
        with nc.Block() as block:
            @block.sync
            def _(sp):
                sp.dma_start(const[:, :], a["const"]).then_inc(loaded, 16)
                sp.dma_start(row[:, :], a["bias"]).then_inc(loaded, 16)
                sp.dma_start(scal[:, :], a["scal"].to_broadcast([P, NSCAL])).then_inc(loaded, 16)
                sp.dma_start(g["h"][:, CLS * DIM:NT * DIM], a["cls"].to_broadcast([P, DIM])).then_inc(loaded, 16)
                sp.dma_start(wout[:, :, :], a["out_w"].rearrange("(k p) n -> p k n", p=P)).then_inc(wout_loaded, 16)
                sp.dma_start(lng[:, :], a["ln_g"]).then_inc(wout_loaded, 16)
                sp.dma_start(lnb[:, :], a["ln_b"]).then_inc(wout_loaded, 16)
                sp.dma_start(ltm[LT:P, :], a["ltm"]).then_inc(ltm_loaded, 16)
                sp.wait_ge(bias_ready, 1)
                sp.dma_start(g["bias3"][:, :], parts[:, :, :]).then_inc(bias_sent, 16)
                sp.wait_ge(bias_sent, 16)

            @block.tensor
            def _(pe):
                pe.wait_ge(wout_loaded, 48)
                pe.wait_ge(loaded, 64)
                for k in range(KC):
                    m = nc.tensor.matmul(ps[0:1, 0:DIM], lnb[:, k:k + 1], wout[:, k, :], start=(k == 0), stop=(k == KC - 1))
                m.then_inc(shift_ready, 1)

            @block.vector
            def _(dve):
                count = [0]

                def done(ins):
                    count[0] += 1
                    ins.then_inc(step_done, 1)
                    dve.wait_ge(step_done, count[0])

                V = nc.vector
                V.memset(g["ones3"][:, :], 1.0)
                V.memset(g["half_pi"][:, :], float(np.float32(np.pi / 2)))
                V.memset(g["eps"][:, :], EPS)
                V.memset(st[:, :, :], 0.0)
                dve.wait_ge(loaded, 64)
                dve.wait_ge(shift_ready, 1)
                done(V.tensor_tensor(row[:, 5 * DIM:6 * DIM], row[:, 5 * DIM:6 * DIM], ps[0:1, 0:DIM], ALU.add))
                for k in range(KC):
                    V.tensor_scalar(wout[:, k, :], wout[:, k, :], lng[:, k:k + 1], None, ALU.mult)
                for i in range(3):
                    done(V.tensor_copy(parts[:, i, :], row[:, :]))
                    if i < 2:
                        done(V.tensor_tensor(row[:, :], row[:, :], parts[:, i, :], ALU.subtract))
                V.memset(zero[:, :], 0.0).then_inc(bias_ready, 1)
                p3 = ph[:, :].rearrange("p (t f) -> p t f", f=PLANES)
                done(V.tensor_tensor(p3, const[:, C_POS:C_POS + TPB].unsqueeze(2).to_broadcast([P, TPB, PLANES]),
                                     scal[:, S_FREQ:S_FREQ + PLANES].unsqueeze(1).to_broadcast([P, TPB, PLANES]), ALU.mult))
                done(V.tensor_scalar(ph[:, :], ph[:, :], TWO_PI, None, ALU.mult))
                done(V.tensor_scalar(turns[:, :], ph[:, :], float(np.float32(1 / (2 * np.pi))), MAGIC, ALU.mult, ALU.add))
                done(V.tensor_scalar(turns[:, :], turns[:, :], MAGIC, None, ALU.subtract))
                for part in (TP1, TP2, TP3):
                    done(V.scalar_tensor_tensor(out=ph[:, :], in0=turns[:, :], scalar=-part, in1=ph[:, :], op0=ALU.mult, op1=ALU.add))
                done(V.tensor_scalar(ph[:, :], ph[:, :], PI_IN, -PI_IN, ALU.min, ALU.max))
                done(V.scalar_tensor_tensor(out=turns[:, :], in0=ph[:, :], scalar=-1.0, in1=ph[:, :], op0=ALU.mult, op1=ALU.max))
                done(V.tensor_reduce(t[:, 0:1], scal[:, S_SETW:S_SETW + SETS], AX_X, ALU.max))
                done(V.tensor_scalar(sc["setw"], scal[:, S_SETW:S_SETW + SETS], t[:, 0:1], None, ALU.subtract))
                V.tensor_scalar(sc["posw"], scal[:, S_POSW:S_POSW + 1], 0.5, None, ALU.mult)
                V.tensor_scalar(sc["rscale"], scal[:, S_RSCALE:S_RSCALE + 1], 1.0, 20.0, ALU.max, ALU.min)
                V.tensor_scalar(sc["rthr"], scal[:, S_RTHR:S_RTHR + 1], 0.1, 0.9, ALU.max, ALU.min)
                V.tensor_scalar(sc["count"], scal[:, S_COUNT:S_COUNT + 1], 1.0, float(PLANES), ALU.max, ALU.mult)
                V.tensor_scalar(posn[:, :], const[:, C_POS:C_POS + TPB], 1.0, None, ALU.max)
                done(V.tensor_scalar(sc["ltmw"], scal[:, S_LTMW:S_LTMW + 1], 0.5, None, ALU.mult))
                done(V.tensor_tensor(sc["nthr"], sc["rscale"], sc["rthr"], ALU.mult))
                V.tensor_scalar(sc["nthr"], sc["nthr"], -1.0, None, ALU.mult).then_inc(arguments_ready, 1)
                dve.wait_ge(act_done, 7)
                done(V.reciprocal(t[:, 1:2], t[:, 1:2]))
                V.tensor_scalar(sc["setw"], sc["setw"], t[:, 1:2], None, ALU.mult)
                V.tensor_scalar(sc["posw"], sc["posw"], 0.5, 0.5, ALU.mult, ALU.add)
                V.tensor_scalar(sc["ltmw"], sc["ltmw"], 0.5, 0.5, ALU.mult, ALU.add)
                V.reciprocal(rpos[:, :], posn[:, :])
                done(V.reciprocal(sc["count"], sc["count"]))
                done(V.tensor_tensor(t[:, 2:3], sc["ltmw"], sc["count"], ALU.mult))
                dve.wait_ge(ltm_loaded, 16)
                for i in range(2):
                    V.tensor_scalar(st[LT:P, i, :], ltm[LT:P, :], t[LT:P, 2:3], None, ALU.mult)
                V.memset(sc["wtab"], 1.0).then_inc(step_done, 1)
                count[0] += 1
                dve.wait_ge(step_done, count[0])
                V.tensor_copy(sc["wtab"][:, JOINT:].rearrange("p (s j) -> p s j", s=SETS),
                              sc["setw"].unsqueeze(2).to_broadcast([P, SETS, JOINT]))
                V.memset(post[:, TPB, 0, :], 1.0)
                V.memset(post[:, TPB, 1, :], 0.0)
            @block.scalar
            def _(act):
                act.wait_ge(arguments_ready, 1)
                p3 = ph[:, :].rearrange("p (t f) -> p t f", f=PLANES)
                n3 = turns[:, :].rearrange("p (t f) -> p t f", f=PLANES)
                nc.scalar.activation(sc["setw"], sc["setw"], ACT.Exp, accum_out=t[:, 1:2]).then_inc(act_done, 1)
                nc.scalar.activation(sc["posw"], sc["posw"], ACT.Tanh).then_inc(act_done, 1)
                nc.scalar.activation(sc["ltmw"], sc["ltmw"], ACT.Tanh).then_inc(act_done, 1)
                nc.scalar.activation(post[:, 0:TPB, 1, :], p3, ACT.Sin).then_inc(act_done, 1)
                nc.scalar.activation(post[:, 0:TPB, 0, :], n3, ACT.Sin, bias=g["half_pi"][:, :], scale=-1.0).then_inc(act_done, 1)
                nc.scalar.activation(posn[:, :], posn[:, :], ACT.Sqrt).then_inc(act_done, 1)
                nc.scalar.activation(sc["count"], sc["count"], ACT.Sqrt).then_inc(act_done, 1)


def phasors(nc, g):
    with ExitStack() as ctx:
        sb = lambda name, shape, dt=F32: ctx.enter_context(nc.sbuf_tensor(name, shape, dt))
        sem = lambda name: ctx.enter_context(nc.semaphore(name))
        th, trig, wg, gg, sc, const, rpos = g["th"], g["trig"], g["wg"], g["gg"], g["sc"], g["const"], g["rpos"]
        t3 = th[:, :].rearrange("p (t n) -> p t n", n=NCOL)
        NJ = B * 2 * JOINT * TPB
        turn = sb("turn", [P, NT, 2, JOINT])
        part = [sb(f"part{i}", [P, NT, 2, JOINT]) for i in range(2)]
        tot, km = sb("tot", [P, NJ]), sb("km", [P, NJ])
        pr = [x[:, :, :, :].rearrange("p t q j -> p (t q j)")[:, i * NJ // 2:(i + 1) * NJ // 2]
              .rearrange("p (b f t) -> p b f t", b=B, f=JOINT) for x in (turn, part[1]) for i in range(2)]
        mag = sb("mag", [P, NT])
        joint_ready, sin_done, abs_done, trig_ready = sem("joint_ready"), sem("sin_done"), sem("abs_done"), sem("trig_ready")
        step_done, sums_ready, square_ready, root_ready = sem("ph_step_done"), sem("sums_ready"), sem("square_ready"), sem("root_ready")
        arg_ready, surprise_ready, arg2_ready, gate_ready = sem("arg_ready"), sem("surprise_ready"), sem("arg2_ready"), sem("gate_ready")
        ps_pre, ps_tot = g["bank"][0:2]
        with nc.Block() as block:
            @block.vector
            def _(dve):
                count = [0]
                V = nc.vector

                def done(ins):
                    count[0] += 1
                    ins.then_inc(step_done, 1)
                    dve.wait_ge(step_done, count[0])

                V.memset(g["kq"][:, :, :, :], 0.0)
                def sets(c, s):
                    return t3[:, :, c + JOINT + s * JOINT:c + JOINT + (s + 1) * JOINT]
                for q, c in enumerate((COL_K, COL_Q)):
                    V.tensor_tensor(part[0][:, :, q, :], sets(c, 0), sets(c, 1), ALU.add)
                    V.tensor_tensor(part[1][:, :, q, :], sets(c, 2), sets(c, 3), ALU.add)
                done(V.memset(mag[:, CLS:NT], 0.0))
                done(V.tensor_tensor(part[0][:, :, :, :], part[0][:, :, :, :], part[1][:, :, :, :], ALU.add))
                done(V.tensor_scalar(turn[:, :, :, :], part[0][:, :, :, :], 0.5, MAGIC, ALU.mult, ALU.add))
                done(V.tensor_scalar(turn[:, :, :, :], turn[:, :, :, :], MAGIC, None, ALU.subtract))
                for q, c in enumerate((COL_K, COL_Q)):
                    n = V.scalar_tensor_tensor(out=t3[:, :, c:c + JOINT], in0=turn[:, :, q, :], scalar=-2.0,
                                               in1=part[0][:, :, q, :], op0=ALU.mult, op1=ALU.add)
                n.then_inc(joint_ready, 1)
                V.tensor_scalar(gg[:, 0, :], t3[:, :, COL_G], 0.1, 0.1, ALU.mult, ALU.add)
                done(V.tensor_scalar(gg[:, 1, :], t3[:, :, COL_G], -0.5, 0.5, ALU.mult, ALU.add))
                V.tensor_scalar(gg[:, 1, :], gg[:, 1, :], sc["posw"], None, ALU.mult)
                dve.wait_ge(sin_done, 1)
                dve.wait_ge(joint_ready, 1)
                V.scalar_tensor_tensor(out=t3[:, :, 0:NPH], in0=t3[:, :, 0:NPH], scalar=-1.0, in1=t3[:, :, 0:NPH],
                                       op0=ALU.mult, op1=ALU.max).then_inc(abs_done, 1)
                dve.wait_ge(sums_ready, 1)
                half = 2 * JOINT * TPB
                for b in range(B):
                    n = V.tensor_tensor_scan(tot[:, b * half:(b + 1) * half], const[:, C_SEG:C_SEG + half],
                                             ps_tot[:, b * half:(b + 1) * half], 0.0, ALU.mult, ALU.add)
                done(n)
                done(V.tensor_tensor(tot[:, :], tot[:, :], ps_tot[:, :], ALU.subtract))
                done(V.tensor_tensor(km[:, :], tot[:, :], ps_pre[:, :], ALU.add))
                k5 = km[:, :].rearrange("p (b c f t) -> p b c f t", b=B, c=2, f=JOINT)
                for b in range(B):
                    n = V.tensor_tensor(k5[:, b].rearrange("p c f t -> p (c f) t"), k5[:, b].rearrange("p c f t -> p (c f) t"),
                                        g["jcls"][:, :].unsqueeze(2).to_broadcast([P, 2 * JOINT, TPB]), ALU.add)
                done(n)
                jq = [trig[:, 0:NPAIR, c, COL_Q:COL_Q + JOINT].rearrange("p (b t) f -> p b f t", b=B) for c in range(2)]
                V.tensor_tensor(pr[0][:, :, :, :], k5[:, :, 0], jq[0], ALU.mult)
                V.tensor_tensor(pr[1][:, :, :, :], k5[:, :, 1], jq[1], ALU.mult)
                V.tensor_tensor(pr[2][:, :, :, :], k5[:, :, 1], jq[0], ALU.mult)
                done(V.tensor_tensor(pr[3][:, :, :, :], k5[:, :, 0], jq[1], ALU.mult))
                V.tensor_tensor(pr[0][:, :, :, :], pr[0][:, :, :, :], pr[1][:, :, :, :], ALU.add)
                done(V.tensor_tensor(pr[2][:, :, :, :], pr[2][:, :, :, :], pr[3][:, :, :, :], ALU.subtract))
                V.tensor_tensor(pr[0][:, :, :, :], pr[0][:, :, :, :], pr[0][:, :, :, :], ALU.mult)
                done(V.tensor_tensor(pr[2][:, :, :, :], pr[2][:, :, :, :], pr[2][:, :, :, :], ALU.mult))
                V.tensor_tensor(pr[0][:, :, :, :], pr[0][:, :, :, :], pr[2][:, :, :, :], ALU.add).then_inc(square_ready, 1)
                dve.wait_ge(root_ready, 1)
                done(V.tensor_reduce(mag[:, 0:NPAIR].rearrange("p (b t) -> p b t", b=B),
                                     pr[1][:, :, :, :].rearrange("p b f t -> p b t f"), AX_X, ALU.add))
                m3 = mag[:, 0:NPAIR].rearrange("p (b t) -> p b t", b=B)
                done(V.scalar_tensor_tensor(out=m3, in0=m3, scalar=1.0 / JOINT, in1=rpos[:, :].unsqueeze(1).to_broadcast([P, B, TPB]),
                                            op0=ALU.mult, op1=ALU.mult))
                V.tensor_scalar(mag[:, :], mag[:, :], sc["rscale"], sc["nthr"], ALU.mult, ALU.add).then_inc(arg_ready, 1)
                dve.wait_ge(surprise_ready, 1)
                done(V.tensor_scalar(mag[:, :], mag[:, :], -0.5, g["scal"][:, S_SSCALE:S_SSCALE + 1], ALU.mult, ALU.mult))
                V.tensor_scalar(mag[:, :], mag[:, :], g["scal"][:, S_SBIAS:S_SBIAS + 1], 0.5, ALU.add, ALU.mult).then_inc(arg2_ready, 1)
                dve.wait_ge(gate_ready, 1)
                V.tensor_scalar(wg[:, :], mag[:, :], 0.5, 0.5, ALU.mult, ALU.add)

            @block.scalar
            def _(act):
                act.wait_ge(joint_ready, 1)
                nc.scalar.activation(trig[:, :, 1, :], t3[:, :, 0:NPH], ACT.Sin, scale=PI_IN).then_inc(sin_done, 1)
                act.wait_ge(abs_done, 1)
                nc.scalar.activation(trig[:, :, 0, :], t3[:, :, 0:NPH], ACT.Sin, bias=g["half_pi"][:, :], scale=-PI).then_inc(trig_ready, 1)
                act.wait_ge(trig_ready, 1)
                nc.scalar.activation(g["jcls"][:, :].rearrange("p (c f) -> p c f", c=2), trig[:, CLS, :, 0:JOINT], ACT.Copy).then_inc(trig_ready, 1)
                act.wait_ge(square_ready, 1)
                nc.scalar.activation(pr[1][:, :, :, :], pr[0][:, :, :, :], ACT.Sqrt).then_inc(root_ready, 1)
                act.wait_ge(arg_ready, 1)
                nc.scalar.activation(mag[:, :], mag[:, :], ACT.Tanh).then_inc(surprise_ready, 1)
                act.wait_ge(arg2_ready, 1)
                nc.scalar.activation(mag[:, :], mag[:, :], ACT.Tanh).then_inc(gate_ready, 1)

            @block.tensor
            def _(pe):
                pe.wait_ge(trig_ready, 2)
                for b in range(B):
                    for c in range(2):
                        keys = trig[:, b * TPB:(b + 1) * TPB, c, COL_K:COL_K + JOINT].rearrange("p t f -> p f t")
                        at = (b * 2 + c) * JOINT * TPB
                        for dst, col in ((ps_pre, C_STRICT), (ps_tot, C_ONES)):
                            n = nc.tensor.matmul(dst[:, at:at + JOINT * TPB], const[:, col:col + P], keys, start=True, stop=True)
                n.then_inc(sums_ready, 1)


def retrieval(nc, g):
    with ExitStack() as ctx:
        sb = lambda name, shape, dt=F32: ctx.enter_context(nc.sbuf_tensor(name, shape, dt))
        sem = lambda name: ctx.enter_context(nc.semaphore(name))
        kq, st, post, trig, V, h, raw = g["kq"], g["st"], g["post"], g["trig"], g["V"], g["h"], g["raw"]
        wg, gg, sc, const, wout, ones3, bias3 = g["wg"], g["gg"], g["sc"], g["const"], g["wout"], g["ones3"], g["bias3"]
        ident = const[:, C_ID:C_ID + P]
        kq_t = sb("kq_t", [P, 2, 2, P])
        kcls, vcls = sb("kcls", [1, P]), sb("vcls", [1, DIM])
        masked = sb("masked", [P, 2, P])
        ln_raw, ln_agg, ln_std, ln_rstd = sb("ln_raw", [P, 2, 6]), sb("ln_agg", [P, 2, 2]), sb("ln_std", [P, 2]), sb("ln_rstd", [P, 2])
        y, y_t = sb("y", [P, 2, DIM]), sb("y_t", [P, 2, KC, P])
        kq_ready, kqt_ready, kqt_copied, query_scaled = sem("kq_ready"), sem("kqt_ready"), sem("kqt_copied"), sem("query_scaled")
        s_ready, masked_ready, o_ready, state_ready, state_copied = sem("s_ready"), sem("masked_ready"), sem("o_ready"), sem("state_ready"), sem("state_copied")
        raw_done, agg_done, std_done, rstd_done, y_ready = sem("raw_done"), sem("agg_done"), sem("std_done"), sem("rstd_done"), sem("y_ready")
        yt_ready, yt_copied, w_ready, h_done, cls_kept = sem("yt_ready"), sem("yt_copied"), sem("w_ready"), sem("h_done"), sem("cls_kept")
        ps_kq, ps_s, ps_o0, ps_o1, ps_state, ps_yt, ps_w = g["bank"][0:7]
        ps_o = (ps_o0, ps_o1)
        LAGS = 4
        STATES = TPB + 1

        def order(eng, step):
            for s in range(1 + LAGS):
                step(0, CLS, s, 1, None, s % 4)
            with eng.Fori(0, B) as b:
                for s in range(LAGS):
                    step(1 + b * TPB, b * TPB, s, TPB, b, s % 4)
                with eng.Fori(LAGS // 4, TPB // 4) as r:
                    for i in range(4):
                        step(1 + b * TPB, b * TPB, r * 4 + i, TPB, b, i)
                for s in range(TPB, TPB + LAGS):
                    step(1 + b * TPB, b * TPB, s, TPB, b, s % 4)

        def live(s, lag, n):
            return not isinstance(s, int) or 0 <= s - lag < n

        def two_before(no, t):
            return no if isinstance(t, int) and t == 0 else no - 1

        with nc.Block() as block:
            @block.gpsimd
            def _(pool):
                def wide(column):
                    return column.unsqueeze(2).to_broadcast([P, 2, KF // 2])

                def step(n0, t0, s, n, b, q):
                    if live(s, 0, n):
                        no, t = n0 + s, t0 + s
                        tile = trig[:, bass.ds(t, 1), :, :].rearrange("p a c f -> p (a c) f")
                        pos = post[:, bass.ds(TPB if b is None else s, 1), :, :].rearrange("p a c f -> p (a c f)")
                        if isinstance(s, int) and s == 0:
                            after(pool, o_ready, no)
                            if b is not None:
                                pool.wait_ge(cls_kept, 2)
                        elif not (isinstance(s, int) and s < 3):
                            pool.wait_ge(o_ready, no - 2)
                        fk = kq[:, q, 0, 0:KF].rearrange("p (c f) -> p c f", c=2)
                        fq = kq[:, q, 1, 0:KF].rearrange("p (c f) -> p c f", c=2)
                        nc.gpsimd.tensor_tensor(fq, tile[:, :, COL_Q:COL_Q + KF // 2], wide(gg[:, 0, bass.ds(t, 1)]), ALU.mult).then_inc(query_scaled, 1)
                        nc.gpsimd.tensor_tensor(fk, tile[:, :, COL_K:COL_K + KF // 2], wide(wg[:, bass.ds(t, 1)]), ALU.mult)
                        nc.gpsimd.tensor_copy(kq[:, q, 0, KF:KF + PF], pos)
                        nc.gpsimd.tensor_tensor(kq[:, q, 1, KF:KF + PF], pos, gg[:, 1, bass.ds(t, 1)].to_broadcast([P, PF]), ALU.mult)
                        nc.gpsimd.tensor_copy(kq[:, q, 1, LT:P].rearrange("p (c f) -> p c f", c=2), tile[:, :, COL_L:COL_L + PLANES])
                        pool.wait_ge(query_scaled, no + 1)
                        nc.gpsimd.tensor_tensor(fq, fq, sc["wtab"].unsqueeze(1).to_broadcast([P, 2, KF // 2]), ALU.mult).then_inc(kq_ready, 1)
                order(pool, step)

            @block.tensor
            def _(pe):
                def step(n0, t0, s, n, b, q):
                    m = q % 2
                    if live(s, 0, n):
                        no = n0 + s
                        pe.wait_ge(kq_ready, no + 1)
                        after(pe, kqt_copied, no)
                        nc.tensor.transpose(ps_kq[:, 0:P], kq[:, q, 0, :], ident)
                        nc.tensor.transpose(ps_kq[:, P:2 * P], kq[:, q, 1, :], ident).then_inc(kqt_ready, 1)
                    if b is not None and isinstance(s, int) and s == 2:
                        pe.wait_ge(cls_kept, 2)
                        pe.wait_ge(yt_copied, n0)
                        nc.tensor.matmul(ps_state[0:LT, 0:DIM], kcls[0:1, 0:LT], vcls[:, :], start=True, stop=False,
                                         skip_group_check=True).then_inc(state_ready, 1)
                    if live(s, 2, n):
                        no, t = n0 + s - 2, s - 2
                        v = V[:, bass.ds((t0 + t) * DIM, DIM)]
                        pe.wait_ge(masked_ready, no + 1)
                        after(pe, y_ready, two_before(no, t))
                        nc.tensor.matmul(ps_o[m][:, 0:DIM], masked[:, m, :], v, start=True, stop=False)
                        if b is not None:
                            pe.wait_ge(state_copied, b * STATES + t + 1)
                        nc.tensor.matmul(ps_o[m][:, 0:DIM], kq_t[:, m, 1, :], st[:, m if b is not None else 1, :],
                                         start=False, stop=True).then_inc(o_ready, 1)
                        if b is not None:
                            nc.tensor.matmul(ps_state[0:LT, 0:DIM], kq[:, (q - 2) % 4, 0, 0:LT], v, start=False, stop=False,
                                             skip_group_check=True).then_inc(state_ready, 1)
                    if live(s, 1, n):
                        no = n0 + s - 1
                        pe.wait_ge(kqt_copied, no + 1)
                        after(pe, masked_ready, no)
                        nc.tensor.matmul(ps_s[:, 0:P], kq_t[:, 1 - m, 0, :], kq_t[:, 1 - m, 1, :], start=True, stop=True).then_inc(s_ready, 1)
                    if live(s, 3, n):
                        no = n0 + s - 3
                        pe.wait_ge(y_ready, no + 1)
                        after(pe, yt_copied, no)
                        for k in range(KC):
                            x = nc.tensor.transpose(ps_yt[:, k * P:(k + 1) * P], y[:, 1 - m, k * P:(k + 1) * P], ident)
                        x.then_inc(yt_ready, 1)
                    if live(s, 4, n):
                        no = n0 + s - 4
                        pe.wait_ge(yt_copied, no + 1)
                        after(pe, h_done, no)
                        for k in range(KC):
                            nc.tensor.matmul(ps_w[:, 0:DIM], y_t[:, m, k, :], wout[:, k, :], start=(k == 0), stop=False)
                        nc.tensor.matmul(ps_w[:, 0:DIM], ones3[:, :], bias3[:, 5 * DIM:6 * DIM], start=False, stop=True).then_inc(w_ready, 1)
                order(pe, step)

            @block.scalar
            def _(act):
                def step(n0, t0, s, n, b, q):
                    m = q % 2
                    if b is not None and isinstance(s, int) and s == 2:
                        act.wait_ge(state_ready, b * STATES + 1)
                        nc.scalar.activation(st[0:LT, 0, :], ps_state[0:LT, 0:DIM], ACT.Copy).then_inc(state_copied, 1)
                    if live(s, 0, n):
                        no = n0 + s
                        act.wait_ge(kqt_ready, no + 1)
                        after(act, o_ready, two_before(no, s))
                        nc.scalar.activation(kq_t[:, m, :, :], ps_kq[:, 0:2 * P].rearrange("p (c n) -> p c n", c=2), ACT.Copy).then_inc(kqt_copied, 1)
                    if live(s, 2, n):
                        no, t = n0 + s - 2, s - 2
                        if b is not None:
                            act.wait_ge(state_ready, b * STATES + t + 2)
                            nc.scalar.activation(st[0:LT, 1 - m, :], ps_state[0:LT, 0:DIM], ACT.Copy).then_inc(state_copied, 1)
                        act.wait_ge(agg_done, no + 1)
                        after(act, rstd_done, two_before(no, t))
                        nc.scalar.activation(ln_std[:, m:m + 1], ln_agg[:, m, 1:2], ACT.Sqrt, bias=g["eps"][:, :]).then_inc(std_done, 1)
                    if live(s, 3, n):
                        no, t = n0 + s - 3, s - 3
                        act.wait_ge(yt_ready, no + 1)
                        after(act, w_ready, two_before(no, t))
                        nc.scalar.activation(y_t[:, 1 - m, :, :], ps_yt[:, 0:DIM].rearrange("p (k n) -> p k n", k=KC), ACT.Copy).then_inc(yt_copied, 1)
                order(act, step)

            @block.vector
            def _(dve):
                def step(n0, t0, s, n, b, q):
                    m = q % 2
                    if b is None and s == 0:
                        dve.wait_ge(kq_ready, 1)
                        nc.vector.tensor_copy(kcls[:, :], kq[0:1, 0, 0, :]).then_inc(cls_kept, 1)
                        nc.vector.tensor_copy(vcls[:, :], V[0:1, CLS * DIM:NT * DIM]).then_inc(cls_kept, 1)
                    if live(s, 2, n):
                        no, t = n0 + s - 2, s - 2
                        dve.wait_ge(o_ready, no + 1)
                        nc.vector.bn_stats(ln_raw[:, m, :], ps_o[m][:, 0:DIM]).then_inc(raw_done, 1)
                        after(dve, y_ready, two_before(no, t))
                        dve.wait_ge(raw_done, no + 1)
                    if live(s, 1, n):
                        no, t = n0 + s - 1, s - 1
                        dve.wait_ge(s_ready, no + 1)
                        after(dve, o_ready, two_before(no, t))
                        mask = ident if b is None else const[:, C_TRI:C_TRI + P]
                        nc.vector.tensor_tensor(masked[:, 1 - m, :], ps_s[:, 0:P], mask, ALU.mult).then_inc(masked_ready, 1)
                    if live(s, 3, n):
                        no = n0 + s - 3
                        dve.wait_ge(std_done, no + 1)
                        nc.vector.reciprocal(ln_rstd[:, 1 - m:2 - m], ln_std[:, 1 - m:2 - m]).then_inc(rstd_done, 1)
                        dve.wait_ge(rstd_done, no + 1)
                        after(dve, yt_ready, two_before(no, s - 3))
                        nc.vector.tensor_scalar(y[:, 1 - m, :], ps_o[1 - m][:, 0:DIM], ln_agg[:, 1 - m, 0:1], ln_rstd[:, 1 - m:2 - m],
                                                ALU.subtract, ALU.mult).then_inc(y_ready, 1)
                    if live(s, 2, n):
                        nc.vector.bn_aggr(ln_agg[:, m, :], ln_raw[:, m, :]).then_inc(agg_done, 1)
                    if live(s, 4, n):
                        no, t = n0 + s - 4, t0 + s - 4
                        dve.wait_ge(w_ready, no + 1)
                        tile = h[:, bass.ds(t * DIM, DIM)]
                        nc.vector.tensor_tensor(tile, ps_w[:, 0:DIM], tile, ALU.add).then_inc(h_done, 1)
                        dve.wait_ge(h_done, no + 1)
                        nc.vector.bn_stats(raw[:, bass.ds(t * 6, 6)], tile)
                order(dve, step)


ROUTED = (IMG * IMG + 1) // 2 - 1
FH = 4 * DIM
FC = FH // P
DIGIT, ROUNDS = 4, 8
NCAND = 2 ** DIGIT - 1
COLS = TPB + 1


def router(nc, g, a):
    with ExitStack() as ctx:
        sb = lambda name, shape, dt=F32: ctx.enter_context(nc.sbuf_tensor(name, shape, dt))
        sem = lambda name: ctx.enter_context(nc.semaphore(name))
        h, mean, rstd, sw, const = g["h"], g["mean"], g["rstd"], g["sw"], g["const"]
        SLOTS = 8
        wr, prod = sb("wr", [P, DIM + 1]), sb("w_prod", [P, SLOTS, DIM])
        tok_w = sb("tok_w", [P, NT])
        w = sb("w_cols", [P, B, COLS])
        ge = sb("ge", [P, B, NCAND, COLS])
        cnt = sb("cnt", [P, B, NCAND])
        key, cand, sign, cut = (sb(n, [P, B, NCAND], I32) for n in ("key", "cand", "sign", "cut"))
        over = sb("over", [P, B, NCAND])
        dig_f, dig_i = sb("dig_f", [P, B]), sb("dig_i", [P, B], I32)
        prefix = sb("prefix", [P, B], I32)
        gt, eq, rank = sb("gt", [P, B, COLS]), sb("eq", [P, B, COLS]), sb("rank", [P, B, COLS])
        ngt = sb("ngt", [P, B])
        step_done, sums_wanted, sums_ready = sem("r_step_done"), sem("sums_wanted"), sem("r_sums_ready")
        w_done, wr_loaded, w_high = sem("w_done"), sem("wr_loaded"), sem("ffn_w_high")
        digits = sb("digits", [P, ROUNDS, NCAND], I32)
        ps, ps_rank, ps_cols = g["bank"][0:3]
        ones, tri = const[:, C_ONES:C_ONES + P], const[:, C_TRI:C_TRI + P]
        with nc.Block() as block:
            @block.sync
            def _(sp):
                sp.dma_start(wr[:, :], a["ffn_wr"].to_broadcast([P, DIM + 1])).then_inc(wr_loaded, 16)
                sp.dma_start(digits[:, :, :], a["digits"].to_broadcast([P, ROUNDS * NCAND])
                             .rearrange("p (r n) -> p r n", r=ROUNDS)).then_inc(wr_loaded, 16)
                sp.dma_start(g["ffn_w1"][:, :, :], a["ffn_w1"].rearrange("(k p) n -> p k n", p=P)).then_inc(wr_loaded, 16)
                sp.dma_start(g["ffn_w2"][:, :, :], a["ffn_w2"].rearrange("(k p) n -> p k n", p=P)).then_inc(wr_loaded, 16)
                sp.dma_start(g["ffn_b1"][:, :], a["ffn_b1"]).then_inc(wr_loaded, 16)
                sp.wait_ge(wr_loaded, 80)

            @block.scalar
            def _(act):
                act.wait_ge(wr_loaded, 80)
                for name in ("ffn_w1", "ffn_w2"):
                    nc.scalar.activation(g[name + "_hl"][:, HI], g[name][:, :, :], ACT.Copy).then_inc(w_high, 1)

            @block.gpsimd
            def _(pool):
                for i, name in enumerate(("ffn_w1", "ffn_w2")):
                    pool.wait_ge(w_high, i + 1)
                    nc.gpsimd.tensor_tensor(g[name + "_hl"][:, LO], g[name][:, :, :], high(g[name + "_hl"][:, HI]), ALU.subtract)

            @block.vector
            def _(dve):
                dve.wait_ge(wr_loaded, 80)
                V = nc.vector
                count = [0]

                def done(ins):
                    count[0] += 1
                    ins.then_inc(step_done, 1)
                    dve.wait_ge(step_done, count[0])

                def weigh(t, i):
                    return V.scalar_tensor_tensor(out=prod[:, i, :], in0=h[:, bass.ds(t * DIM, DIM)], scalar=mean[:, bass.ds(t, 1)], in1=wr[:, 0:DIM],
                                                  op0=ALU.subtract, op1=ALU.mult, accum_out=tok_w[:, bass.ds(t, 1)])
                with dve.Fori(0, NPAIR // SLOTS) as r:
                    for i in range(SLOTS):
                        weigh(r * SLOTS + i, i).then_inc(w_done, 1)
                    dve.wait_ge(w_done, (r + 1) * SLOTS)
                done(weigh(CLS, 0))
                done(V.memset(w[:, :, :], -3.4e38))
                done(V.tensor_tensor(tok_w[:, :], tok_w[:, :], rstd[:, :], ALU.mult))
                done(V.memset(prefix[:, :], 0))
                done(V.tensor_scalar(tok_w[:, :], tok_w[:, :], wr[:, DIM:DIM + 1], None, ALU.add))
                V.tensor_copy(w[:, :, 1:COLS], tok_w[:, 0:NPAIR].rearrange("p (b t) -> p b t", b=B))
                done(V.tensor_copy(w[0:1, :, 0:1], tok_w[0:1, CLS:NT].unsqueeze(1).to_broadcast([1, B, 1])))
                four = [P, B, NCAND, COLS]
                for r in range(ROUNDS):
                    shift = DIGIT * (ROUNDS - 1 - r)
                    done(V.tensor_tensor(cand[:, :, :], prefix[:, :].unsqueeze(2).to_broadcast([P, B, NCAND]),
                                         digits[:, r, :].unsqueeze(1).to_broadcast([P, B, NCAND]), ALU.bitwise_or))
                    done(V.tensor_scalar(sign[:, :, :], cand[:, :, :], 31, 0x7FFFFFFF, ALU.arith_shift_right, ALU.bitwise_and))
                    done(V.tensor_tensor(cut[:, :, :], cand[:, :, :], sign[:, :, :], ALU.bitwise_xor))
                    done(V.tensor_scalar(cut[:, :, :], cut[:, :, :], -1, None, ALU.bitwise_xor))
                    for b in range(B):
                        n = V.tensor_tensor(ge[:, b], w[:, b, :].unsqueeze(1).to_broadcast([P, NCAND, COLS]),
                                            cut[:, b, :].bitcast(F32).unsqueeze(2).to_broadcast([P, NCAND, COLS]), ALU.is_ge)
                    done(n)
                    V.tensor_reduce(cnt[:, :, :], ge[:, :, :, :], AX_X, ALU.add).then_inc(sums_wanted, 1)
                    dve.wait_ge(sums_ready, r + 1)
                    done(V.tensor_scalar(over[:, :, :], ps[:, 0:B * NCAND].rearrange("p (b n) -> p b n", b=B), float(ROUTED), None, ALU.is_ge))
                    done(V.tensor_reduce(dig_f[:, :], over[:, :, :], AX_X, ALU.add))
                    done(V.tensor_copy(dig_i[:, :], dig_f[:, :]))
                    if shift:
                        done(V.tensor_scalar(dig_i[:, :], dig_i[:, :], shift, None, ALU.logical_shift_left))
                    done(V.tensor_tensor(prefix[:, :], prefix[:, :], dig_i[:, :], ALU.bitwise_or))
                done(V.tensor_scalar(dig_i[:, :], prefix[:, :], 31, 0x7FFFFFFF, ALU.arith_shift_right, ALU.bitwise_and))
                done(V.tensor_tensor(prefix[:, :], prefix[:, :], dig_i[:, :], ALU.bitwise_xor))
                done(V.tensor_scalar(prefix[:, :], prefix[:, :], -1, None, ALU.bitwise_xor))
                thr = prefix[:, :].bitcast(F32).unsqueeze(2).to_broadcast([P, B, COLS])
                V.tensor_tensor(gt[:, :, :], w[:, :, :], thr, ALU.is_gt)
                done(V.tensor_tensor(eq[:, :, :], w[:, :, :], thr, ALU.is_equal))
                V.tensor_reduce(ngt[:, :], gt[:, :, :], AX_X, ALU.add).then_inc(sums_wanted, 1)
                dve.wait_ge(sums_ready, ROUNDS + 1)
                done(V.tensor_scalar(ngt[:, :], ps[:, 0:B], -1.0, float(ROUTED), ALU.mult, ALU.add))
                for b in range(B):
                    n = V.tensor_tensor_scan(rank[:, b, :], ones[:, 0:COLS], ps_cols[:, b * COLS:(b + 1) * COLS], 0.0, ALU.mult, ALU.add)
                done(n)
                flat = rank[:, :, :].rearrange("p b t -> p (b t)")
                done(V.tensor_tensor(flat, flat, ps_cols[:, 0:B * COLS], ALU.subtract))
                done(V.tensor_tensor(flat, flat, ps_rank[:, 0:B * COLS], ALU.add))
                for b in range(B):
                    n = V.tensor_scalar(rank[:, b, :], rank[:, b, :], ngt[:, b:b + 1], None, ALU.is_le)
                done(n)
                done(V.tensor_tensor(eq[:, :, :], eq[:, :, :], rank[:, :, :], ALU.mult))
                done(V.tensor_tensor(gt[:, :, :], gt[:, :, :], eq[:, :, :], ALU.add))
                V.tensor_tensor(sw[:, 0:NPAIR].rearrange("p (b t) -> p b t", b=B), gt[:, :, 1:COLS], w[:, :, 1:COLS], ALU.mult)
                V.tensor_tensor(sw[:, NPAIR:NPAIR + B], gt[:, :, 0], w[:, :, 0], ALU.mult)

            @block.tensor
            def _(pe):
                for r in range(ROUNDS):
                    pe.wait_ge(sums_wanted, r + 1)
                    nc.tensor.matmul(ps[:, 0:B * NCAND], ones, cnt[:, :, :].rearrange("p b n -> p (b n)"), start=True, stop=True).then_inc(sums_ready, 1)
                pe.wait_ge(sums_wanted, ROUNDS + 1)
                eqs = eq[:, :, :].rearrange("p b t -> p (b t)")
                nc.tensor.matmul(ps_rank[:, 0:B * COLS], tri, eqs, start=True, stop=True)
                nc.tensor.matmul(ps_cols[:, 0:B * COLS], ones, eqs, start=True, stop=True)
                nc.tensor.matmul(ps[:, 0:B], ones, ngt[:, :], start=True, stop=True).then_inc(sums_ready, 1)


def feed_forward(nc, g, a, out):
    with ExitStack() as ctx:
        sb = lambda name, shape, dt=F32: ctx.enter_context(nc.sbuf_tensor(name, shape, dt))
        sem = lambda name: ctx.enter_context(nc.semaphore(name))
        RING = 4
        w1, w2, b1 = g["ffn_w1_hl"], g["ffn_w2_hl"], g["ffn_b1"]
        xn = sb("f_xn", [P, UNIT, DIM])
        xn_t = sb("f_xn_t", [P, 2, KC, UTOK], F32R)
        hid = sb("f_hid", [P, RING, UTOK])
        hid_hl = sb("f_hid_hl", [P, 2, FC, UTOK], F32R)
        res = sb("f_res", [P, 2, UNIT, DIM])
        xn_ready, base_done, xt_ready, xt_high, xt_split = sem("f_xn_ready"), sem("f_base_done"), sem("f_xt_ready"), sem("f_xt_high"), sem("f_xt_split")
        hid_ready, gelu_done, hid_high, hid_split = sem("f_hid_ready"), sem("f_gelu_done"), sem("f_hid_high"), sem("f_hid_split")
        y_ready, res_ready = sem("f_y_ready"), sem("f_res_ready")
        stored = [sem("stored0"), sem("stored1")]
        ps_t0, ps_t1 = g["bank"][0:2]
        ring, ps_y = g["bank"][2:2 + RING], g["bank"][2 + RING:8]
        h, mean, rstd, sw, ident = g["h"], g["mean"], g["rstd"], g["sw"], g["const"][:, C_ID:C_ID + P]
        ones3, bias3 = g["ones3"], g["bias3"]
        HC = UNIT // 2
        is_cls = lambda u: isinstance(u, int) and u == NUNIT
        tiles = lambda u: 1 if is_cls(u) else UNIT
        first = lambda u: isinstance(u, int) and u == 0

        def order(eng, unit):
            unit(0, 0)
            unit(1, 1)
            with eng.Fori(1, NUNIT // 2 - 1) as r:
                unit(r * 2, 0)
                unit(r * 2 + 1, 1)
            unit(NUNIT - 2, 0)
            unit(NUNIT - 1, 1)
            unit(NUNIT, 0)

        with nc.Block() as block:
            @block.sync
            def _(sp):
                rows = out.rearrange("b t d -> (b t) d")
                seq = IMG * IMG + 1
                for b in range(B):
                    with sp.Fori(0, NUNIT // B // 2) as r:
                        for i in range(2):
                            sp.wait_ge(res_ready, (b * (NUNIT // B) + r * 2 + i + 1) * HC)
                            sp.dma_start(rows[bass.ds(b * seq + 1 + (r * 2 + i) * UTOK, UTOK), :].rearrange("(i p) d -> p i d", p=P),
                                         res[:, i, :, :]).then_inc(stored[i], 16)
                for b in range(B):
                    sp.wait_ge(res_ready, NUNIT * HC + b + 1)
                    sp.dma_start(rows[b * seq:b * seq + 1, :], res[0:1, 0, b, :]).then_inc(stored[0], 16)
                sp.wait_ge(stored[0], 16 * (NUNIT // 2 + B))
                sp.wait_ge(stored[1], 16 * (NUNIT // 2))

            @block.vector
            def _(dve):
                def normalise(u):
                    after(dve, xt_ready, u)
                    after(dve, base_done, u)
                    for i in range(tiles(u)):
                        t = u * UNIT + i
                        n = nc.vector.tensor_scalar(xn[:, i, :], h[:, bass.ds(t * DIM, DIM)], mean[:, bass.ds(t, 1)],
                                                    rstd[:, bass.ds(t, 1)], ALU.subtract, ALU.mult)
                    n.then_inc(xn_ready, 1)

                def low_xt(u):
                    dve.wait_ge(xt_high, u + 1)
                    n = tiles(u) * P
                    for k, src in enumerate((ps_t0, ps_t1)):
                        t = nc.vector.tensor_tensor(xn_t[:, LO, k, 0:n], src[:, 0:n], high(xn_t[:, HI, k, 0:n]), ALU.subtract)
                    t.then_inc(xt_split, 1)

                def low_hid(u, chunks):
                    n = tiles(u) * P
                    for c in chunks:
                        dve.wait_ge(hid_high, u * FC + c + 1)
                        nc.vector.tensor_tensor(hid_hl[:, LO, c, 0:n], hid[:, c % RING, 0:n], high(hid_hl[:, HI, c, 0:n]),
                                                ALU.subtract).then_inc(hid_split, 1)

                def combine(u, m):
                    for c in range(1 if is_cls(u) else HC):
                        dve.wait_ge(y_ready, u * HC + c + 1)
                        dve.wait_ge(base_done, u + 1)
                        if not (isinstance(u, int) and u < 2):
                            dve.wait_ge(stored[m], 16 * ((u - m) // 2) if isinstance(u, int) else (u - m) * 8)
                        for i in range(2):
                            t = NPAIR + i if is_cls(u) else u * UNIT + 2 * c + i
                            src = 0 if is_cls(u) else i
                            base = h[:, CLS * DIM:NT * DIM] if is_cls(u) else h[:, bass.ds(t * DIM, DIM)]
                            k = nc.vector.scalar_tensor_tensor(out=res[:, m, 2 * c + i, :], in0=ps_y[c][:, src * DIM:(src + 1) * DIM],
                                                               scalar=sw[:, bass.ds(t, 1)], in1=base, op0=ALU.mult, op1=ALU.add)
                            if is_cls(u):
                                k.then_inc(res_ready, 1)
                        if not is_cls(u):
                            k.then_inc(res_ready, 1)

                def unit(u, m):
                    if first(u):
                        normalise(u)
                        low_xt(u)
                    low_hid(u, range(FC // 2))
                    if not is_cls(u):
                        normalise(u + 1)
                    low_hid(u, range(FC // 2, FC))
                    if not is_cls(u):
                        low_xt(u + 1)
                    combine(u, m)
                order(dve, unit)

            @block.gpsimd
            def _(pool):
                def unit(u, m):
                    pool.wait_ge(xn_ready, u + 1)
                    for i in range(tiles(u)):
                        tile = h[:, bass.ds((u * UNIT + i) * DIM, DIM)]
                        n = nc.gpsimd.tensor_tensor(tile, tile, xn[:, i, :], ALU.add)
                    n.then_inc(base_done, 1)
                order(pool, unit)

            @block.scalar
            def _(act):
                def high_xt(u):
                    act.wait_ge(xt_ready, u + 1)
                    after(act, hid_ready, u * FC)
                    n = tiles(u) * P
                    for k, src in enumerate((ps_t0, ps_t1)):
                        t = nc.scalar.activation(xn_t[:, HI, k, 0:n], src[:, 0:n], ACT.Copy)
                    t.then_inc(xt_high, 1)

                def high_hid(u, c):
                    n = tiles(u) * P
                    act.wait_ge(gelu_done, u * FC + c + 1)
                    nc.scalar.activation(hid_hl[:, HI, c, 0:n], hid[:, c % RING, 0:n], ACT.Copy).then_inc(hid_high, 1)

                def unit(u, m):
                    n = tiles(u) * P
                    if first(u):
                        high_xt(u)
                    for c in range(FC):
                        act.wait_ge(hid_ready, u * FC + c + 1)
                        if c == 1:
                            after(act, y_ready, u * HC)
                        if c >= RING:
                            act.wait_ge(hid_split, u * FC + c + 1 - RING)
                        elif c == 0:
                            after(act, hid_split, u * FC)
                        nc.scalar.activation(hid[:, c % RING, 0:n], ring[c % RING][:, 0:n], ACT.Gelu_apprx_tanh, bias=b1[:, c:c + 1]).then_inc(gelu_done, 1)
                        if c:
                            high_hid(u, c - 1)
                    high_hid(u, FC - 1)
                    if not is_cls(u):
                        high_xt(u + 1)
                order(act, unit)

            @block.tensor
            def _(pe):
                def turn(u):
                    pe.wait_ge(xn_ready, u + 1)
                    after(pe, xt_split, u)
                    for k, dst in enumerate((ps_t0, ps_t1)):
                        for i in range(tiles(u)):
                            t = nc.tensor.transpose(dst[:, i * P:(i + 1) * P], xn[:, i, k * P:(k + 1) * P], ident)
                    t.then_inc(xt_ready, 1)

                def unit(u, m):
                    n = tiles(u) * P
                    if first(u):
                        turn(u)
                    pe.wait_ge(xt_split, u + 1)
                    for c in range(FC):
                        if c >= RING:
                            pe.wait_ge(gelu_done, u * FC + c + 1 - RING)
                        for k in range(KC):
                            t = product(nc, ring[c % RING][:, 0:n], parts(lambda e: w1[:, e, k, c * P:(c + 1) * P]),
                                        parts(lambda e: xn_t[:, e, k, 0:n]), k == 0, k == KC - 1)
                        t.then_inc(hid_ready, 1)
                    if not is_cls(u):
                        turn(u + 1)
                    for c in range(1 if is_cls(u) else HC):
                        after(pe, res_ready, (u - 1) * HC + c + 1)
                        for i in range(1 if is_cls(u) else 2):
                            i0 = (2 * c + i) * P
                            y = ps_y[c][:, i * DIM:(i + 1) * DIM]
                            nc.tensor.matmul(y, ones3[:, :], bias3[:, 6 * DIM:7 * DIM], start=True, stop=False)
                            for k in range(FC):
                                if c == 0 and i == 0:
                                    pe.wait_ge(hid_split, u * FC + k + 1)
                                t = product(nc, y, parts(lambda e: hid_hl[:, e, k, i0:i0 + P]), parts(lambda e: w2[:, e, k, :]), False, k == FC - 1)
                        t.then_inc(y_ready, 1)
                order(pe, unit)


def constants():
    c = np.zeros((P, NCONST), np.float32)
    p = np.arange(P)
    c[:, C_ID:C_ID + P] = np.eye(P)
    c[:, C_TRI:C_TRI + P] = p[:, None] <= p[None, :]
    c[:, C_STRICT:C_STRICT + P] = p[:, None] < p[None, :]
    c[:, C_ONES:C_ONES + P] = 1
    half = HD // 2
    inv_freq = (1.0 / 10000.0 ** (np.arange(0, half, 2, dtype=np.float32) / half)).astype(np.float32)
    row, col = (p % WTOK) // WIN, p % WIN
    ang = np.concatenate([row[:, None] * inv_freq, col[:, None] * inv_freq], 1).astype(np.float32)
    c[:, C_COS:C_COS + HD] = np.repeat(np.cos(ang), 2, axis=1)
    s = np.repeat(np.sin(ang), 2, axis=1)
    s[:, 0::2] *= -1
    c[:, C_SIN:C_SIN + HD] = s
    c[:, C_HEAD:C_HEAD + 4] = p[:, None] // HD == np.arange(4)
    c[:, C_POS:C_POS + TPB] = 1 + p[:, None] + P * np.arange(TPB)
    seg = np.ones((8, TPB))
    seg[:, 0] = 0
    c[:, C_SEG:] = seg.reshape(1, -1)
    return c


def program(nc, a, out):
    with ExitStack() as ctx:
        sb = lambda name, shape, dt=F32: ctx.enter_context(nc.sbuf_tensor(name, shape, dt))
        g = {"bank": [ctx.enter_context(nc.psum_tensor(f"bank{i}", [P, 512], F32)) for i in range(8)]}
        g["const"] = sb("const", [P, NCONST])
        g["h"] = sb("h", [P, NT * DIM])
        g["raw"] = sb("raw", [P, NT * 6])
        g["mean"], g["rstd"] = sb("mean", [P, NT]), sb("rstd", [P, NT])
        g["scal"] = sb("scal", [P, NSCAL])
        scalars = sb("scalars", [P, 10 + KF // 2])
        at = 0
        g["sc"] = {}
        for name, n in (("setw", SETS), ("posw", 1), ("rscale", 1), ("rthr", 1), ("count", 1), ("ltmw", 1), ("nthr", 1), ("wtab", KF // 2)):
            g["sc"][name] = scalars[:, at:at + n]
            at += n
        g["ones3"], g["bias3"] = sb("ones3", [3, P], BF16), sb("bias3", [3, NBIAS], BF16)
        g["half_pi"], g["eps"] = sb("half_pi", [P, 1]), sb("eps", [P, 1])
        g["sw"] = sb("sw", [P, NPAIR + B])
        with ExitStack() as mid:
            sm = lambda name, shape, dt=F32: mid.enter_context(nc.sbuf_tensor(name, shape, dt))
            g["wout"] = sm("wout", [P, KC, DIM])
            g["st"] = sm("st", [P, 2, DIM])
            g["post"] = sm("post", [P, TPB + 1, 2, PLANES])
            g["rpos"] = sm("rpos", [P, TPB])
            g["wg"], g["gg"], g["jcls"] = sm("wg", [P, NT]), sm("gg", [P, 2, NT]), sm("jcls", [P, 2 * JOINT])
            prologue(nc, g, a)
            g["V"], g["th"] = sm("V", [P, NT * DIM]), sm("th", [P, NT * NCOL])
            with ExitStack() as early:
                se = lambda name, shape: early.enter_context(nc.sbuf_tensor(name, shape, F32R))
                g["enc_w1"], g["enc_wv"], g["enc_w2"] = se("enc_w1", [P, 2, KC, NHID * P]), se("enc_wv", [P, 2, KC, DIM]), se("enc_w2", [P, 2, NHID, NCOL])
                tokenizer(nc, g, a)
                normaliser(nc, g, "_1")
                encoders(nc, g, a)
            g["trig"], g["kq"] = sm("trig", [P, NT, 2, NPH]), sm("kq", [P, 4, 2, P])
            phasors(nc, g)
            retrieval(nc, g)
        normaliser(nc, g, "_2")
        g["ffn_w1"], g["ffn_w2"], g["ffn_b1"] = sb("ffn_w1", [P, KC, FH]), sb("ffn_w2", [P, FC, DIM]), sb("ffn_b1", [P, FC])
        g["ffn_w1_hl"], g["ffn_w2_hl"] = sb("ffn_w1_hl", [P, 2, KC, FH], F32R), sb("ffn_w2_hl", [P, 2, FC, DIM], F32R)
        router(nc, g, a)
        feed_forward(nc, g, a, out)


def columns(v):
    return v.reshape(-1, P).T


def kernel(**inputs):
    import concourse.bacc as bacc
    from concourse.bass_utils import run_bass_kernel_spmd

    i = {k.removeprefix("L0_"): np.asarray(v) for k, v in inputs.items()}
    w = WIN
    mem = i["attn_ltm_binding_mem"]
    w2 = np.zeros((NHID * P, NCOL), np.float32)
    b2 = np.zeros((NCOL, 2), np.float32)
    b2[:, 1] = 1.0
    b2[COL_G, 1] = 0.5
    at = 0
    for name, col, n in (("ke", COL_K + JOINT, PLANES), ("qe", COL_Q + JOINT, PLANES), ("lke", COL_L, PLANES), ("gate", COL_G, 1)):
        hidden = i[f"attn_{name}_w2"].shape[0]
        w2[at:at + hidden, col:col + n] = i[f"attn_{name}_w2"]
        b2[col:col + n, 0] = i[f"attn_{name}_b2"]
        at += hidden
    digits = (np.arange(1, NCAND + 1, dtype=np.int64)[None, :] << (DIGIT * (ROUNDS - 1 - np.arange(ROUNDS)))[:, None])
    arrays = {
        "const": constants(),
        "digits": digits.astype(np.uint32).view(np.int32).reshape(1, -1),
        "x_t": i["x"].reshape(B, IMG // w, w, IMG // w, w, DIM).transpose(5, 0, 1, 3, 2, 4).reshape(DIM, NUNIT, UTOK),
        "cls": i["cls_tok"].reshape(1, DIM),
        "qkv_w": i["tok_qkv_w"].T,
        "proj_w": i["tok_proj_w"].T,
        "bias": np.concatenate([i["tok_qkv_b"], i["tok_proj_b"], i["attn_v_b"], i["attn_out_b"], i["ffn_b2"]])[None],
        "scal": np.concatenate([i["attn_set_weights"]] + [i[f"attn_{n}"].reshape(1) for n in (
            "pos_weight", "surprise_scale", "surprise_bias", "resonance_scale", "resonance_threshold", "ltm_weight", "ltm_count")]
            + [i["attn_pos_freqs"]])[None],
        "enc_w1": np.concatenate([i[f"attn_{n}_w1"] for n in ("ke", "qe", "lke", "gate")], axis=1),
        "enc_b1": columns(np.concatenate([i[f"attn_{n}_b1"] for n in ("ke", "qe", "lke", "gate")])),
        "enc_w2": w2,
        "enc_b2": b2,
        "enc_wv": i["attn_v_w"],
        "out_w": i["attn_out_w"],
        "ln_g": columns(i["attn_out_ln_g"]),
        "ln_b": columns(i["attn_out_ln_b"]),
        "ltm": np.concatenate([mem.real, mem.imag], axis=0),
        "ffn_wr": np.concatenate([i["ffn_wr"].reshape(-1), i["ffn_br"]])[None],
        "ffn_w1": i["ffn_w1"],
        "ffn_b1": columns(i["ffn_b1"]),
        "ffn_w2": i["ffn_w2"],
    }
    arrays = {k: np.ascontiguousarray(v) for k, v in arrays.items()}
    nc = bacc.Bacc("TRN2", target_bir_lowering=False, num_devices=1)
    a = {k: nc.dram_tensor(f"in_{k}", v.shape, mybir.dt.from_np(v.dtype), kind="ExternalInput").ap() for k, v in arrays.items()}
    out = nc.dram_tensor("out", [B, IMG * IMG + 1, DIM], F32, kind="ExternalOutput").ap()
    program(nc, a, out)
    r = run_bass_kernel_spmd(nc, [{f"in_{k}": v for k, v in arrays.items()}], core_ids=[0])
    return r.results[0]["out"]
```

```python
from contextlib import ExitStack

import numpy as np

import concourse.bass as bass
from concourse import mybir

ALU = mybir.AluOpType
ACT = mybir.ActivationFunctionType
AX_X = mybir.AxisListType.X
F32 = mybir.dt.float32
F32R = mybir.dt.float32r
BF16 = mybir.dt.bfloat16
I32 = mybir.dt.int32

P = 128
B, IMG, DIM = 2, 64, 256
KC = DIM // P
WIN, HEADS = 8, 8
HD = DIM // HEADS
WTOK = WIN * WIN
NPAIR = B * IMG * IMG // P
UNIT = 4
NUNIT = NPAIR // UNIT
UTOK = UNIT * P
TPB = IMG * IMG // P
CLS = NPAIR
NT = NPAIR + 1
EPS = 1e-5
SCALE = HD ** -0.5

C_ID, C_TRI, C_STRICT, C_ONES = 0, P, 2 * P, 3 * P
C_COS = 4 * P
C_SIN = C_COS + HD
C_HEAD = C_SIN + HD
C_POS = C_HEAD + 4
C_SEG = C_POS + TPB
SEQ = IMG * IMG + 1
ROUTED = SEQ // 2 - 1
PACK = -(-ROUTED // P)
COLS = TPB + 1
NCONST = C_SEG + 8 * TPB
C_IOTA = 0
C_HIGH = C_IOTA + P
C_LOW = C_HIGH + COLS
C_BASE = C_LOW + COLS
NPLACE = C_BASE + B * PACK


def after(eng, sem, value):
    if not isinstance(value, int) or value > 0:
        eng.wait_ge(sem, value)


HI, LO = 0, 1


def high(ap):
    return ap.bitcast(F32)


def parts(f):
    return f(HI), f(LO)


def product(nc, out, lhs, rhs, start, stop):
    nc.tensor.matmul(out, lhs[HI], rhs[HI], start=start, stop=False)
    nc.tensor.matmul(out, lhs[HI], rhs[LO], start=False, stop=False)
    return nc.tensor.matmul(out, lhs[LO], rhs[HI], start=False, stop=stop)


def tokenizer(nc, g, a):
    with ExitStack() as ctx:
        sb = lambda name, shape, dt=F32: ctx.enter_context(nc.sbuf_tensor(name, shape, dt))
        sem = lambda name: ctx.enter_context(nc.semaphore(name))
        early = g["early"]
        wqkv_hl, wproj, xt, x_loaded = g["wqkv_hl"], g["wproj"], g["xt"], g["x_loaded"]
        enc_w = [early(n, m) for n, m in ((KC, NHID * P), (KC, DIM), (NHID, NCOL))]
        x_t, enc_hl = a["x_t"], (g["enc_w1"], g["enc_wv"], g["enc_w2"])
        xt_hl = sb("xt_hl", [P, 2, 2, KC, P], F32R)
        rope_c, rope_s, qk_rot = (early(1, 2 * DIM)[:, 0] for _ in range(3))
        q_t = sb("q_t", [P, KC, P])
        k_blk = early(KC, 8 * WTOK).rearrange("p k (w h n) -> p k w h n", w=2, h=4)
        v_half = early(UNIT, 2 * P).rearrange("p j (w n) -> p j w n", w=2)
        probs = early(2, HEADS * WTOK).rearrange("p j (h n) -> p j h n", h=HEADS)
        smax = sb("smax", [P, HEADS])
        ssum = sb("ssum", [P, HEADS])
        sinv = sb("sinv", [P, HEADS])
        p_t = sb("p_t", [P, 4, 2, WTOK])
        o_t = early(KC, UTOK)

        enc_loaded, enc_high = sem("enc_loaded"), sem("enc_high")
        x_high, x_split = sem("x_high"), sem("x_split")
        qk_ready, v_ready, tq_ready, sc_ready = sem("qk_ready"), sem("v_ready"), sem("tq_ready"), sem("sc_ready")
        pt_ready, av_ready, proj_ready = sem("pt_ready"), sem("av_ready"), sem("proj_ready")
        rope_done, rope_added, v_copied, qt_copied = sem("rope_done"), sem("rope_added"), sem("v_copied"), sem("qt_copied")
        kblk_done, max_done, sub_done, exp_done, sum_done = sem("kblk_done"), sem("max_done"), sem("sub_done"), sem("exp_done"), sem("sum_done")
        inv_done = sem("inv_done")
        p_ready, pt_copied, out0_copied, out1_copied = sem("p_ready"), sem("pt_copied"), sem("out0_copied"), sem("out1_copied")
        h_copied = sem("h_copied")

        ps_qk, ps_v, ps_tq, ps_sc, ps_pt, ps_av0, ps_av1, ps_proj = g["bank"]
        const, h, raw = g["const"], g["h"], g["raw"]
        ident = const[:, C_ID:C_ID + P]
        cos = const[:, C_COS:C_COS + HD]
        sin = const[:, C_SIN:C_SIN + HD]
        ones3, bias3 = g["ones3"], g["bias3"]
        LAST = NPAIR

        def live(s, lag):
            return not isinstance(s, int) or 0 <= s - lag < LAST

        def steps(eng, step):
            for s in range(2 * UNIT):
                step(s, s % UNIT, s // UNIT)
            with eng.Fori(2, NUNIT) as u:
                for j in range(UNIT):
                    step(u * UNIT + j, j, u)
            for s in range(LAST, LAST + 4):
                step(s, s % UNIT, NUNIT)

        def split_steps(eng, step):
            for s in range(UNIT):
                step(s, s, 0)
            with eng.Fori(1, NUNIT - 1) as u:
                for j in range(UNIT):
                    step(u * UNIT + j, j, u)
            for s in range(LAST - UNIT, LAST + 4):
                step(s, s % UNIT, s // UNIT)

        def next_x(s, j, u, split):
            if not isinstance(s, int) or s + 1 < LAST:
                split(s + 1, (j + 1) % UNIT, u + (j + 1) // UNIT)

        def o_rows(q, c, pair):
            return o_t[q * HD:(q + 1) * HD, c, :].rearrange("p (r w n) -> p w r n", r=WIN, w=WIN)[:, 2 * pair:2 * pair + 2]

        def o_head(ps, q):
            return ps[q * HD:(q + 1) * HD, :].rearrange("p (w h r n) -> p w h r n", w=2, h=4, r=WIN)[:, :, q]

        def unit_done(s, j, half):
            return j == 2 + half and (not isinstance(s, int) or s >= UNIT)

        with nc.Block() as block:
            @block.sync
            def _(sp):
                for w, name in zip(enc_w, ("enc_w1", "enc_wv", "enc_w2")):
                    sp.dma_start(w[:, :, :], a[name].rearrange("(k p) n -> p k n", p=P)).then_inc(enc_loaded, 16)
                with sp.Fori(1, NUNIT) as u:
                    for j in range(UNIT):
                        sp.wait_ge(x_split, u * UNIT + j - 3)
                        sp.dma_start(xt[:, j, :, :], x_t[:, bass.ds(u, 1), j * P:(j + 1) * P]
                                     .rearrange("(k p) a n -> p k (a n)", p=P)).then_inc(x_loaded[j], 16)

            @block.tensor
            def _(pe):
                def project(u, half):
                    if half:
                        pe.wait_ge(h_copied, (u - 1) * 2 + half)
                    for i in range(2):
                        po, tile = ps_proj[:, i * DIM:(i + 1) * DIM], 2 * half + i
                        for k in range(KC):
                            nc.tensor.matmul(po, o_t[:, k, tile * P:(tile + 1) * P], wproj[:, k, :], start=(k == 0), stop=False)
                        t = nc.tensor.matmul(po, ones3[:, :], bias3[:, 3 * DIM:4 * DIM], start=False, stop=True)
                    t.then_inc(proj_ready, 1)

                def step(s, j, u):
                    if live(s, 1):
                        pe.wait_ge(rope_added, s)
                        after(pe, kblk_done, s - 1)
                        for c in range(4):
                            t = nc.tensor.transpose(ps_tq[:, c * P:(c + 1) * P], qk_rot[:, c * P:(c + 1) * P], ident)
                        t.then_inc(tq_ready, 1)
                    if live(s, 0):
                        pe.wait_ge(x_split, s + 1)
                        after(pe, rope_done, s)
                        for k in range(KC):
                            product(nc, ps_qk[:, :], parts(lambda c: xt_hl[:, j % 2, c, k, :]),
                                    parts(lambda c: wqkv_hl[:, c, k, 0:2 * DIM]), k == 0, False)
                        nc.tensor.matmul(ps_qk[:, :], ones3[:, :], bias3[:, 0:2 * DIM], start=False, stop=True).then_inc(qk_ready, 1)
                    if unit_done(s, j, 1):
                        project(u, 1)
                    if live(s, 3):
                        pe.wait_ge(pt_copied, s - 2)
                        pe.wait_ge(v_copied, s - 2)
                        after(pe, out0_copied, s - 3)
                        after(pe, out1_copied, s - 3)
                        for c, dst in enumerate((ps_av0, ps_av1)):
                            for w in range(2):
                                t = nc.tensor.matmul(dst[:, w * 256:(w + 1) * 256],
                                                     v_half[c * WTOK:(c + 1) * WTOK, (j - 3) % UNIT, w, :],
                                                     p_t[c * WTOK:(c + 1) * WTOK, :, w, :], start=True, stop=True)
                        t.then_inc(av_ready, 1)
                    if live(s, 0):
                        after(pe, v_copied, s)
                        for k in range(KC):
                            product(nc, ps_v[:, 0:DIM], parts(lambda c: xt_hl[:, j % 2, c, k, :]),
                                    parts(lambda c: wqkv_hl[:, c, k, 2 * DIM:3 * DIM]), k == 0, False)
                        nc.tensor.matmul(ps_v[:, 0:DIM], ones3[:, :], bias3[:, 2 * DIM:3 * DIM], start=False, stop=True).then_inc(v_ready, 1)
                    if live(s, 1):
                        pe.wait_ge(qt_copied, s)
                        pe.wait_ge(kblk_done, s)
                        after(pe, sub_done, s - 1)
                        for w in range(2):
                            for c in range(KC):
                                t = nc.tensor.matmul(ps_sc[w * WTOK:(w + 1) * WTOK, :].rearrange("p (t c n) -> p t c n", t=4, c=KC)[:, :, c, :],
                                                     q_t[:, c, w * WTOK:(w + 1) * WTOK],
                                                     k_blk[:, c, w, :, :], start=True, stop=True)
                        t.then_inc(sc_ready, 1)
                    if live(s, 2):
                        pe.wait_ge(p_ready, s - 1)
                        after(pe, pt_copied, s - 2)
                        for c in range(4):
                            t = nc.tensor.transpose(ps_pt[:, c * P:(c + 1) * P], probs[:, j % 2, 2 * c:2 * c + 2, :], ident)
                        t.then_inc(pt_ready, 1)
                    if unit_done(s, j, 0):
                        pe.wait_ge(out0_copied, (u - 1) * UNIT + UNIT)
                        pe.wait_ge(out1_copied, (u - 1) * UNIT + UNIT)
                        project(u, 0)
                steps(pe, step)

            @block.vector
            def _(dve):
                BEHIND = 2 * UNIT

                def statistics(t):
                    nc.vector.bn_stats(raw[:, bass.ds(t * 6, 6)], h[:, bass.ds(t * DIM, DIM)])

                def step(s, j, u):
                    if live(s, 1):
                        dve.wait_ge(tq_ready, s)
                        dve.wait_ge(qt_copied, s)
                        after(dve, sc_ready, s - 1)
                        for c in range(KC):
                            kt = ps_tq[:, (2 + c) * P:(3 + c) * P].rearrange("p (w n) -> p w n", w=2)
                            mask = const[:, C_HEAD:C_HEAD + 4]
                            t = nc.vector.tensor_tensor(k_blk[:, c, :, :, :], kt.unsqueeze(2).to_broadcast([P, 2, 4, WTOK]),
                                                        mask.unsqueeze(1).unsqueeze(3).to_broadcast([P, 2, 4, WTOK]), ALU.mult)
                        t.then_inc(kblk_done, 1)
                    if live(s, 2):
                        dve.wait_ge(exp_done, s - 1)
                        nc.vector.tensor_reduce(ssum[:, :], probs[:, j % 2], AX_X, ALU.add).then_inc(sum_done, 1)
                        dve.wait_ge(sum_done, s - 1)
                        after(dve, p_ready, s - 2)
                        nc.vector.reciprocal(sinv[:, :], ssum[:, :]).then_inc(inv_done, 1)
                    if live(s, 0):
                        dve.wait_ge(qk_ready, s + 1)
                        after(dve, rope_added, s)
                        z = ps_qk[:, :].rearrange("p (a n) -> p a n", n=HD)
                        nc.vector.tensor_tensor(rope_c.rearrange("p (a n) -> p a n", n=HD), z,
                                                cos.unsqueeze(1).to_broadcast([P, 2 * HEADS, HD]), ALU.mult)
                        rs = rope_s.rearrange("p (a n) -> p a n", n=HD)
                        for e in range(2):
                            t = nc.vector.tensor_tensor(rs[:, :, e::2], z[:, :, 1 - e::2],
                                                        sin[:, e::2].unsqueeze(1).to_broadcast([P, 2 * HEADS, HD // 2]), ALU.mult)
                        t.then_inc(rope_done, 1)
                    if live(s, 3):
                        dve.wait_ge(av_ready, s - 2)
                        for q in range(4):
                            t = nc.vector.tensor_copy(
                                o_rows(q, 0, (j - 3) % UNIT),
                                o_head(ps_av0, q))
                        t.then_inc(out0_copied, 1)
                    if live(s, 1):
                        dve.wait_ge(sc_ready, s)
                        sc = ps_sc[:, :].rearrange("p (h n) -> p h n", h=HEADS)
                        nc.vector.tensor_reduce(smax[:, :], sc, AX_X, ALU.max).then_inc(max_done, 1)
                        dve.wait_ge(max_done, s)
                        after(dve, pt_ready, s - 2)
                        nc.vector.tensor_tensor(probs[:, (j - 1) % 2], sc, smax[:, :].unsqueeze(2).to_broadcast([P, HEADS, WTOK]),
                                                ALU.subtract).then_inc(sub_done, 1)
                    if not isinstance(s, int) or s >= BEHIND:
                        if j == BEHIND % UNIT:
                            dve.wait_ge(h_copied, (u - 1) * 2)
                        statistics(s - BEHIND)
                steps(dve, step)
                dve.wait_ge(h_copied, 2 * NUNIT)
                for t in range(LAST + 4 - BEHIND, LAST):
                    statistics(t)
                nc.vector.bn_stats(raw[:, CLS * 6:NT * 6], h[:, CLS * DIM:NT * DIM])

            @block.gpsimd
            def _(pool):
                def low_x(s, j, u):
                    pool.wait_ge(x_high, s + 1)
                    nc.gpsimd.tensor_tensor(xt_hl[:, j % 2, LO], xt[:, j], high(xt_hl[:, j % 2, HI]), ALU.subtract).then_inc(x_split, 1)

                def step(s, j, u):
                    if live(s, 2):
                        pool.wait_ge(inv_done, s - 1)
                        nc.gpsimd.tensor_tensor(probs[:, j % 2], probs[:, j % 2], sinv[:, :].unsqueeze(2).to_broadcast([P, HEADS, WTOK]),
                                                ALU.mult).then_inc(p_ready, 1)
                    if live(s, 0):
                        pool.wait_ge(rope_done, s + 1)
                        after(pool, tq_ready, s)
                        nc.gpsimd.tensor_tensor(qk_rot, rope_c, rope_s, ALU.add).then_inc(rope_added, 1)
                    next_x(s, j, u, low_x)
                low_x(0, 0, 0)
                split_steps(pool, step)
                for i in range(len(enc_w)):
                    pool.wait_ge(enc_high, i + 1)
                    nc.gpsimd.tensor_tensor(enc_hl[i][:, LO], enc_w[i][:, :, :], high(enc_hl[i][:, HI]), ALU.subtract)

            @block.scalar
            def _(act):
                def move_h(u, half):
                    act.wait_ge(proj_ready, (u - 1) * 2 + half + 1)
                    nc.scalar.activation(h[:, bass.ds(((u - 1) * 2 + half) * 2 * DIM, 2 * DIM)], ps_proj[:, :], ACT.Copy).then_inc(h_copied, 1)

                def high_x(s, j, u):
                    act.wait_ge(x_loaded[j], u * 16 + 16)
                    after(act, v_ready, s - 1)
                    nc.scalar.activation(xt_hl[:, j % 2, HI], xt[:, j], ACT.Copy).then_inc(x_high, 1)

                def step(s, j, u):
                    if live(s, 1):
                        act.wait_ge(tq_ready, s)
                        after(act, sc_ready, s - 1)
                        nc.scalar.activation(q_t[:, :, :], ps_tq[:, 0:2 * P].rearrange("p (k n) -> p k n", k=KC), ACT.Copy).then_inc(qt_copied, 1)
                    if live(s, 2):
                        act.wait_ge(sub_done, s - 1)
                        nc.scalar.activation(probs[:, j % 2], probs[:, j % 2], ACT.Exp, scale=SCALE).then_inc(exp_done, 1)
                    next_x(s, j, u, high_x)
                    if unit_done(s, j, 1):
                        move_h(u, 1)
                    if live(s, 3):
                        act.wait_ge(av_ready, s - 2)
                        for q in range(4):
                            t = nc.scalar.activation(
                                o_rows(q, 1, (j - 3) % UNIT),
                                o_head(ps_av1, q), ACT.Copy)
                        t.then_inc(out1_copied, 1)
                    if live(s, 0):
                        act.wait_ge(v_ready, s + 1)
                        after(act, av_ready, s - 3)
                        for c in range(KC):
                            for w in range(2):
                                t = nc.scalar.activation(v_half[c * WTOK:(c + 1) * WTOK, j, w, :],
                                                         ps_v[w * WTOK:(w + 1) * WTOK, c * P:(c + 1) * P], ACT.Copy)
                        t.then_inc(v_copied, 1)
                    if live(s, 2):
                        act.wait_ge(pt_ready, s - 1)
                        after(act, av_ready, s - 2)
                        nc.scalar.activation(p_t[:, :, :, :], ps_pt[:, :].rearrange("p (c w n) -> p c w n", c=4, w=2), ACT.Copy).then_inc(pt_copied, 1)
                    if unit_done(s, j, 0):
                        move_h(u, 0)
                    if isinstance(s, int) and s == UNIT - 1:
                        act.wait_ge(enc_loaded, len(enc_w) * 16)
                        for part, w in zip(enc_hl, enc_w):
                            nc.scalar.activation(part[:, HI], w, ACT.Copy).then_inc(enc_high, 1)
                high_x(0, 0, 0)
                split_steps(act, step)


NHID = 7
PLANES, SETS = 16, 4
JOINT = PLANES // SETS
NPH = 2 * (JOINT + PLANES) + PLANES
COL_K, COL_Q, COL_L, COL_G = 0, JOINT + PLANES, 2 * (JOINT + PLANES), NPH
NCOL = NPH + 1
KF = 2 * (JOINT + PLANES)
PF = 2 * PLANES
LT = P - PF
MAGIC = 1.5 * 2.0 ** 23
PI = float(np.float32(np.pi))


def normaliser(nc, g, block_name):
    with ExitStack() as ctx:
        sb = lambda name, shape, dt=F32: ctx.enter_context(nc.sbuf_tensor(name + block_name, shape, dt))
        sem = lambda name: ctx.enter_context(nc.semaphore(name + block_name))
        raw, mean, rstd = g["raw"], g["mean"], g["rstd"]
        view = raw[:, :].rearrange("p (t f) -> p t f", f=6)
        dif, var = sb("dif", [P, NT]), sb("var", [P, NT])
        step_done, var_ready, std_ready = sem("ln_step_done"), sem("var_ready"), sem("std_ready")
        with nc.Block() as block:
            @block.vector
            def _(dve):
                nc.vector.tensor_tensor(mean[:, :], view[:, :, 1], view[:, :, 4], ALU.add)
                nc.vector.tensor_tensor(dif[:, :], view[:, :, 1], view[:, :, 4], ALU.subtract)
                nc.vector.tensor_tensor(var[:, :], view[:, :, 2], view[:, :, 5], ALU.add).then_inc(step_done, 1)
                dve.wait_ge(step_done, 1)
                nc.vector.tensor_scalar(mean[:, :], mean[:, :], 0.5, None, ALU.mult)
                nc.vector.tensor_tensor(dif[:, :], dif[:, :], dif[:, :], ALU.mult)
                nc.vector.tensor_scalar(var[:, :], var[:, :], 1.0 / DIM, EPS, ALU.mult, ALU.add).then_inc(step_done, 1)
                dve.wait_ge(step_done, 2)
                nc.vector.scalar_tensor_tensor(out=var[:, :], in0=dif[:, :], scalar=0.25, in1=var[:, :],
                                               op0=ALU.mult, op1=ALU.add).then_inc(var_ready, 1)
                dve.wait_ge(std_ready, 1)
                nc.vector.reciprocal(rstd[:, :], var[:, :])

            @block.scalar
            def _(act):
                act.wait_ge(var_ready, 1)
                nc.scalar.activation(var[:, :], var[:, :], ACT.Sqrt).then_inc(std_ready, 1)


def encoders(nc, g, a):
    with ExitStack() as ctx:
        sb = lambda name, shape, dt=F32: ctx.enter_context(nc.sbuf_tensor(name, shape, dt))
        sem = lambda name: ctx.enter_context(nc.semaphore(name))
        EU, RING, BUF = 2, 4, 3
        SPLIT = NHID - 1
        UNITS, ETOK = NPAIR // EU, EU * P
        w1, wv, w2 = g["enc_w1"], g["enc_wv"], g["enc_w2"]
        b1 = sb("enc_b1", [P, NHID])
        b2 = sb("enc_b2", [NCOL, 2])
        xn = sb("xn", [P, EU, DIM])
        xn_t = sb("xn_t", [P, 2, KC, ETOK], F32R)
        hid = sb("hid", [P, BUF, ETOK])
        hid_hl = sb("hid_hl", [P, 2, SPLIT, ETOK], F32R)
        ph_t = sb("ph_t", [P, ETOK])
        b_loaded, b2_ready = sem("enc_b_loaded"), sem("b2_ready")
        xn_ready, xt_ready, xt_high, xt_split = sem("xn_ready"), sem("xt_ready"), sem("xt_high"), sem("xt_split")
        hid_ready, gelu_done, hid_high, hid_split = sem("hid_ready"), sem("gelu_done"), sem("hid_high"), sem("hid_split")
        v_ready, v_copied = sem("ev_ready"), sem("ev_copied")
        l2_begun = sem("l2_begun")
        l2_ready, tanh_done, pht_ready, ph_copied = sem("l2_ready"), sem("tanh_done"), sem("pht_ready"), sem("ph_copied")
        ps_t, ps_v, ps_l2, ps_ph = g["bank"][0:4]
        ring = g["bank"][4:8]
        h, V, th, mean, rstd, ident = g["h"], g["V"], g["th"], g["mean"], g["rstd"], g["const"][:, C_ID:C_ID + P]
        ones3, bias3 = g["ones3"], g["bias3"]
        is_cls = lambda u: isinstance(u, int) and u == UNITS
        first = lambda u: isinstance(u, int) and u == 0
        tiles = lambda u: 1 if is_cls(u) else EU

        def tokens(u, ap):
            return ap[:, :].rearrange("p (k n) -> p k n", k=KC)[:, :, 0:tiles(u) * P]

        def order(eng, unit):
            unit(0)
            with eng.Fori(1, UNITS - 1) as u:
                unit(u)
            unit(UNITS - 1)
            unit(UNITS)

        with nc.Block() as block:
            @block.sync
            def _(sp):
                for dst, src in ((b1[:, :], a["enc_b1"]), (b2[:, :], a["enc_b2"])):
                    sp.dma_start(dst, src).then_inc(b_loaded, 16)

            @block.vector
            def _(dve):
                nc.vector.memset(ph_t[:, :], 0.0).then_inc(b2_ready, 1)

                def normalise(u):
                    after(dve, xt_ready, u)
                    for i in range(tiles(u)):
                        t = u * EU + i
                        n = nc.vector.tensor_scalar(xn[:, i, :], h[:, bass.ds(t * DIM, DIM)], mean[:, bass.ds(t, 1)],
                                                    rstd[:, bass.ds(t, 1)], ALU.subtract, ALU.mult)
                    n.then_inc(xn_ready, 1)

                def low_xt(u):
                    dve.wait_ge(xt_high, u + 1)
                    n = tiles(u) * P
                    nc.vector.tensor_tensor(xn_t[:, LO, :, 0:n], tokens(u, ps_t), high(xn_t[:, HI, :, 0:n]), ALU.subtract).then_inc(xt_split, 1)

                def low_hid(u, chunks):
                    n = tiles(u) * P
                    for c in chunks:
                        dve.wait_ge(hid_high, u * NHID + c + 1)
                        nc.vector.tensor_tensor(hid_hl[:, LO, c % SPLIT, 0:n], hid[:, c % BUF, 0:n], high(hid_hl[:, HI, c % SPLIT, 0:n]),
                                                ALU.subtract).then_inc(hid_split, 1)

                def move_phases(u):
                    dve.wait_ge(pht_ready, u + 1)
                    m = tiles(u)
                    nc.vector.tensor_copy(th[:, bass.ds(u * EU * NCOL, m * NCOL)].rearrange("p (i n) -> p i n", n=NCOL),
                                          ps_ph[:, 0:m * P].rearrange("p (i n) -> p i n", n=P)[:, :, 0:NCOL]).then_inc(ph_copied, 1)

                def unit(u):
                    if first(u):
                        normalise(u)
                        dve.wait_ge(b_loaded, 2 * 16)
                        nc.vector.tensor_scalar(b2[:, 0:1], b2[:, 0:1], b2[:, 1:2], None, ALU.mult).then_inc(b2_ready, 1)
                        low_xt(u)
                    low_hid(u, range(NHID // 2))
                    if not is_cls(u):
                        normalise(u + 1)
                    low_hid(u, range(NHID // 2, NHID))
                    if not is_cls(u):
                        low_xt(u + 1)
                    if not first(u):
                        move_phases(u - 1)
                    dve.wait_ge(v_ready, u + 1)
                    n = tiles(u) * DIM
                    nc.vector.tensor_copy(V[:, bass.ds(u * EU * DIM, n)], ps_v[:, 0:n]).then_inc(v_copied, 1)
                order(dve, unit)
                move_phases(UNITS)

            @block.scalar
            def _(act):
                def high_xt(u):
                    act.wait_ge(xt_ready, u + 1)
                    after(act, v_ready, u)
                    n = tiles(u) * P
                    nc.scalar.activation(xn_t[:, HI, :, 0:n], tokens(u, ps_t), ACT.Copy).then_inc(xt_high, 1)

                def high_hid(u, c):
                    n = tiles(u) * P
                    act.wait_ge(gelu_done, u * NHID + c + 1)
                    if c == SPLIT:
                        act.wait_ge(l2_begun, u + 1)
                    nc.scalar.activation(hid_hl[:, HI, c % SPLIT, 0:n], hid[:, c % BUF, 0:n], ACT.Copy).then_inc(hid_high, 1)

                def tanh(u):
                    n = tiles(u) * P
                    act.wait_ge(l2_ready, u + 1)
                    after(act, pht_ready, u)
                    nc.scalar.activation(ph_t[0:NCOL, 0:n], ps_l2[0:NCOL, 0:n], ACT.Tanh, bias=b2[:, 0:1], scale=b2[:, 1:2]).then_inc(tanh_done, 1)

                def unit(u):
                    n = tiles(u) * P
                    for c in range(NHID):
                        act.wait_ge(hid_ready, u * NHID + c + 1)
                        if c >= BUF:
                            act.wait_ge(hid_split, u * NHID + c + 1 - BUF)
                        elif c == 0:
                            after(act, hid_split, u * NHID)
                        nc.scalar.activation(hid[:, c % BUF, 0:n], ring[c % RING][:, 0:n], ACT.Gelu, bias=b1[:, c:c + 1]).then_inc(gelu_done, 1)
                        if c == 0 and not first(u):
                            tanh(u - 1)
                        if c:
                            high_hid(u, c - 1)
                    high_hid(u, NHID - 1)
                    if not is_cls(u):
                        high_xt(u + 1)
                act.wait_ge(b_loaded, 2 * 16)
                act.wait_ge(b2_ready, 2)
                high_xt(0)
                order(act, unit)
                tanh(UNITS)

            @block.tensor
            def _(pe):
                def turn(u):
                    pe.wait_ge(xn_ready, u + 1)
                    after(pe, xt_split, u)
                    for k in range(KC):
                        for i in range(tiles(u)):
                            t = nc.tensor.transpose(ps_t[:, (k * EU + i) * P:(k * EU + i + 1) * P], xn[:, i, k * P:(k + 1) * P], ident)
                    t.then_inc(xt_ready, 1)

                def turn_phases(u):
                    pe.wait_ge(tanh_done, u + 1)
                    after(pe, ph_copied, u)
                    for i in range(tiles(u)):
                        t = nc.tensor.transpose(ps_ph[:, i * P:(i + 1) * P], ph_t[:, i * P:(i + 1) * P], ident)
                    t.then_inc(pht_ready, 1)

                def unit(u):
                    n = tiles(u) * P
                    pe.wait_ge(xt_split, u + 1)

                    def second(c):
                        pe.wait_ge(hid_split, u * NHID + c + 1)
                        return product(nc, ps_l2[0:NCOL, 0:n], parts(lambda e: w2[:, e, c, :]), parts(lambda e: hid_hl[:, e, c % SPLIT, 0:n]),
                                       c == 0, c == NHID - 1)
                    for c in range(NHID):
                        if c == SPLIT:
                            after(pe, tanh_done, u)
                            second(0).then_inc(l2_begun, 1)
                        if c >= RING:
                            pe.wait_ge(gelu_done, u * NHID + c + 1 - RING)
                        for k in range(KC):
                            t = product(nc, ring[c % RING][:, 0:n], parts(lambda e: w1[:, e, k, c * P:(c + 1) * P]),
                                        parts(lambda e: xn_t[:, e, k, 0:n]), k == 0, k == KC - 1)
                        t.then_inc(hid_ready, 1)
                    if not is_cls(u):
                        turn(u + 1)
                    if not first(u):
                        turn_phases(u - 1)
                    after(pe, v_copied, u)
                    for i in range(tiles(u)):
                        v = ps_v[:, i * DIM:(i + 1) * DIM]
                        for k in range(KC):
                            product(nc, v, parts(lambda e: xn_t[:, e, k, i * P:(i + 1) * P]), parts(lambda e: wv[:, e, k, :]), k == 0, False)
                        t = nc.tensor.matmul(v, ones3[:, :], bias3[:, 4 * DIM:5 * DIM], start=False, stop=True)
                    t.then_inc(v_ready, 1)
                    for c in range(1, NHID):
                        t = second(c)
                    t.then_inc(l2_ready, 1)
                turn(0)
                order(pe, unit)
                turn_phases(UNITS)


PI_IN = 3.1415925
TWO_PI = float(np.float32(2 * np.pi))
TP1 = 6.28125
TP2 = 253 / 2.0 ** 17
TP3 = float(np.float32(2 * np.pi - TP1 - TP2))
(S_SETW, S_POSW, S_SSCALE, S_SBIAS, S_RSCALE, S_RTHR, S_LTMW, S_COUNT, S_FREQ, NSCAL) = (0, 4, 5, 6, 7, 8, 9, 10, 11, 27)
NBIAS = 7 * DIM


def prologue(nc, g, a):
    with ExitStack() as ctx:
        sb = lambda name, shape, dt=F32: ctx.enter_context(nc.sbuf_tensor(name, shape, dt))
        sem = lambda name: ctx.enter_context(nc.semaphore(name))
        NVEC, OUT_B = NBIAS // DIM, 5
        row = sb("bias_row", [NVEC, DIM])
        parts = sb("bias_parts", [NVEC, 3, DIM], BF16)
        shifts = sb("shifts", [P, KC, NVEC])
        t = sb("pro_t", [P, 16])
        ph, turns = sb("pos_phase", [P, TPB * PLANES]), sb("pos_turns", [P, TPB * PLANES])
        posn = sb("pos_n", [P, TPB])
        zero = sb("pro_zero", [P, 1])
        lnb, lng = sb("lnb", [P, KC]), sb("lng", [P, KC])
        ltm = sb("ltm_rows", [P, DIM])
        loaded, bias_sent, step_done, act_done = sem("pro_loaded"), sem("bias_sent"), sem("pro_step_done"), sem("pro_act_done")
        scal_loaded, shifts_ready, w_loaded, w_high = sem("scal_loaded"), sem("shifts_ready"), sem("w_loaded"), sem("w_high")
        shift_ready, wout_loaded, ltm_loaded = sem("shift_ready"), sem("wout_loaded"), sem("ltm_loaded")
        const, scal, sc, wout, st, post, rpos = g["const"], g["scal"], g["sc"], g["wout"], g["st"], g["post"], g["rpos"]
        bias_ready, arguments_ready = sem("bias_ready"), sem("arguments_ready")
        ps = g["bank"][0]
        with nc.Block() as block:
            @block.sync
            def _(sp):
                sp.dma_start(scal[:, :], a["scal"].to_broadcast([P, NSCAL])).then_inc(scal_loaded, 16)
                sp.dma_start(const[:, :], a["const"]).then_inc(scal_loaded, 16)
                sp.dma_start(row[:, :], a["bias"]).then_inc(loaded, 16)
                sp.dma_start(g["h"][:, CLS * DIM:NT * DIM], a["cls"].to_broadcast([P, DIM])).then_inc(loaded, 16)
                sp.dma_start(wout[:, :, :], a["out_w"].rearrange("(k p) n -> p k n", p=P)).then_inc(wout_loaded, 16)
                sp.dma_start(lng[:, :], a["ln_g"]).then_inc(wout_loaded, 16)
                sp.dma_start(lnb[:, :], a["ln_b"]).then_inc(wout_loaded, 16)
                sp.dma_start(g["wqkv"], a["qkv_w"].rearrange("(k p) n -> p k n", p=P)).then_inc(w_loaded, 16)
                sp.dma_start(ltm[LT:P, :], a["ltm"]).then_inc(ltm_loaded, 16)
                sp.dma_start(g["wproj"], a["proj_w"].rearrange("(k p) n -> p k n", p=P)).then_inc(w_loaded, 16)
                for j in range(UNIT):
                    sp.dma_start(g["xt"][:, j], a["x_t"][:, 0:1, j * P:(j + 1) * P].rearrange("(k p) a n -> p k (a n)", p=P)).then_inc(g["x_loaded"][j], 16)
                sp.wait_ge(bias_ready, 1)
                for e in range(3):
                    sp.dma_start(g["bias3"][e:e + 1, :], parts[:, e, :]).then_inc(bias_sent, 16)
                sp.wait_ge(bias_sent, 3 * 16)

            @block.tensor
            def _(pe):
                pe.wait_ge(shifts_ready, 2)
                pe.wait_ge(loaded, 32)
                for k in range(KC):
                    m = nc.tensor.matmul(ps[0:NVEC, 0:DIM], shifts[:, k, :], wout[:, k, :], start=(k == 0), stop=(k == KC - 1))
                m.then_inc(shift_ready, 1)

            @block.vector
            def _(dve):
                count = [0]

                def done(ins):
                    count[0] += 1
                    ins.then_inc(step_done, 1)
                    dve.wait_ge(step_done, count[0])

                V = nc.vector
                V.memset(shifts[:, :, :], 0.0).then_inc(shifts_ready, 1)
                V.memset(g["ones3"][:, :], 1.0)
                V.memset(g["half_pi"][:, :], float(np.float32(np.pi / 2)))
                V.memset(g["eps"][:, :], EPS)
                V.memset(st[:, :, :], 0.0)
                dve.wait_ge(scal_loaded, 32)
                p3 = ph[:, :].rearrange("p (t f) -> p t f", f=PLANES)
                done(V.tensor_tensor(p3, const[:, C_POS:C_POS + TPB].unsqueeze(2).to_broadcast([P, TPB, PLANES]),
                                     scal[:, S_FREQ:S_FREQ + PLANES].unsqueeze(1).to_broadcast([P, TPB, PLANES]), ALU.mult))
                done(V.tensor_scalar(ph[:, :], ph[:, :], TWO_PI, None, ALU.mult))
                done(V.tensor_scalar(turns[:, :], ph[:, :], float(np.float32(1 / (2 * np.pi))), MAGIC, ALU.mult, ALU.add))
                done(V.tensor_scalar(turns[:, :], turns[:, :], MAGIC, None, ALU.subtract))
                for part in (TP1, TP2, TP3):
                    done(V.scalar_tensor_tensor(out=ph[:, :], in0=turns[:, :], scalar=-part, in1=ph[:, :], op0=ALU.mult, op1=ALU.add))
                done(V.tensor_scalar(ph[:, :], ph[:, :], PI_IN, -PI_IN, ALU.min, ALU.max))
                done(V.scalar_tensor_tensor(out=turns[:, :], in0=ph[:, :], scalar=-1.0, in1=ph[:, :], op0=ALU.mult, op1=ALU.max))
                done(V.tensor_reduce(t[:, 0:1], scal[:, S_SETW:S_SETW + SETS], AX_X, ALU.max))
                done(V.tensor_scalar(sc["setw"], scal[:, S_SETW:S_SETW + SETS], t[:, 0:1], None, ALU.subtract))
                V.tensor_scalar(sc["posw"], scal[:, S_POSW:S_POSW + 1], 0.5, None, ALU.mult)
                V.tensor_scalar(sc["rscale"], scal[:, S_RSCALE:S_RSCALE + 1], 1.0, 20.0, ALU.max, ALU.min)
                V.tensor_scalar(sc["rthr"], scal[:, S_RTHR:S_RTHR + 1], 0.1, 0.9, ALU.max, ALU.min)
                V.tensor_scalar(sc["count"], scal[:, S_COUNT:S_COUNT + 1], 1.0, float(PLANES), ALU.max, ALU.mult)
                V.tensor_scalar(posn[:, :], const[:, C_POS:C_POS + TPB], 1.0, None, ALU.max)
                done(V.tensor_scalar(sc["ltmw"], scal[:, S_LTMW:S_LTMW + 1], 0.5, None, ALU.mult))
                done(V.tensor_tensor(sc["nthr"], sc["rscale"], sc["rthr"], ALU.mult))
                V.tensor_scalar(sc["nthr"], sc["nthr"], -1.0, None, ALU.mult).then_inc(arguments_ready, 1)
                dve.wait_ge(wout_loaded, 48)
                dve.wait_ge(shifts_ready, 1)
                V.tensor_copy(shifts[:, :, OUT_B], lnb[:, :]).then_inc(shifts_ready, 1)
                dve.wait_ge(loaded, 32)
                dve.wait_ge(shift_ready, 1)
                done(V.tensor_tensor(row[:, :], row[:, :], ps[0:NVEC, 0:DIM], ALU.add))
                for k in range(KC):
                    V.tensor_scalar(wout[:, k, :], wout[:, k, :], lng[:, k:k + 1], None, ALU.mult)
                for i in range(3):
                    done(V.tensor_copy(parts[:, i, :], row[:, :]))
                    if i < 2:
                        done(V.tensor_tensor(row[:, :], row[:, :], parts[:, i, :], ALU.subtract))
                V.memset(zero[:, :], 0.0).then_inc(bias_ready, 1)
                dve.wait_ge(act_done, 7)
                done(V.reciprocal(t[:, 1:2], t[:, 1:2]))
                V.tensor_scalar(sc["setw"], sc["setw"], t[:, 1:2], None, ALU.mult)
                V.tensor_scalar(sc["posw"], sc["posw"], 0.5, 0.5, ALU.mult, ALU.add)
                V.tensor_scalar(sc["ltmw"], sc["ltmw"], 0.5, 0.5, ALU.mult, ALU.add)
                V.reciprocal(rpos[:, :], posn[:, :])
                done(V.reciprocal(sc["count"], sc["count"]))
                done(V.tensor_tensor(t[:, 2:3], sc["ltmw"], sc["count"], ALU.mult))
                dve.wait_ge(ltm_loaded, 16)
                for i in range(2):
                    V.tensor_scalar(st[LT:P, i, :], ltm[LT:P, :], t[LT:P, 2:3], None, ALU.mult)
                V.memset(sc["wtab"], 1.0).then_inc(step_done, 1)
                count[0] += 1
                dve.wait_ge(step_done, count[0])
                V.tensor_copy(sc["wtab"][:, JOINT:].rearrange("p (s j) -> p s j", s=SETS),
                              sc["setw"].unsqueeze(2).to_broadcast([P, SETS, JOINT]))
                V.memset(post[:, TPB, 0, :], 1.0)
                V.memset(post[:, TPB, 1, :], 0.0)
            @block.gpsimd
            def _(pool):
                pool.wait_ge(w_high, 1)
                nc.gpsimd.tensor_tensor(g["wqkv_hl"][:, LO], g["wqkv"], high(g["wqkv_hl"][:, HI]), ALU.subtract)

            @block.scalar
            def _(act):
                act.wait_ge(w_loaded, 32)
                nc.scalar.activation(g["wqkv_hl"][:, HI], g["wqkv"], ACT.Copy).then_inc(w_high, 1)
                act.wait_ge(arguments_ready, 1)
                p3 = ph[:, :].rearrange("p (t f) -> p t f", f=PLANES)
                n3 = turns[:, :].rearrange("p (t f) -> p t f", f=PLANES)
                nc.scalar.activation(sc["setw"], sc["setw"], ACT.Exp, accum_out=t[:, 1:2]).then_inc(act_done, 1)
                nc.scalar.activation(sc["posw"], sc["posw"], ACT.Tanh).then_inc(act_done, 1)
                nc.scalar.activation(sc["ltmw"], sc["ltmw"], ACT.Tanh).then_inc(act_done, 1)
                nc.scalar.activation(post[:, 0:TPB, 1, :], p3, ACT.Sin).then_inc(act_done, 1)
                nc.scalar.activation(post[:, 0:TPB, 0, :], n3, ACT.Sin, bias=g["half_pi"][:, :], scale=-1.0).then_inc(act_done, 1)
                nc.scalar.activation(posn[:, :], posn[:, :], ACT.Sqrt).then_inc(act_done, 1)
                nc.scalar.activation(sc["count"], sc["count"], ACT.Sqrt).then_inc(act_done, 1)


def phasors(nc, g):
    with ExitStack() as ctx:
        sb = lambda name, shape, dt=F32: ctx.enter_context(nc.sbuf_tensor(name, shape, dt))
        sem = lambda name: ctx.enter_context(nc.semaphore(name))
        th, trig, wg, gg, sc, const, rpos = g["th"], g["trig"], g["wg"], g["gg"], g["sc"], g["const"], g["rpos"]
        t3 = th[:, :].rearrange("p (t n) -> p t n", n=NCOL)
        NJ = B * 2 * JOINT * TPB
        turn = sb("turn", [P, NT, 2, JOINT])
        part = [sb(f"part{i}", [P, NT, 2, JOINT]) for i in range(2)]
        tot, km = sb("tot", [P, NJ]), sb("km", [P, NJ])
        pr = [x[:, :, :, :].rearrange("p t q j -> p (t q j)")[:, i * NJ // 2:(i + 1) * NJ // 2]
              .rearrange("p (b f t) -> p b f t", b=B, f=JOINT) for x in (turn, part[1]) for i in range(2)]
        mag = sb("mag", [P, NT])
        joint_ready, abs_done, trig_ready = sem("joint_ready"), sem("abs_done"), sem("trig_ready")
        step_done, sums_ready, square_ready, root_ready = sem("ph_step_done"), sem("sums_ready"), sem("square_ready"), sem("root_ready")
        arg_ready, surprise_ready, arg2_ready, gate_ready = sem("arg_ready"), sem("surprise_ready"), sem("arg2_ready"), sem("gate_ready")
        ps_pre, ps_tot = g["bank"][0:2]
        with nc.Block() as block:
            @block.vector
            def _(dve):
                count = [0]
                V = nc.vector

                def done(ins):
                    count[0] += 1
                    ins.then_inc(step_done, 1)
                    dve.wait_ge(step_done, count[0])

                def sets(c, s):
                    return t3[:, :, c + JOINT + s * JOINT:c + JOINT + (s + 1) * JOINT]
                for q, c in enumerate((COL_K, COL_Q)):
                    V.tensor_tensor(part[0][:, :, q, :], sets(c, 0), sets(c, 1), ALU.add)
                    V.tensor_tensor(part[1][:, :, q, :], sets(c, 2), sets(c, 3), ALU.add)
                done(V.memset(mag[:, CLS:NT], 0.0))
                done(V.tensor_tensor(part[0][:, :, :, :], part[0][:, :, :, :], part[1][:, :, :, :], ALU.add))
                done(V.tensor_scalar(turn[:, :, :, :], part[0][:, :, :, :], 0.5, MAGIC, ALU.mult, ALU.add))
                done(V.tensor_scalar(turn[:, :, :, :], turn[:, :, :, :], MAGIC, None, ALU.subtract))
                for q, c in enumerate((COL_K, COL_Q)):
                    n = V.scalar_tensor_tensor(out=t3[:, :, c:c + JOINT], in0=turn[:, :, q, :], scalar=-2.0,
                                               in1=part[0][:, :, q, :], op0=ALU.mult, op1=ALU.add)
                n.then_inc(joint_ready, 1)
                V.tensor_scalar(gg[:, 0, :], t3[:, :, COL_G], 0.1, 0.1, ALU.mult, ALU.add)
                done(V.tensor_scalar(gg[:, 1, :], t3[:, :, COL_G], -0.5, 0.5, ALU.mult, ALU.add))
                V.tensor_scalar(gg[:, 1, :], gg[:, 1, :], sc["posw"], None, ALU.mult)
                dve.wait_ge(joint_ready, 1)
                V.scalar_tensor_tensor(out=trig[:, :, 0, :], in0=t3[:, :, 0:NPH], scalar=-1.0, in1=t3[:, :, 0:NPH],
                                       op0=ALU.mult, op1=ALU.max).then_inc(abs_done, 1)
                V.memset(g["kq"][:, :, :, :], 0.0)
                dve.wait_ge(sums_ready, 1)
                half = 2 * JOINT * TPB
                for b in range(B):
                    n = V.tensor_tensor_scan(tot[:, b * half:(b + 1) * half], const[:, C_SEG:C_SEG + half],
                                             ps_tot[:, b * half:(b + 1) * half], 0.0, ALU.mult, ALU.add)
                done(n)
                done(V.tensor_tensor(tot[:, :], tot[:, :], ps_tot[:, :], ALU.subtract))
                done(V.tensor_tensor(km[:, :], tot[:, :], ps_pre[:, :], ALU.add))
                k5 = km[:, :].rearrange("p (b c f t) -> p b c f t", b=B, c=2, f=JOINT)
                for b in range(B):
                    n = V.tensor_tensor(k5[:, b].rearrange("p c f t -> p (c f) t"), k5[:, b].rearrange("p c f t -> p (c f) t"),
                                        g["jcls"][:, :].unsqueeze(2).to_broadcast([P, 2 * JOINT, TPB]), ALU.add)
                done(n)
                jq = [trig[:, 0:NPAIR, c, COL_Q:COL_Q + JOINT].rearrange("p (b t) f -> p b f t", b=B) for c in range(2)]
                V.tensor_tensor(pr[0][:, :, :, :], k5[:, :, 0], jq[0], ALU.mult)
                V.tensor_tensor(pr[1][:, :, :, :], k5[:, :, 1], jq[1], ALU.mult)
                V.tensor_tensor(pr[2][:, :, :, :], k5[:, :, 1], jq[0], ALU.mult)
                done(V.tensor_tensor(pr[3][:, :, :, :], k5[:, :, 0], jq[1], ALU.mult))
                V.tensor_tensor(pr[0][:, :, :, :], pr[0][:, :, :, :], pr[1][:, :, :, :], ALU.add)
                done(V.tensor_tensor(pr[2][:, :, :, :], pr[2][:, :, :, :], pr[3][:, :, :, :], ALU.subtract))
                V.tensor_tensor(pr[0][:, :, :, :], pr[0][:, :, :, :], pr[0][:, :, :, :], ALU.mult)
                done(V.tensor_tensor(pr[2][:, :, :, :], pr[2][:, :, :, :], pr[2][:, :, :, :], ALU.mult))
                V.tensor_tensor(pr[0][:, :, :, :], pr[0][:, :, :, :], pr[2][:, :, :, :], ALU.add).then_inc(square_ready, 1)
                dve.wait_ge(root_ready, 1)
                done(V.tensor_reduce(mag[:, 0:NPAIR].rearrange("p (b t) -> p b t", b=B),
                                     pr[1][:, :, :, :].rearrange("p b f t -> p b t f"), AX_X, ALU.add))
                m3 = mag[:, 0:NPAIR].rearrange("p (b t) -> p b t", b=B)
                done(V.scalar_tensor_tensor(out=m3, in0=m3, scalar=1.0 / JOINT, in1=rpos[:, :].unsqueeze(1).to_broadcast([P, B, TPB]),
                                            op0=ALU.mult, op1=ALU.mult))
                V.tensor_scalar(mag[:, :], mag[:, :], sc["rscale"], sc["nthr"], ALU.mult, ALU.add).then_inc(arg_ready, 1)
                dve.wait_ge(surprise_ready, 1)
                done(V.tensor_scalar(mag[:, :], mag[:, :], -0.5, g["scal"][:, S_SSCALE:S_SSCALE + 1], ALU.mult, ALU.mult))
                V.tensor_scalar(mag[:, :], mag[:, :], g["scal"][:, S_SBIAS:S_SBIAS + 1], 0.5, ALU.add, ALU.mult).then_inc(arg2_ready, 1)
                dve.wait_ge(gate_ready, 1)
                V.tensor_scalar(wg[:, :], mag[:, :], 0.5, 0.5, ALU.mult, ALU.add)

            @block.scalar
            def _(act):
                act.wait_ge(joint_ready, 1)
                nc.scalar.activation(trig[:, :, 1, :], t3[:, :, 0:NPH], ACT.Sin, scale=PI_IN)
                act.wait_ge(abs_done, 1)
                nc.scalar.activation(trig[:, :, 0, :], trig[:, :, 0, :], ACT.Sin, bias=g["half_pi"][:, :], scale=-PI).then_inc(trig_ready, 1)
                act.wait_ge(trig_ready, 1)
                nc.scalar.activation(g["jcls"][:, :].rearrange("p (c f) -> p c f", c=2), trig[:, CLS, :, 0:JOINT], ACT.Copy).then_inc(trig_ready, 1)
                act.wait_ge(square_ready, 1)
                nc.scalar.activation(pr[1][:, :, :, :], pr[0][:, :, :, :], ACT.Sqrt).then_inc(root_ready, 1)
                act.wait_ge(arg_ready, 1)
                nc.scalar.activation(mag[:, :], mag[:, :], ACT.Tanh).then_inc(surprise_ready, 1)
                act.wait_ge(arg2_ready, 1)
                nc.scalar.activation(mag[:, :], mag[:, :], ACT.Tanh).then_inc(gate_ready, 1)

            @block.tensor
            def _(pe):
                pe.wait_ge(trig_ready, 2)
                for b in range(B):
                    for c in range(2):
                        keys = trig[:, b * TPB:(b + 1) * TPB, c, COL_K:COL_K + JOINT].rearrange("p t f -> p f t")
                        at = (b * 2 + c) * JOINT * TPB
                        for dst, col in ((ps_pre, C_STRICT), (ps_tot, C_ONES)):
                            n = nc.tensor.matmul(dst[:, at:at + JOINT * TPB], const[:, col:col + P], keys, start=True, stop=True)
                n.then_inc(sums_ready, 1)


def retrieval(nc, g, a):
    with ExitStack() as ctx:
        sb = lambda name, shape, dt=F32: ctx.enter_context(nc.sbuf_tensor(name, shape, dt))
        sem = lambda name: ctx.enter_context(nc.semaphore(name))
        kq, st, post, trig, V, h, raw = g["kq"], g["st"], g["post"], g["trig"], g["V"], g["h"], g["raw"]
        wg, gg, sc, const, wout, ones3, bias3 = g["wg"], g["gg"], g["sc"], g["const"], g["wout"], g["ones3"], g["bias3"]
        ident = const[:, C_ID:C_ID + P]
        kq_t = sb("kq_t", [P, 2, 2, P])
        kcls, vcls = sb("kcls", [1, P]), sb("vcls", [1, DIM])
        masked = sb("masked", [P, 2, P])
        ln_raw, ln_agg, ln_std, ln_rstd = sb("ln_raw", [P, 2, 6]), sb("ln_agg", [P, 2, 2]), sb("ln_std", [P, 2]), sb("ln_rstd", [P, 2])
        wr, prod = sb("t_wr", [P, DIM]), sb("t_prod", [P, DIM])
        mean, tok_w = g["mean"], g["tok_w"]
        wr_loaded, stats_done, mean_done, weighed = sem("t_wr_loaded"), sem("stats_done"), sem("mean_done"), sem("weighed")
        y, y_t = sb("y", [P, 2, DIM]), sb("y_t", [P, 2, KC, P])
        kq_ready, kqt_ready, kqt_copied, query_scaled = sem("kq_ready"), sem("kqt_ready"), sem("kqt_copied"), sem("query_scaled")
        s_ready, masked_ready, o_ready, state_ready, state_copied = sem("s_ready"), sem("masked_ready"), sem("o_ready"), sem("state_ready"), sem("state_copied")
        raw_done, agg_done, std_done, rstd_done, y_ready = sem("raw_done"), sem("agg_done"), sem("std_done"), sem("rstd_done"), sem("y_ready")
        yt_ready, yt_copied, w_ready, h_done, cls_kept = sem("yt_ready"), sem("yt_copied"), sem("w_ready"), sem("h_done"), sem("cls_kept")
        ps_kq, ps_s, ps_o0, ps_o1, ps_state, ps_yt, ps_w = g["bank"][0:7]
        ps_o = (ps_o0, ps_o1)
        LAGS = 4
        STATES = TPB + 1

        def order(eng, step):
            for s in range(1 + LAGS):
                step(0, CLS, s, 1, None, s % 4)
            for b in range(B):
                for s in range(b * TPB, b * TPB + 2 * LAGS):
                    step(1, 0, s, NPAIR, b, s % 4)
                with eng.Fori((b * TPB + 2 * LAGS) // 4, (b + 1) * TPB // 4) as r:
                    for i in range(4):
                        step(1, 0, r * 4 + i, NPAIR, b, i)
            for s in range(NPAIR, NPAIR + LAGS):
                step(1, 0, s, NPAIR, B, s % 4)

        def states(t, b):
            return t + 1 + (t // TPB if isinstance(t, int) else b)

        def cls_state(s, b):
            return b is not None and isinstance(s, int) and s < NPAIR and s % TPB == 2

        def live(s, lag, n):
            return not isinstance(s, int) or 0 <= s - lag < n

        def two_before(no, t):
            return no if isinstance(t, int) and t == 0 else no - 1

        with nc.Block() as block:
            @block.sync
            def _(sp):
                sp.dma_start(wr[:, :], a["ffn_wr"][:, 0:DIM].to_broadcast([P, DIM])).then_inc(wr_loaded, 16)
                sp.wait_ge(h_done, 1)
                for b in range(B):
                    sp.dma_start(g["rows"][b * SEQ:b * SEQ + 1, :], h[0:1, CLS * DIM:NT * DIM]).then_inc(g["rows_stored"], 16)
                for b in range(B):
                    with sp.Fori(0, TPB // UNIT) as r:
                        sp.wait_ge(h_done, 1 + b * TPB + (r + 1) * UNIT)
                        sp.dma_start(g["rows"][bass.ds(b * SEQ + 1 + r * UTOK, UTOK), :].rearrange("(i p) d -> p i d", p=P),
                                     h[:, bass.ds((b * TPB + r * UNIT) * DIM, UNIT * DIM)].rearrange("p (i d) -> p i d", d=DIM)
                                     ).then_inc(g["rows_stored"], 16)

            @block.gpsimd
            def _(pool):
                def wide(column):
                    return column.unsqueeze(2).to_broadcast([P, 2, KF // 2])

                def step(n0, t0, s, n, b, q):
                    if live(s, 0, n):
                        no, t = n0 + s, t0 + s
                        tile = trig[:, bass.ds(t, 1), :, :].rearrange("p a c f -> p (a c) f")
                        pos = post[:, bass.ds(TPB if b is None else s - b * TPB, 1), :, :].rearrange("p a c f -> p (a c f)")
                        if isinstance(s, int) and s == 0:
                            after(pool, o_ready, no)
                            if b is not None:
                                pool.wait_ge(cls_kept, 2)
                        elif not (isinstance(s, int) and s < 3):
                            pool.wait_ge(o_ready, no - 2)
                        fk = kq[:, q, 0, 0:KF].rearrange("p (c f) -> p c f", c=2)
                        fq = kq[:, q, 1, 0:KF].rearrange("p (c f) -> p c f", c=2)
                        nc.gpsimd.tensor_tensor(fq, tile[:, :, COL_Q:COL_Q + KF // 2], wide(gg[:, 0, bass.ds(t, 1)]), ALU.mult).then_inc(query_scaled, 1)
                        nc.gpsimd.tensor_tensor(fk, tile[:, :, COL_K:COL_K + KF // 2], wide(wg[:, bass.ds(t, 1)]), ALU.mult)
                        nc.gpsimd.tensor_copy(kq[:, q, 0, KF:KF + PF], pos)
                        nc.gpsimd.tensor_tensor(kq[:, q, 1, KF:KF + PF], pos, gg[:, 1, bass.ds(t, 1)].to_broadcast([P, PF]), ALU.mult)
                        nc.gpsimd.tensor_copy(kq[:, q, 1, LT:P].rearrange("p (c f) -> p c f", c=2), tile[:, :, COL_L:COL_L + PLANES])
                        pool.wait_ge(query_scaled, no + 1)
                        nc.gpsimd.tensor_tensor(fq, fq, sc["wtab"].unsqueeze(1).to_broadcast([P, 2, KF // 2]), ALU.mult).then_inc(kq_ready, 1)
                order(pool, step)

            @block.tensor
            def _(pe):
                def step(n0, t0, s, n, b, q):
                    m = q % 2
                    if live(s, 0, n):
                        no = n0 + s
                        pe.wait_ge(kq_ready, no + 1)
                        after(pe, kqt_copied, no)
                        nc.tensor.transpose(ps_kq[:, 0:P], kq[:, q, 0, :], ident)
                        nc.tensor.transpose(ps_kq[:, P:2 * P], kq[:, q, 1, :], ident).then_inc(kqt_ready, 1)
                    if cls_state(s, b):
                        pe.wait_ge(cls_kept, 2)
                        after(pe, state_copied, b * STATES)
                        nc.tensor.matmul(ps_state[0:LT, 0:DIM], kcls[0:1, 0:LT], vcls[:, :], start=True, stop=False,
                                         skip_group_check=True).then_inc(state_ready, 1)
                    if live(s, 2, n):
                        no, t = n0 + s - 2, s - 2
                        v = V[:, bass.ds((t0 + t) * DIM, DIM)]
                        pe.wait_ge(masked_ready, no + 1)
                        after(pe, y_ready, two_before(no, t))
                        nc.tensor.matmul(ps_o[m][:, 0:DIM], masked[:, m, :], v, start=True, stop=False)
                        if b is not None:
                            pe.wait_ge(state_copied, states(t, b))
                        nc.tensor.matmul(ps_o[m][:, 0:DIM], kq_t[:, m, 1, :], st[:, m if b is not None else 1, :],
                                         start=False, stop=True).then_inc(o_ready, 1)
                        if b is not None:
                            nc.tensor.matmul(ps_state[0:LT, 0:DIM], kq[:, (q - 2) % 4, 0, 0:LT], v, start=False, stop=False,
                                             skip_group_check=True).then_inc(state_ready, 1)
                    if live(s, 1, n):
                        no = n0 + s - 1
                        pe.wait_ge(kqt_copied, no + 1)
                        after(pe, masked_ready, no)
                        nc.tensor.matmul(ps_s[:, 0:P], kq_t[:, 1 - m, 0, :], kq_t[:, 1 - m, 1, :], start=True, stop=True).then_inc(s_ready, 1)
                    if live(s, 3, n):
                        no = n0 + s - 3
                        pe.wait_ge(y_ready, no + 1)
                        after(pe, yt_copied, no)
                        for k in range(KC):
                            x = nc.tensor.transpose(ps_yt[:, k * P:(k + 1) * P], y[:, 1 - m, k * P:(k + 1) * P], ident)
                        x.then_inc(yt_ready, 1)
                    if live(s, 4, n):
                        no = n0 + s - 4
                        pe.wait_ge(yt_copied, no + 1)
                        after(pe, h_done, no)
                        for k in range(KC):
                            nc.tensor.matmul(ps_w[:, 0:DIM], y_t[:, m, k, :], wout[:, k, :], start=(k == 0), stop=False)
                        nc.tensor.matmul(ps_w[:, 0:DIM], ones3[:, :], bias3[:, 5 * DIM:6 * DIM], start=False, stop=True).then_inc(w_ready, 1)
                order(pe, step)

            @block.scalar
            def _(act):
                def step(n0, t0, s, n, b, q):
                    m = q % 2
                    if cls_state(s, b):
                        act.wait_ge(state_ready, b * STATES + 1)
                        nc.scalar.activation(st[0:LT, 0, :], ps_state[0:LT, 0:DIM], ACT.Copy).then_inc(state_copied, 1)
                    if live(s, 0, n):
                        no = n0 + s
                        act.wait_ge(kqt_ready, no + 1)
                        after(act, o_ready, two_before(no, s))
                        nc.scalar.activation(kq_t[:, m, :, :], ps_kq[:, 0:2 * P].rearrange("p (c n) -> p c n", c=2), ACT.Copy).then_inc(kqt_copied, 1)
                    if live(s, 2, n):
                        no, t = n0 + s - 2, s - 2
                        if b is not None:
                            act.wait_ge(state_ready, states(t, b) + 1)
                            nc.scalar.activation(st[0:LT, 1 - m, :], ps_state[0:LT, 0:DIM], ACT.Copy).then_inc(state_copied, 1)
                        act.wait_ge(agg_done, no + 1)
                        after(act, rstd_done, two_before(no, t))
                        nc.scalar.activation(ln_std[:, m:m + 1], ln_agg[:, m, 1:2], ACT.Sqrt, bias=g["eps"][:, :]).then_inc(std_done, 1)
                    if live(s, 3, n):
                        no, t = n0 + s - 3, s - 3
                        act.wait_ge(yt_ready, no + 1)
                        after(act, w_ready, two_before(no, t))
                        nc.scalar.activation(y_t[:, 1 - m, :, :], ps_yt[:, 0:DIM].rearrange("p (k n) -> p k n", k=KC), ACT.Copy).then_inc(yt_copied, 1)
                order(act, step)

            @block.vector
            def _(dve):
                dve.wait_ge(wr_loaded, 16)

                def centre(no, t):
                    dve.wait_ge(stats_done, no + 1)
                    nc.vector.tensor_scalar(mean[:, bass.ds(t, 1)], raw[:, bass.ds(t * 6 + 1, 1)], raw[:, bass.ds(t * 6 + 4, 1)], 0.5,
                                            ALU.add, ALU.mult).then_inc(mean_done, 1)

                def weigh(no, t):
                    dve.wait_ge(mean_done, no + 1)
                    after(dve, weighed, no)
                    nc.vector.scalar_tensor_tensor(out=prod[:, :], in0=h[:, bass.ds(t * DIM, DIM)], scalar=mean[:, bass.ds(t, 1)], in1=wr[:, :],
                                                   op0=ALU.subtract, op1=ALU.mult, accum_out=tok_w[:, bass.ds(t, 1)]).then_inc(weighed, 1)

                def step(n0, t0, s, n, b, q):
                    behind = live(s, 4, n) and not (isinstance(s, int) and s == 4)
                    m = q % 2
                    if b is None and s == 0:
                        dve.wait_ge(kq_ready, 1)
                        nc.vector.tensor_copy(kcls[:, :], kq[0:1, 0, 0, :]).then_inc(cls_kept, 1)
                        nc.vector.tensor_copy(vcls[:, :], V[0:1, CLS * DIM:NT * DIM]).then_inc(cls_kept, 1)
                    def normalise():
                        if live(s, 3, n):
                            no = n0 + s - 3
                            dve.wait_ge(rstd_done, no + 1)
                            after(dve, yt_ready, two_before(no, s - 3))
                            nc.vector.tensor_scalar(y[:, 1 - m, :], ps_o[1 - m][:, 0:DIM], ln_agg[:, 1 - m, 0:1], ln_rstd[:, 1 - m:2 - m],
                                                    ALU.subtract, ALU.mult).then_inc(y_ready, 1)
                    if live(s, 1, n):
                        normalise()
                    if live(s, 2, n):
                        no, t = n0 + s - 2, s - 2
                        dve.wait_ge(o_ready, no + 1)
                        nc.vector.bn_stats(ln_raw[:, m, :], ps_o[m][:, 0:DIM]).then_inc(raw_done, 1)
                        after(dve, y_ready, two_before(no, t))
                        dve.wait_ge(raw_done, no + 1)
                    if live(s, 1, n):
                        no, t = n0 + s - 1, s - 1
                        dve.wait_ge(s_ready, no + 1)
                        after(dve, o_ready, two_before(no, t))
                        mask = ident if b is None else const[:, C_TRI:C_TRI + P]
                        nc.vector.tensor_tensor(masked[:, 1 - m, :], ps_s[:, 0:P], mask, ALU.mult).then_inc(masked_ready, 1)
                    else:
                        normalise()
                    if behind:
                        centre(n0 + s - 5, t0 + s - 5)
                    if live(s, 2, n):
                        nc.vector.bn_aggr(ln_agg[:, m, :], ln_raw[:, m, :]).then_inc(agg_done, 1)
                    if behind:
                        weigh(n0 + s - 5, t0 + s - 5)
                    if live(s, 4, n):
                        no, t = n0 + s - 4, t0 + s - 4
                        dve.wait_ge(w_ready, no + 1)
                        tile = h[:, bass.ds(t * DIM, DIM)]
                        nc.vector.tensor_tensor(tile, ps_w[:, 0:DIM], tile, ALU.add).then_inc(h_done, 1)
                    if live(s, 2, n):
                        no = n0 + s - 2
                        dve.wait_ge(std_done, no + 1)
                        nc.vector.reciprocal(ln_rstd[:, m:m + 1], ln_std[:, m:m + 1]).then_inc(rstd_done, 1)
                    if live(s, 4, n):
                        no, t = n0 + s - 4, t0 + s - 4
                        dve.wait_ge(h_done, no + 1)
                        nc.vector.bn_stats(raw[:, bass.ds(t * 6, 6)], h[:, bass.ds(t * DIM, DIM)]).then_inc(stats_done, 1)
                        if isinstance(s, int) and s == n + 3:
                            centre(no, t)
                            weigh(no, t)
                order(dve, step)


FH = 4 * DIM
FC = FH // P
DIGIT, ROUNDS = 4, 8
NCAND = 2 ** DIGIT - 1
ROW_STORES = B * (TPB // UNIT + 1)


def router(nc, g, a, out):
    with ExitStack() as ctx:
        sb = lambda name, shape, dt=F32: ctx.enter_context(nc.sbuf_tensor(name, shape, dt))
        sem = lambda name: ctx.enter_context(nc.semaphore(name))
        h, mean, rstd, wr, const = g["h"], g["mean"], g["rstd"], g["wr"], g["const"]
        tok_w = g["tok_w"]
        w = sb("w_cols", [P, B, COLS])
        ge = sb("ge", [P, B, NCAND, COLS])
        cnt = sb("cnt", [P, B, NCAND])
        cand, sign, cut = (sb(n, [P, B, NCAND], I32) for n in ("cand", "sign", "cut"))
        over = sb("over", [P, B, NCAND])
        dig_f, dig_i = sb("dig_f", [P, B]), sb("dig_i", [P, B], I32)
        prefix = sb("prefix", [P, B], I32)
        gt, eq, rank = sb("gt", [P, B, COLS]), sb("eq", [P, B, COLS]), sb("rank", [P, B, COLS])
        ngt = sb("ngt", [P, B])
        shift_n = sb("shift_n", [P, NT])
        xn = sb("r_xn", [P, 2, UNIT, DIM])
        place, digit = sb("place", [P, B, COLS], I32), sb("place_digit", [P, 2, B, COLS], I32)
        row_of, tile_of = sb("row_of", [P, B, COLS]), sb("tile_of", [P, B, COLS])
        in_tile = sb("in_tile", [P, B, COLS, PACK])
        at_row = sb("at_row", [P, B, COLS, P], BF16)
        found = sb("found", [P, B, COLS, 2, PACK], BF16)
        place_c = sb("place_c", [P, NPLACE])
        spot = sb("spot", [P, B, PACK])
        shift_ready, base_scaled, base_ready, found_ready, idx_ready = sem("r_shift_ready"), sem("base_scaled"), sem("base_ready"), sem("found_ready"), sem("idx_ready")
        step_done, sums_wanted, sums_ready = sem("r_step_done"), sem("sums_wanted"), sem("r_sums_ready")
        wr_loaded, w_loaded, w_high = sem("wr_loaded"), sem("ffn_w_loaded"), sem("ffn_w_high")
        digits = sb("digits", [P, ROUNDS, NCAND], I32)
        ps, ps_rank, ps_cols, ps_idx = g["bank"][0:4]
        rows = out.rearrange("b t d -> (b t) d")
        base_stored = g["base_stored"]
        ones, tri = const[:, C_ONES:C_ONES + P], const[:, C_TRI:C_TRI + P]
        with nc.Block() as block:
            @block.sync
            def _(sp):
                sp.dma_start(wr[:, :], a["ffn_wr"].to_broadcast([P, DIM + 1])).then_inc(wr_loaded, 16)
                sp.dma_start(digits[:, :, :], a["digits"].to_broadcast([P, ROUNDS * NCAND])
                             .rearrange("p (r n) -> p r n", r=ROUNDS)).then_inc(wr_loaded, 16)
                sp.dma_start(place_c[:, :], a["places"]).then_inc(wr_loaded, 16)
                sp.dma_start(g["ffn_w1"][:, :, :], a["ffn_w1"].rearrange("(k p) n -> p k n", p=P)).then_inc(w_loaded, 16)
                sp.dma_start(g["ffn_w2"][:, :, :], a["ffn_w2"].rearrange("(k p) n -> p k n", p=P)).then_inc(w_loaded, 16)
                sp.dma_start(g["ffn_b1"][:, :], a["ffn_b1"]).then_inc(w_loaded, 16)
                for b in range(B):
                    with sp.Fori(0, TPB // UNIT) as r:
                        sp.wait_ge(base_ready, b * (TPB // UNIT) + r + 1)
                        sp.dma_start(rows[bass.ds(b * SEQ + 1 + r * UTOK, UTOK), :].rearrange("(i p) d -> p i d", p=P),
                                     h[:, bass.ds((b * TPB + r * UNIT) * DIM, UNIT * DIM)].rearrange("p (i d) -> p i d", d=DIM)
                                     ).then_inc(base_stored, 16)
                sp.wait_ge(base_ready, NUNIT + 1)
                for b in range(B):
                    sp.dma_start(rows[b * SEQ:b * SEQ + 1, :], h[0:1, CLS * DIM:NT * DIM]).then_inc(base_stored, 16)

            def two_at_a_time(eng, unit):
                unit(0, 0)
                unit(1, 1)
                with eng.Fori(1, NUNIT // 2) as r:
                    unit(r * 2, 0)
                    unit(r * 2 + 1, 1)
                unit(NUNIT, 0)

            @block.scalar
            def _(act):
                act.wait_ge(w_loaded, 3 * 16)
                for name in ("ffn_w1", "ffn_w2"):
                    nc.scalar.activation(g[name + "_hl"][:, HI], g[name][:, :, :], ACT.Copy).then_inc(w_high, 1)

                def normalise(u, m):
                    after(act, base_ready, u - 1)
                    for i in range(1 if isinstance(u, int) and u == NUNIT else UNIT):
                        t = u * UNIT + i
                        n = nc.scalar.activation(xn[:, m, i, :], h[:, bass.ds(t * DIM, DIM)], ACT.Identity,
                                                 bias=shift_n[:, bass.ds(t, 1)], scale=rstd[:, bass.ds(t, 1)])
                    n.then_inc(base_scaled, 1)
                act.wait_ge(shift_ready, 2)
                two_at_a_time(act, normalise)

            @block.gpsimd
            def _(pool):
                for i, name in enumerate(("ffn_w1", "ffn_w2")):
                    pool.wait_ge(w_high, i + 1)
                    nc.gpsimd.tensor_tensor(g[name + "_hl"][:, LO], g[name][:, :, :], high(g[name + "_hl"][:, HI]), ALU.subtract)

                def add(u, m):
                    n = 1 if isinstance(u, int) and u == NUNIT else UNIT
                    pool.wait_ge(base_scaled, u + 1)
                    tiles = h[:, bass.ds(u * UNIT * DIM, n * DIM)]
                    nc.gpsimd.tensor_tensor(tiles, tiles, xn[:, m, 0:n, :].rearrange("p i d -> p (i d)"), ALU.add).then_inc(base_ready, 1)
                pool.wait_ge(g["rows_stored"], 16 * ROW_STORES)
                two_at_a_time(pool, add)

            @block.vector
            def _(dve):
                V = nc.vector
                V.tensor_tensor(shift_n[:, :], mean[:, :], rstd[:, :], ALU.mult).then_inc(shift_ready, 1)
                dve.wait_ge(shift_ready, 1)
                V.tensor_scalar(shift_n[:, :], shift_n[:, :], -1.0, None, ALU.mult).then_inc(shift_ready, 1)
                dve.wait_ge(wr_loaded, 3 * 16)
                count = [0]

                def done(ins):
                    count[0] += 1
                    ins.then_inc(step_done, 1)
                    dve.wait_ge(step_done, count[0])

                done(V.memset(w[:, :, :], -3.4e38))
                done(V.tensor_tensor(tok_w[:, :], tok_w[:, :], rstd[:, :], ALU.mult))
                done(V.memset(prefix[:, :], 0))
                done(V.tensor_scalar(tok_w[:, :], tok_w[:, :], wr[:, DIM:DIM + 1], None, ALU.add))
                V.tensor_copy(w[:, :, 1:COLS], tok_w[:, 0:NPAIR].rearrange("p (b t) -> p b t", b=B))
                done(V.tensor_copy(w[0:1, :, 0:1], tok_w[0:1, CLS:NT].unsqueeze(1).to_broadcast([1, B, 1])))
                for r in range(ROUNDS):
                    shift = DIGIT * (ROUNDS - 1 - r)
                    done(V.tensor_tensor(cand[:, :, :], prefix[:, :].unsqueeze(2).to_broadcast([P, B, NCAND]),
                                         digits[:, r, :].unsqueeze(1).to_broadcast([P, B, NCAND]), ALU.bitwise_or))
                    done(V.tensor_scalar(sign[:, :, :], cand[:, :, :], 31, 0x7FFFFFFF, ALU.arith_shift_right, ALU.bitwise_and))
                    done(V.tensor_tensor(cut[:, :, :], cand[:, :, :], sign[:, :, :], ALU.bitwise_xor))
                    done(V.tensor_scalar(cut[:, :, :], cut[:, :, :], -1, None, ALU.bitwise_xor))
                    for b in range(B):
                        n = V.tensor_tensor(ge[:, b], w[:, b, :].unsqueeze(1).to_broadcast([P, NCAND, COLS]),
                                            cut[:, b, :].bitcast(F32).unsqueeze(2).to_broadcast([P, NCAND, COLS]), ALU.is_ge)
                    done(n)
                    V.tensor_reduce(cnt[:, :, :], ge[:, :, :, :], AX_X, ALU.add).then_inc(sums_wanted, 1)
                    dve.wait_ge(sums_ready, r + 1)
                    done(V.tensor_scalar(over[:, :, :], ps[:, 0:B * NCAND].rearrange("p (b n) -> p b n", b=B), float(ROUTED), None, ALU.is_ge))
                    done(V.tensor_reduce(dig_f[:, :], over[:, :, :], AX_X, ALU.add))
                    done(V.tensor_copy(dig_i[:, :], dig_f[:, :]))
                    if shift:
                        done(V.tensor_scalar(dig_i[:, :], dig_i[:, :], shift, None, ALU.logical_shift_left))
                    done(V.tensor_tensor(prefix[:, :], prefix[:, :], dig_i[:, :], ALU.bitwise_or))
                done(V.tensor_scalar(dig_i[:, :], prefix[:, :], 31, 0x7FFFFFFF, ALU.arith_shift_right, ALU.bitwise_and))
                done(V.tensor_tensor(prefix[:, :], prefix[:, :], dig_i[:, :], ALU.bitwise_xor))
                done(V.tensor_scalar(prefix[:, :], prefix[:, :], -1, None, ALU.bitwise_xor))
                thr = prefix[:, :].bitcast(F32).unsqueeze(2).to_broadcast([P, B, COLS])
                V.tensor_tensor(gt[:, :, :], w[:, :, :], thr, ALU.is_gt)
                done(V.tensor_tensor(eq[:, :, :], w[:, :, :], thr, ALU.is_equal))
                V.tensor_reduce(ngt[:, :], gt[:, :, :], AX_X, ALU.add).then_inc(sums_wanted, 1)
                dve.wait_ge(sums_ready, ROUNDS + 1)
                done(V.tensor_scalar(ngt[:, :], ps[:, 0:B], -1.0, float(ROUTED), ALU.mult, ALU.add))

                def ranks():
                    for b in range(B):
                        n = V.tensor_tensor_scan(rank[:, b, :], ones[:, 0:COLS], ps_cols[:, b * COLS:(b + 1) * COLS], 0.0, ALU.mult, ALU.add)
                    done(n)
                    flat = rank[:, :, :].rearrange("p b t -> p (b t)")
                    done(V.tensor_tensor(flat, flat, ps_cols[:, 0:B * COLS], ALU.subtract))
                    done(V.tensor_tensor(flat, flat, ps_rank[:, 0:B * COLS], ALU.add))
                ranks()
                for b in range(B):
                    n = V.tensor_scalar(rank[:, b, :], rank[:, b, :], ngt[:, b:b + 1], None, ALU.is_le)
                done(n)
                done(V.tensor_tensor(eq[:, :, :], eq[:, :, :], rank[:, :, :], ALU.mult))
                V.tensor_tensor(gt[:, :, :], gt[:, :, :], eq[:, :, :], ALU.add).then_inc(sums_wanted, 1)
                dve.wait_ge(sums_ready, ROUNDS + 2)
                ranks()
                done(V.tensor_tensor(rank[:, :, :], rank[:, :, :], gt[:, :, :], ALU.mult))
                done(V.tensor_scalar(rank[:, :, :], rank[:, :, :], -1.0, None, ALU.add))
                done(V.tensor_copy(place[:, :, :], rank[:, :, :]))
                V.tensor_scalar(digit[:, 0], place[:, :, :], P - 1, None, ALU.bitwise_and)
                done(V.tensor_scalar(digit[:, 1], place[:, :, :], P.bit_length() - 1, None, ALU.arith_shift_right))
                V.tensor_copy(row_of[:, :, :], digit[:, 0])
                done(V.tensor_copy(tile_of[:, :, :], digit[:, 1]))
                for b in range(B):
                    n = V.tensor_tensor(in_tile[:, b], tile_of[:, b, :].unsqueeze(2).to_broadcast([P, COLS, PACK]),
                                        place_c[:, C_IOTA:C_IOTA + PACK].unsqueeze(1).to_broadcast([P, COLS, PACK]), ALU.is_equal)
                done(n)
                for b in range(B):
                    for e, c in enumerate((C_HIGH, C_LOW)):
                        V.tensor_tensor(found[:, b, :, e, :], in_tile[:, b], place_c[:, c:c + COLS].unsqueeze(2).to_broadcast([P, COLS, PACK]), ALU.mult)
                    V.tensor_tensor(at_row[:, b], row_of[:, b, :].unsqueeze(2).to_broadcast([P, COLS, P]),
                                    place_c[:, C_IOTA:C_IOTA + P].unsqueeze(1).to_broadcast([P, COLS, P]), ALU.is_equal).then_inc(found_ready, 1)
                dve.wait_ge(idx_ready, B)
                sums = ps_idx[:, 0:B * 2 * PACK].rearrange("p (b e n) -> p b e n", b=B, e=2)
                done(V.tensor_scalar(spot[:, :, :], sums[:, :, 0, :], float(P), None, ALU.mult))
                done(V.tensor_tensor(spot[:, :, :], spot[:, :, :], sums[:, :, 1, :], ALU.add))
                flat = spot[:, :, :].rearrange("p b n -> p (b n)")
                done(V.tensor_tensor(flat, flat, place_c[:, C_BASE:C_BASE + B * PACK], ALU.add))
                V.tensor_copy(g["idx"][:, :], flat)

            @block.tensor
            def _(pe):
                for r in range(ROUNDS):
                    pe.wait_ge(sums_wanted, r + 1)
                    nc.tensor.matmul(ps[:, 0:B * NCAND], ones, cnt[:, :, :].rearrange("p b n -> p (b n)"), start=True, stop=True).then_inc(sums_ready, 1)
                pe.wait_ge(sums_wanted, ROUNDS + 1)

                def prefix_sums(marks):
                    marks = marks[:, :, :].rearrange("p b t -> p (b t)")
                    nc.tensor.matmul(ps_rank[:, 0:B * COLS], tri, marks, start=True, stop=True)
                    return nc.tensor.matmul(ps_cols[:, 0:B * COLS], ones, marks, start=True, stop=True)
                prefix_sums(eq)
                nc.tensor.matmul(ps[:, 0:B], ones, ngt[:, :], start=True, stop=True).then_inc(sums_ready, 1)
                pe.wait_ge(sums_wanted, ROUNDS + 2)
                prefix_sums(gt).then_inc(sums_ready, 1)
                for b in range(B):
                    pe.wait_ge(found_ready, b + 1)
                    for c in range(COLS):
                        n = nc.tensor.matmul(ps_idx[:, b * 2 * PACK:(b + 1) * 2 * PACK], at_row[:, b, c, :], found[:, b, c, :, :],
                                             start=(c == 0), stop=(c == COLS - 1))
                    n.then_inc(idx_ready, 1)


def feed_forward(nc, g, a, out):
    with ExitStack() as ctx:
        sb = lambda name, shape, dt=F32: ctx.enter_context(nc.sbuf_tensor(name, shape, dt))
        sem = lambda name: ctx.enter_context(nc.semaphore(name))
        RING = 4
        UNITS = B * PACK // UNIT
        w1, w2, b1, wr = g["ffn_w1_hl"], g["ffn_w2_hl"], g["ffn_b1"], g["wr"]
        hc = sb("f_h", [P, 2, UNIT, DIM])
        xn = sb("f_xn", [P, UNIT, DIM])
        xn_t = sb("f_xn_t", [P, 2, KC, UTOK], F32R)
        hid = sb("f_hid", [P, RING, UTOK])
        hid_hl = sb("f_hid_hl", [P, 2, FC, UTOK], F32R)
        res = sb("f_res", [P, 2, UNIT, DIM])
        ln_raw, ln_agg, ln_std, ln_rstd = sb("f_raw", [P, UNIT, 6]), sb("f_agg", [P, UNIT, 2]), sb("f_std", [P, UNIT]), sb("f_rstd", [P, UNIT])
        prod, sw = sb("f_prod", [P, UNIT, DIM]), sb("f_sw", [P, 2, UNIT])
        h_cleared = sem("h_cleared")
        gathered, scattered = [sem("gathered0"), sem("gathered1")], [sem("scattered0"), sem("scattered1")]
        raw_ready, agg_ready, std_ready, rstd_ready, sums_done, sw_ready = sem("f_raw_ready"), sem("f_agg_ready"), sem("f_std_ready"), sem("f_rstd_ready"), sem("f_sums_done"), sem("f_sw_ready")
        xn_ready, base_done, xt_ready, xt_high, xt_split = sem("f_xn_ready"), sem("f_base_done"), sem("f_xt_ready"), sem("f_xt_high"), sem("f_xt_split")
        hid_ready, gelu_done, hid_high, hid_split = sem("f_hid_ready"), sem("f_gelu_done"), sem("f_hid_high"), sem("f_hid_split")
        y_ready, res_ready = sem("f_y_ready"), sem("f_res_ready")
        ps_t0, ps_t1 = g["bank"][0:2]
        ring, ps_y = g["bank"][2:2 + RING], g["bank"][2 + RING:8]
        idx, ident = g["idx"], g["const"][:, C_ID:C_ID + P]
        ones3, bias3 = g["ones3"], g["bias3"]
        HC = UNIT // 2
        rows = out.rearrange("b t d -> (b t) d")
        first = lambda u: isinstance(u, int) and u == 0
        exists = lambda u: not isinstance(u, int) or u < UNITS

        def order(eng, unit):
            unit(0, 0)
            unit(1, 1)
            with eng.Fori(1, UNITS // 2 - 1) as r:
                unit(r * 2, 0)
                unit(r * 2 + 1, 1)
            unit(UNITS - 2, 0)
            unit(UNITS - 1, 1)

        def dmas(u, m):
            return 16 * UNIT * ((u - m) // 2) if isinstance(u, int) else (u - m) * (16 * UNIT // 2)

        with nc.Block() as block:
            @block.gpsimd
            def _(pool):
                last_row = pool.to_reg(B * SEQ - 1)

                def gather(u):
                    after(pool, xn_ready, u - 1)
                    for i in range(UNIT):
                        nc.gpsimd.indirect_dma_start(hc[:, u % 2, i, :], None, g["rows"], bass.IndirectOffsetOnAxis(ap=places(u, i), axis=0),
                                                     bounds_check=last_row, oob_is_err=False).then_inc(gathered[u % 2], 16)

                def add(u):
                    pool.wait_ge(xn_ready, u + 1)
                    after(pool, scattered[u % 2], dmas(u, u % 2))
                    nc.gpsimd.tensor_tensor(res[:, u % 2, :, :], hc[:, u % 2, :, :], xn[:, :, :], ALU.add).then_inc(base_done, 1)

                def scatter(u):
                    for i in range(UNIT):
                        if i % 2 == 0:
                            pool.wait_ge(res_ready, u * HC + i // 2 + 1)
                        nc.gpsimd.indirect_dma_start(rows, bass.IndirectOffsetOnAxis(ap=places(u, i), axis=0), res[:, u % 2, i, :], None,
                                                     bounds_check=last_row, oob_is_err=False).then_inc(scattered[u % 2], 16)

                def places(u, i):
                    return idx[:, u * UNIT + i:u * UNIT + i + 1]
                pool.wait_ge(h_cleared, 1)
                gather(0)
                gather(1)
                add(0)
                pool.wait_ge(g["base_stored"], 16 * ROW_STORES)
                for u in range(UNITS):
                    if u + 2 < UNITS:
                        after(pool, base_done, u + 1)
                        gather(u + 2)
                    if u + 1 < UNITS:
                        add(u + 1)
                    scatter(u)
                for m in range(2):
                    pool.wait_ge(scattered[m], 16 * UNIT * (UNITS // 2))

            @block.vector
            def _(dve):
                nc.vector.memset(hc[:, :, UNIT - 1, :], 0.0).then_inc(h_cleared, 1)

                def statistics(u, m):
                    dve.wait_ge(gathered[m], dmas(u + 2, m))
                    for i in range(UNIT):
                        n = nc.vector.bn_stats(ln_raw[:, i, :], hc[:, m, i, :])
                    n.then_inc(raw_ready, 1)

                def aggregate(u):
                    for i in range(UNIT):
                        n = nc.vector.bn_aggr(ln_agg[:, i, :], ln_raw[:, i, :])
                    n.then_inc(agg_ready, 1)

                def normalise(u, m):
                    dve.wait_ge(std_ready, u + 1)
                    nc.vector.reciprocal(ln_rstd[:, :], ln_std[:, :]).then_inc(rstd_ready, 1)
                    dve.wait_ge(rstd_ready, u + 1)
                    after(dve, xt_ready, u)
                    after(dve, base_done, u)
                    for i in range(UNIT):
                        n = nc.vector.tensor_scalar(xn[:, i, :], hc[:, m, i, :], ln_agg[:, i, 0:1], ln_rstd[:, i:i + 1], ALU.subtract, ALU.mult)
                    n.then_inc(xn_ready, 1)
                    dve.wait_ge(xn_ready, u + 1)
                    for i in range(UNIT):
                        nc.vector.scalar_tensor_tensor(out=prod[:, i, :], in0=xn[:, i, :], scalar=1.0, in1=wr[:, 0:DIM],
                                                       op0=ALU.mult, op1=ALU.mult, accum_out=sw[:, m, i:i + 1]).then_inc(sums_done, 1)
                    dve.wait_ge(sums_done, (u + 1) * UNIT)
                    nc.vector.tensor_scalar(sw[:, m, :], sw[:, m, :], wr[:, DIM:DIM + 1], None, ALU.add).then_inc(sw_ready, 1)

                def low_xt(u):
                    dve.wait_ge(xt_high, u + 1)
                    for k, src in enumerate((ps_t0, ps_t1)):
                        t = nc.vector.tensor_tensor(xn_t[:, LO, k, :], src[:, :], high(xn_t[:, HI, k, :]), ALU.subtract)
                    t.then_inc(xt_split, 1)

                def low_hid(u, chunks):
                    for c in chunks:
                        dve.wait_ge(hid_high, u * FC + c + 1)
                        nc.vector.tensor_tensor(hid_hl[:, LO, c, :], hid[:, c % RING, :], high(hid_hl[:, HI, c, :]),
                                                ALU.subtract).then_inc(hid_split, 1)

                def combine(u, m, c):
                    dve.wait_ge(sw_ready, u + 1)
                    dve.wait_ge(base_done, u + 1)
                    dve.wait_ge(y_ready, u * HC + c + 1)
                    for i in range(2):
                        y = res[:, m, 2 * c + i, :]
                        k = nc.vector.scalar_tensor_tensor(out=y, in0=ps_y[c][:, i * DIM:(i + 1) * DIM],
                                                           scalar=sw[:, m, 2 * c + i:2 * c + i + 1], in1=y, op0=ALU.mult, op1=ALU.add)
                    k.then_inc(res_ready, 1)

                def unit(u, m):
                    if first(u):
                        statistics(0, 0)
                        dve.wait_ge(raw_ready, 1)
                        aggregate(0)
                        normalise(0, 0)
                        low_xt(0)
                        statistics(1, 1)
                        dve.wait_ge(raw_ready, 2)
                        aggregate(1)
                    low_hid(u, range(FC // 2))
                    if exists(u + 1):
                        normalise(u + 1, 1 - m)
                    low_hid(u, range(FC // 2, FC))
                    if exists(u + 1):
                        low_xt(u + 1)
                    if exists(u + 2):
                        statistics(u + 2, m)
                        dve.wait_ge(raw_ready, u + 3)
                    combine(u, m, 0)
                    if exists(u + 2):
                        aggregate(u + 2)
                    combine(u, m, 1)
                order(dve, unit)

            @block.scalar
            def _(act):
                def deviation(u):
                    act.wait_ge(agg_ready, u + 1)
                    nc.scalar.activation(ln_std[:, :], ln_agg[:, :, 1], ACT.Sqrt, bias=g["eps"][:, :]).then_inc(std_ready, 1)

                def high_xt(u):
                    act.wait_ge(xt_ready, u + 1)
                    after(act, hid_ready, u * FC)
                    for k, src in enumerate((ps_t0, ps_t1)):
                        t = nc.scalar.activation(xn_t[:, HI, k, :], src[:, :], ACT.Copy)
                    t.then_inc(xt_high, 1)

                def high_hid(u, c):
                    act.wait_ge(gelu_done, u * FC + c + 1)
                    nc.scalar.activation(hid_hl[:, HI, c, :], hid[:, c % RING, :], ACT.Copy).then_inc(hid_high, 1)

                def unit(u, m):
                    if first(u):
                        deviation(0)
                        high_xt(0)
                        deviation(1)
                    for c in range(FC):
                        act.wait_ge(hid_ready, u * FC + c + 1)
                        if c == 1:
                            after(act, y_ready, u * HC)
                        if c >= RING:
                            act.wait_ge(hid_split, u * FC + c + 1 - RING)
                        elif c == 0:
                            after(act, hid_split, u * FC)
                        nc.scalar.activation(hid[:, c % RING, :], ring[c % RING][:, :], ACT.Gelu_apprx_tanh, bias=b1[:, c:c + 1]).then_inc(gelu_done, 1)
                        if c:
                            high_hid(u, c - 1)
                    high_hid(u, FC - 1)
                    if exists(u + 1):
                        high_xt(u + 1)
                    if exists(u + 2):
                        deviation(u + 2)
                order(act, unit)

            @block.tensor
            def _(pe):
                def turn(u):
                    pe.wait_ge(xn_ready, u + 1)
                    after(pe, xt_split, u)
                    for k, dst in enumerate((ps_t0, ps_t1)):
                        for i in range(UNIT):
                            t = nc.tensor.transpose(dst[:, i * P:(i + 1) * P], xn[:, i, k * P:(k + 1) * P], ident)
                    t.then_inc(xt_ready, 1)

                def unit(u, m):
                    if first(u):
                        turn(u)
                    pe.wait_ge(xt_split, u + 1)
                    for c in range(FC):
                        if c >= RING:
                            pe.wait_ge(gelu_done, u * FC + c + 1 - RING)
                        for k in range(KC):
                            t = product(nc, ring[c % RING][:, :], parts(lambda e: w1[:, e, k, c * P:(c + 1) * P]),
                                        parts(lambda e: xn_t[:, e, k, :]), k == 0, k == KC - 1)
                        t.then_inc(hid_ready, 1)
                    if exists(u + 1):
                        turn(u + 1)
                    for c in range(HC):
                        after(pe, res_ready, (u - 1) * HC + c + 1)
                        for i in range(2):
                            i0 = (2 * c + i) * P
                            y = ps_y[c][:, i * DIM:(i + 1) * DIM]
                            nc.tensor.matmul(y, ones3[:, :], bias3[:, 6 * DIM:7 * DIM], start=True, stop=False)
                            for k in range(FC):
                                if c == 0 and i == 0:
                                    pe.wait_ge(hid_split, u * FC + k + 1)
                                t = product(nc, y, parts(lambda e: hid_hl[:, e, k, i0:i0 + P]), parts(lambda e: w2[:, e, k, :]), False, k == FC - 1)
                        t.then_inc(y_ready, 1)
                order(pe, unit)


def constants():
    c = np.zeros((P, NCONST), np.float32)
    p = np.arange(P)
    c[:, C_ID:C_ID + P] = np.eye(P)
    c[:, C_TRI:C_TRI + P] = p[:, None] <= p[None, :]
    c[:, C_STRICT:C_STRICT + P] = p[:, None] < p[None, :]
    c[:, C_ONES:C_ONES + P] = 1
    half = HD // 2
    inv_freq = (1.0 / 10000.0 ** (np.arange(0, half, 2, dtype=np.float32) / half)).astype(np.float32)
    row, col = (p % WTOK) // WIN, p % WIN
    ang = np.concatenate([row[:, None] * inv_freq, col[:, None] * inv_freq], 1).astype(np.float32)
    c[:, C_COS:C_COS + HD] = np.repeat(np.cos(ang), 2, axis=1)
    s = np.repeat(np.sin(ang), 2, axis=1)
    s[:, 0::2] *= -1
    c[:, C_SIN:C_SIN + HD] = s
    c[:, C_HEAD:C_HEAD + 4] = p[:, None] // HD == np.arange(4)
    c[:, C_POS:C_POS + TPB] = 1 + p[:, None] + P * np.arange(TPB)
    seg = np.ones((8, TPB))
    seg[:, 0] = 0
    c[:, C_SEG:] = seg.reshape(1, -1)
    return c


def places():
    c = np.zeros((P, NPLACE), np.float32)
    p = np.arange(P)
    c[:, C_IOTA:C_HIGH] = p
    c[:, C_HIGH + 1:C_LOW] = np.arange(TPB)
    c[:, C_LOW + 1:C_BASE] = 1 + p[:, None]
    slot = p[:, None] + P * np.arange(PACK)
    for b in range(B):
        c[:, C_BASE + b * PACK:C_BASE + (b + 1) * PACK] = b * SEQ + (slot >= ROUTED) * B * SEQ
    return c


def program(nc, a, out):
    with ExitStack() as ctx:
        sb = lambda name, shape, dt=F32: ctx.enter_context(nc.sbuf_tensor(name, shape, dt))
        g = {"bank": [ctx.enter_context(nc.psum_tensor(f"bank{i}", [P, 512], F32)) for i in range(8)]}
        g["const"] = sb("const", [P, NCONST])
        g["h"] = sb("h", [P, NT * DIM])
        g["raw"] = sb("raw", [P, NT * 6])
        g["mean"], g["rstd"] = sb("mean", [P, NT]), sb("rstd", [P, NT])
        g["scal"] = sb("scal", [P, NSCAL])
        scalars = sb("scalars", [P, 10 + KF // 2])
        at = 0
        g["sc"] = {}
        for name, n in (("setw", SETS), ("posw", 1), ("rscale", 1), ("rthr", 1), ("count", 1), ("ltmw", 1), ("nthr", 1), ("wtab", KF // 2)):
            g["sc"][name] = scalars[:, at:at + n]
            at += n
        g["ones3"], g["bias3"] = sb("ones3", [3, P], BF16), sb("bias3", [3, NBIAS], BF16)
        g["half_pi"], g["eps"] = sb("half_pi", [P, 1]), sb("eps", [P, 1])
        g["rows"] = nc.dram_tensor("rows", [B * SEQ, DIM], F32, kind="Internal").ap()
        g["idx"] = sb("idx", [P, B * PACK], I32)
        g["tok_w"] = sb("tok_w", [P, NT])
        g["rows_stored"] = ctx.enter_context(nc.semaphore("rows_stored"))
        g["base_stored"] = ctx.enter_context(nc.semaphore("base_stored"))
        with ExitStack() as mid:
            sm = lambda name, shape, dt=F32: mid.enter_context(nc.sbuf_tensor(name, shape, dt))
            g["wout"] = sm("wout", [P, KC, DIM])
            g["st"] = sm("st", [P, 2, DIM])
            g["post"] = sm("post", [P, TPB + 1, 2, PLANES])
            g["rpos"] = sm("rpos", [P, TPB])
            g["wg"], g["gg"], g["jcls"] = sm("wg", [P, NT]), sm("gg", [P, 2, NT]), sm("jcls", [P, 2 * JOINT])
            g["V"], g["th"] = sm("V", [P, NT * DIM]), sm("th", [P, NT * NCOL])
            at = [0]

            def early(n, m):
                at[0] += n * m
                return g["V"][:, at[0] - n * m:at[0]].rearrange("p (k n) -> p k n", n=m)
            g["early"] = early
            with ExitStack() as before:
                se = lambda name, shape: before.enter_context(nc.sbuf_tensor(name, shape, F32R))
                g["enc_w1"], g["enc_wv"], g["enc_w2"] = se("enc_w1", [P, 2, KC, NHID * P]), se("enc_wv", [P, 2, KC, DIM]), se("enc_w2", [P, 2, NHID, NCOL])
                with ExitStack() as first:
                    g["wqkv_hl"] = first.enter_context(nc.sbuf_tensor("wqkv_hl", [P, 2, KC, 3 * DIM], F32R))
                    g["wqkv"], g["wproj"] = early(KC, 3 * DIM), early(KC, DIM)
                    g["xt"] = early(UNIT, KC * P).rearrange("p j (k n) -> p j k n", k=KC)
                    g["x_loaded"] = [first.enter_context(nc.semaphore(f"x_loaded{j}")) for j in range(UNIT)]
                    prologue(nc, g, a)
                    tokenizer(nc, g, a)
                normaliser(nc, g, "_1")
                encoders(nc, g, a)
            g["trig"], g["kq"] = sm("trig", [P, NT, 2, NPH]), sm("kq", [P, 4, 2, P])
            phasors(nc, g)
            retrieval(nc, g, a)
        normaliser(nc, g, "_2")
        g["ffn_w1"], g["ffn_w2"], g["ffn_b1"] = sb("ffn_w1", [P, KC, FH]), sb("ffn_w2", [P, FC, DIM]), sb("ffn_b1", [P, FC])
        g["wr"] = sb("wr", [P, DIM + 1])
        g["ffn_w1_hl"], g["ffn_w2_hl"] = sb("ffn_w1_hl", [P, 2, KC, FH], F32R), sb("ffn_w2_hl", [P, 2, FC, DIM], F32R)
        router(nc, g, a, out)
        feed_forward(nc, g, a, out)


def columns(v):
    return v.reshape(-1, P).T


def kernel(**inputs):
    import concourse.bacc as bacc
    from concourse.bass_utils import run_bass_kernel_spmd

    i = {k.removeprefix("L0_"): np.asarray(v) for k, v in inputs.items()}
    w = WIN
    mem = i["attn_ltm_binding_mem"]
    w2 = np.zeros((NHID * P, NCOL), np.float32)
    b2 = np.zeros((NCOL, 2), np.float32)
    b2[:, 1] = 1.0
    b2[COL_G, 1] = 0.5
    at = 0
    for name, col, n in (("ke", COL_K + JOINT, PLANES), ("qe", COL_Q + JOINT, PLANES), ("lke", COL_L, PLANES), ("gate", COL_G, 1)):
        hidden = i[f"attn_{name}_w2"].shape[0]
        w2[at:at + hidden, col:col + n] = i[f"attn_{name}_w2"]
        b2[col:col + n, 0] = i[f"attn_{name}_b2"]
        at += hidden
    digits = (np.arange(1, NCAND + 1, dtype=np.int64)[None, :] << (DIGIT * (ROUNDS - 1 - np.arange(ROUNDS)))[:, None])
    arrays = {
        "const": constants(),
        "places": places(),
        "digits": digits.astype(np.uint32).view(np.int32).reshape(1, -1),
        "x_t": i["x"].reshape(B, IMG // w, w, IMG // w, w, DIM).transpose(5, 0, 1, 3, 2, 4).reshape(DIM, NUNIT, UTOK),
        "cls": i["cls_tok"].reshape(1, DIM),
        "qkv_w": i["tok_qkv_w"].T,
        "proj_w": i["tok_proj_w"].T,
        "bias": np.concatenate([i["tok_qkv_b"], i["tok_proj_b"], i["attn_v_b"], i["attn_out_b"], i["ffn_b2"]]).reshape(-1, DIM),
        "scal": np.concatenate([i["attn_set_weights"]] + [i[f"attn_{n}"].reshape(1) for n in (
            "pos_weight", "surprise_scale", "surprise_bias", "resonance_scale", "resonance_threshold", "ltm_weight", "ltm_count")]
            + [i["attn_pos_freqs"]])[None],
        "enc_w1": np.concatenate([i[f"attn_{n}_w1"] for n in ("ke", "qe", "lke", "gate")], axis=1),
        "enc_b1": columns(np.concatenate([i[f"attn_{n}_b1"] for n in ("ke", "qe", "lke", "gate")])),
        "enc_w2": w2,
        "enc_b2": b2,
        "enc_wv": i["attn_v_w"],
        "out_w": i["attn_out_w"],
        "ln_g": columns(i["attn_out_ln_g"]),
        "ln_b": columns(i["attn_out_ln_b"]),
        "ltm": np.concatenate([mem.real, mem.imag], axis=0),
        "ffn_wr": np.concatenate([i["ffn_wr"].reshape(-1), i["ffn_br"]])[None],
        "ffn_w1": i["ffn_w1"],
        "ffn_b1": columns(i["ffn_b1"]),
        "ffn_w2": i["ffn_w2"],
    }
    arrays = {k: np.ascontiguousarray(v) for k, v in arrays.items()}
    nc = bacc.Bacc("TRN2", target_bir_lowering=False, num_devices=1)
    a = {k: nc.dram_tensor(f"in_{k}", v.shape, mybir.dt.from_np(v.dtype), kind="ExternalInput").ap() for k, v in arrays.items()}
    out = nc.dram_tensor("out", [B, IMG * IMG + 1, DIM], F32, kind="ExternalOutput").ap()
    program(nc, a, out)
    r = run_bass_kernel_spmd(nc, [{f"in_{k}": v for k, v in arrays.items()}], core_ids=[0])
    return r.results[0]["out"]
```
